# Optimizing a Trainium2 kernel written in Bass

```python
import numpy as np
import jax
import jax.numpy as jnp

def _softmax(x, axis=-1):
    return jax.nn.softmax(x, axis=axis)

def _gelu(x):
    return jax.nn.gelu(x, approximate=True)

def _silu(x):
    return jax.nn.silu(x)

def _sigmoid(x):
    return jax.nn.sigmoid(x)

def _layernorm(x, axis=-1, eps=1e-05):
    m = jnp.mean(x, axis=axis, keepdims=True)
    v = jnp.var(x, axis=axis, keepdims=True)
    return (x - m) / jnp.sqrt(v + eps)

def _scatter_add(tgt, idx, src, axis=0):
    return tgt.at[idx].add(src)

def _segment_sum(src, seg, n):
    return jax.ops.segment_sum(src, seg, n)
kernel_name = 'mk_gps_d1_gnn_r8_f77bd2'

def setup_inputs(seed: int=0):
    np.random.seed(seed)
    _w = jnp.asarray

    def _rec_inputs():
        import jax
        import jax.numpy as jnp
        _gk = jax.random.key(seed)
        x = -0.0003713 + 1 * jax.random.normal(jax.random.fold_in(_gk, 1), (6250, 256), jnp.float32)
        _s = jax.random.randint(jax.random.fold_in(_gk, 2), (50000,), 0, 6250, jnp.int32)
        _d = jax.random.randint(jax.random.fold_in(_gk, 3), (50000,), 0, 6250, jnp.int32)
        _loop = jnp.arange(6250, dtype=jnp.int32)
        src = jnp.concatenate([_s, _d, _loop])
        dst = jnp.concatenate([_d, _s, _loop])
        _o = jnp.argsort(dst, stable=True)
        src = src[_o]
        dst = dst[_o]
        return (x, src, dst)
    x, src, dst = _rec_inputs()

    def _L0_gnn_setup():
        import jax, jax.numpy as jnp
        import numpy as np
        N = 6250
        DEG = 16
        E = N * DEG
        F = 256
        H = 8
        DH = 32
        ALPHA = 0.2
        key = jax.random.key(seed)
        ks = jax.random.split(key, 6)
        h = jax.random.normal(ks[0], (N, F), jnp.float32)
        lim_w = 1.414 * np.sqrt(6.0 / (F + DH))
        W = jax.random.uniform(ks[1], (H, F, DH), jnp.float32, -lim_w, lim_w)
        bW = jnp.zeros((H, DH), jnp.float32)
        lim_a = 1.414 * np.sqrt(6.0 / (2 * DH + 1))
        a_src = jax.random.uniform(ks[2], (H, DH), jnp.float32, -lim_a, lim_a)
        a_dst = jax.random.uniform(ks[3], (H, DH), jnp.float32, -lim_a, lim_a)
        a_bias = jnp.zeros((H,), jnp.float32)
        src = jax.random.randint(ks[4], (E,), 0, N, dtype=jnp.int32)
        dst = jnp.repeat(jnp.arange(N, dtype=jnp.int32), DEG)
        return {'h': h, 'W': W, 'bW': bW, 'a_src': a_src, 'a_dst': a_dst, 'a_bias': a_bias, 'src': src, 'dst': dst}
    _L0_gnn_all = _L0_gnn_setup()
    _L0_gnn_in = {k: v for k, v in _L0_gnn_all.items() if k in ('W', 'bW', 'a_src', 'a_dst', 'a_bias')}
    del _L0_gnn_all

    def _L0_mix_setup():
        import jax, jax.numpy as jnp
        import numpy as np
        import math
        EMBED = 256
        HEADS = 4
        HEAD_DIM = EMBED // HEADS
        OUT_DIM = 256
        LN_EPS = 1e-05

        def _qkv_init(key):
            spread = math.sqrt(3.0 / EMBED)
            gain, delta = (0.01, 0.01)
            w = jax.random.uniform(key, (EMBED, EMBED), minval=-spread, maxval=spread) * gain
            return w + delta * jnp.eye(EMBED, dtype=w.dtype)

        def _layer_norm(x, g, b):
            mu = jnp.mean(x, axis=-1, keepdims=True)
            var = jnp.mean(jnp.square(x - mu), axis=-1, keepdims=True)
            return (x - mu) * jax.lax.rsqrt(var + LN_EPS) * g + b

        def _split_heads(x, B, S):
            return x.reshape(B, S, HEADS, HEAD_DIM).transpose(0, 2, 1, 3)
        key = jax.random.key(seed)
        ks = jax.random.split(key, 6)
        seq = jax.random.normal(ks[0], (4, 1024, EMBED), dtype=jnp.float32)
        wq = _qkv_init(ks[1])
        wk = _qkv_init(ks[2])
        wv = _qkv_init(ks[3])
        bound = 1.0 / math.sqrt(EMBED)
        wo = jax.random.uniform(ks[4], (OUT_DIM, EMBED), minval=-bound, maxval=bound)
        bo = jax.random.uniform(ks[5], (OUT_DIM,), minval=-bound, maxval=bound)
        ln_k_g = jnp.ones((HEAD_DIM,), jnp.float32)
        ln_k_b = jnp.zeros((HEAD_DIM,), jnp.float32)
        ln_v_g = jnp.ones((HEAD_DIM,), jnp.float32)
        ln_v_b = jnp.zeros((HEAD_DIM,), jnp.float32)
        return {'seq': seq, 'wq': wq, 'wk': wk, 'wv': wv, 'wo': wo, 'bo': bo, 'ln_k_g': ln_k_g, 'ln_k_b': ln_k_b, 'ln_v_g': ln_v_g, 'ln_v_b': ln_v_b}
    _L0_mix_all = _L0_mix_setup()
    _L0_mix_in = {k: v for k, v in _L0_mix_all.items() if k in ('wq', 'wk', 'wv', 'wo', 'bo', 'ln_k_g', 'ln_k_b', 'ln_v_g', 'ln_v_b')}
    del _L0_mix_all

    def _L0_ffn_setup():
        import jax, jax.numpy as jnp
        import numpy as np
        TOP_K = 2
        key = jax.random.key(seed)
        ks = jax.random.split(key, 4)
        B, L, D, H, E = (8, 512, 256, 1024, 8)
        s = 0.02
        return {'x': jax.random.normal(ks[0], (B, L, D), jnp.float32), 'Wg': jax.random.normal(ks[1], (D, E), jnp.float32) * s, 'bg': jnp.zeros((E,), jnp.float32), 'W1': jax.random.normal(ks[2], (E, D, H), jnp.float32) * s, 'b1': jnp.zeros((E, H), jnp.float32), 'W2': jax.random.normal(ks[3], (E, H, D), jnp.float32) * s, 'b2': jnp.zeros((E, D), jnp.float32)}
    _L0_ffn_all = _L0_ffn_setup()
    _L0_ffn_in = {k: v for k, v in _L0_ffn_all.items() if k in ('Wg', 'bg', 'W1', 'b1', 'W2', 'b2')}
    del _L0_ffn_all
    return {'x': x, 'src': src, 'dst': dst, 'L0_gnn_W': _L0_gnn_in['W'], 'L0_gnn_bW': _L0_gnn_in['bW'], 'L0_gnn_a_src': _L0_gnn_in['a_src'], 'L0_gnn_a_dst': _L0_gnn_in['a_dst'], 'L0_gnn_a_bias': _L0_gnn_in['a_bias'], 'L0_mix_wq': _L0_mix_in['wq'], 'L0_mix_wk': _L0_mix_in['wk'], 'L0_mix_wv': _L0_mix_in['wv'], 'L0_mix_wo': _L0_mix_in['wo'], 'L0_mix_bo': _L0_mix_in['bo'], 'L0_mix_ln_k_g': _L0_mix_in['ln_k_g'], 'L0_mix_ln_k_b': _L0_mix_in['ln_k_b'], 'L0_mix_ln_v_g': _L0_mix_in['ln_v_g'], 'L0_mix_ln_v_b': _L0_mix_in['ln_v_b'], 'L0_ffn_Wg': _L0_ffn_in['Wg'], 'L0_ffn_bg': _L0_ffn_in['bg'], 'L0_ffn_W1': _L0_ffn_in['W1'], 'L0_ffn_b1': _L0_ffn_in['b1'], 'L0_ffn_W2': _L0_ffn_in['W2'], 'L0_ffn_b2': _L0_ffn_in['b2']}

def reference(x, src, dst, L0_gnn_W, L0_gnn_bW, L0_gnn_a_src, L0_gnn_a_dst, L0_gnn_a_bias, L0_mix_wq, L0_mix_wk, L0_mix_wv, L0_mix_wo, L0_mix_bo, L0_mix_ln_k_g, L0_mix_ln_k_b, L0_mix_ln_v_g, L0_mix_ln_v_b, L0_ffn_Wg, L0_ffn_bg, L0_ffn_W1, L0_ffn_b1, L0_ffn_W2, L0_ffn_b2):
    import jax
    import jax.numpy as jnp

    def _L0_gnn_ref(h, W, bW, a_src, a_dst, a_bias, src, dst):
        import jax, jax.numpy as jnp
        import numpy as np
        N = 6250
        DEG = 16
        E = N * DEG
        F = 256
        H = 8
        DH = 32
        ALPHA = 0.2
        Wh = jnp.einsum('nf,hfd->nhd', h, W) + bW
        s1 = jnp.einsum('nhd,hd->nh', Wh, a_src)
        s2 = jnp.einsum('nhd,hd->nh', Wh, a_dst)
        e = jax.nn.leaky_relu(s1[src] + s2[dst] + a_bias, ALPHA)
        m = jax.ops.segment_max(e, dst, num_segments=N)
        ex = jnp.exp(e - m[dst])
        denom = jax.ops.segment_sum(ex, dst, num_segments=N)
        attn = ex / denom[dst]
        hp = jax.ops.segment_sum(attn[:, :, None] * Wh[src], dst, num_segments=N)
        return hp.reshape(N, H * DH)

    def _L0_mix_ref(seq, wq, wk, wv, wo, bo, ln_k_g, ln_k_b, ln_v_g, ln_v_b):
        import jax, jax.numpy as jnp
        import numpy as np
        import math
        EMBED = 256
        HEADS = 4
        HEAD_DIM = EMBED // HEADS
        OUT_DIM = 256
        LN_EPS = 1e-05

        def _qkv_init(key):
            spread = math.sqrt(3.0 / EMBED)
            gain, delta = (0.01, 0.01)
            w = jax.random.uniform(key, (EMBED, EMBED), minval=-spread, maxval=spread) * gain
            return w + delta * jnp.eye(EMBED, dtype=w.dtype)

        def _layer_norm(x, g, b):
            mu = jnp.mean(x, axis=-1, keepdims=True)
            var = jnp.mean(jnp.square(x - mu), axis=-1, keepdims=True)
            return (x - mu) * jax.lax.rsqrt(var + LN_EPS) * g + b

        def _split_heads(x, B, S):
            return x.reshape(B, S, HEADS, HEAD_DIM).transpose(0, 2, 1, 3)
        B, S, _ = seq.shape
        q = _split_heads(seq @ wq.T, B, S)
        k = _split_heads(seq @ wk.T, B, S)
        v = _split_heads(seq @ wv.T, B, S)
        k = _layer_norm(k, ln_k_g, ln_k_b)
        v = _layer_norm(v, ln_v_g, ln_v_b)
        kv = jnp.einsum('bhsd,bhse->bhde', k, v) / S
        ga = jnp.einsum('bhsd,bhde->bhse', q, kv)
        ga = ga.transpose(0, 2, 1, 3).reshape(B, S, EMBED)
        return ga @ wo.T + bo

    def _L0_ffn_ref(x, Wg, bg, W1, b1, W2, b2):
        import jax, jax.numpy as jnp
        import numpy as np
        TOP_K = 2
        B, L, D = x.shape
        E = W1.shape[0]
        xf = x.reshape(-1, D)
        gate_logits = xf @ Wg + bg
        top_w, top_i = jax.lax.top_k(gate_logits, TOP_K)
        top_w = jax.nn.softmax(top_w, axis=-1)
        w_dense = jnp.sum(jax.nn.one_hot(top_i, E, dtype=xf.dtype) * top_w[..., None], axis=1)
        out = jnp.zeros_like(xf)
        for e in range(E):
            h = jax.nn.gelu(xf @ W1[e] + b1[e], approximate=False)
            out = out + w_dense[:, e:e + 1] * (h @ W2[e] + b2[e])
        return out.reshape(B, L, D)
    xn = _layernorm(x, axis=-1)
    x = x + _L0_gnn_ref(xn, L0_gnn_W, L0_gnn_bW, L0_gnn_a_src, L0_gnn_a_dst, L0_gnn_a_bias, src, dst) + _L0_mix_ref(xn[None], L0_mix_wq, L0_mix_wk, L0_mix_wv, L0_mix_wo, L0_mix_bo, L0_mix_ln_k_g, L0_mix_ln_k_b, L0_mix_ln_v_g, L0_mix_ln_v_b)[0]
    x = x + _L0_ffn_ref(_layernorm(x, axis=-1)[None], L0_ffn_Wg, L0_ffn_bg, L0_ffn_W1, L0_ffn_b1, L0_ffn_W2, L0_ffn_b2)[0]
    return x

_drawn_inputs = setup_inputs


def setup_inputs(seed=0):
    import zlib

    import numpy as np

    out = dict(_drawn_inputs(seed))
    spreads = {'L0_gnn_bW': (0.0, 0.1),
     'L0_gnn_a_bias': (0.0, 0.747),
     'L0_mix_ln_k_g': (1.0, 0.6),
     'L0_mix_ln_k_b': (0.0, 0.8),
     'L0_mix_ln_v_g': (1.0, 0.6),
     'L0_mix_ln_v_b': (0.0, 0.8),
     'L0_ffn_bg': (0.0, 0.312),
     'L0_ffn_b1': (0.0, 0.48),
     'L0_ffn_b2': (0.0, 0.358)}
    factors = {'L0_mix_wq': 8.0, 'L0_mix_wk': 8.0, 'L0_mix_wv': 8.0, 'L0_mix_wo': 8.0, 'L0_mix_bo': 4.518}
    for name, (base, spread) in spreads.items():
        noise = np.random.default_rng([zlib.crc32(name.encode()), seed]).standard_normal(out[name].shape)
        drawn = base * np.exp(spread * noise) if base else spread * noise
        out[name] = jnp.asarray(drawn.astype(out[name].dtype))
    for name, factor in factors.items():
        out[name] = (out[name] * factor).astype(out[name].dtype)
    return out
```

```python
from contextlib import ExitStack

import concourse.bass as bass
from concourse import mybir

F32 = mybir.dt.float32
BF16 = mybir.dt.bfloat16
I32 = mybir.dt.int32
ALU = mybir.AluOpType
ACT = mybir.ActivationFunctionType
AX = mybir.AxisListType
MAXOP = bass.bass_isa.ReduceOp.max

P = 128
N = 6250
D = 256
KD = D // P
NT = 50
NP = NT * P
NPAIR = NT // 2
H, DH = 8, 32
ROW = D + H
WCOL = D + 2 * H
MH, MD = 4, 64
E_REAL = 2 * 50000 + N
EC = 832
EP = EC * P
HC = 32
NHIST = EC // (2 * HC)
WIN = 24
SG = 4
NG = WIN // SG
WSTEP, WLEN = 16, 40
NWROW = (EP - WLEN) // WSTEP + 1
WT = 10
NBUCK = 64
BT = 512 // NBUCK
NE, HID = 8, 1024
FC = HID // P
TT = 256
XT = 58
YMIN = 2 * N // TT
TAIL = N - (N // P) * P
TAIL_T = N // P
EPS = 1e-5
ALPHA = 0.2
LOW, LOWER = -1e29, -1e30
assert NPAIR * 2 == NT and E_REAL <= EP and EC == NHIST * 2 * HC and TAIL_T == NT - 2


class Chain:

    def __init__(self, eng, sem):
        self.eng, self.sem, self.base, self.n = eng, sem, 0, 0

    def step(self, ins):
        self.n += 1
        ins.then_inc(self.sem, 1)

    def wait(self):
        self.eng.wait_ge(self.sem, self.base + self.n)

    def link(self, ins):
        self.step(ins)
        self.wait()

    def at(self, base):
        self.base, self.n = base, 0


def gps_layer(nc, x, src, dst, dst_next, gW, gbW, gas, gad, gab, wkvT, wq, woT, bo, lng, lnb,
              Wg, bg, W1, b1, W2, b2, out):
    ctx = ExitStack()

    def sb(name, shape, dt=F32):
        return ctx.enter_context(nc.sbuf_tensor(name, shape, dt))

    def sem(name):
        return ctx.enter_context(nc.semaphore(name))

    def dram(name, shape, dt=F32):
        return nc.dram_tensor(name, shape, dt, kind="Internal").ap()

    with ctx:
        win_tab = dram("win_tab", (NWROW, WLEN), I32)
        wh_tab = dram("wh_tab", (NP, ROW))
        s2_tab = dram("s2_tab", (NP, H))
        base_tab = dram("base_tab", (NP, D))
        ord_tab = dram("ord_tab", (NP, 4), I32)
        xs_tab = dram("xs_tab", (XT * TT, D))
        ys_tab = dram("ys_tab", (XT * TT, D))

        x_all = sb("x_all", [P, NT, D])
        xT_all = sb("xT_all", [P, KD, NP])
        xn2_all = xT_all[:, :, :].rearrange("p k n -> p (k n)").rearrange("p (t d) -> p t d", d=D)
        gath = sb("gath", [P, 2, WIN, ROW])
        g = gath[:, :, :, :].rearrange("p a k r -> p (a k r)")
        shared = sb("shared", [P, 2400])
        ident = sb("ident", [P, P])
        ltf = sb("ltf", [P, P])
        ltb = sb("ltb", [P, P], BF16)
        onesf = sb("onesf", [P, P])
        onesb = sb("onesb", [P, P], BF16)
        zeros = sb("zeros", [P, D])
        iota_f = sb("iota_f", [P, P])
        iota_i = sb("iota_i", [P, P], I32)
        node_i = sb("node_i", [P, NT], I32)
        abias = sb("abias", [P, H])
        bo_b = sb("bo_b", [P, D])
        mixw = sb("mixw", [P, KD, D])
        wg_s = sb("wg_s", [P, KD, NE])
        bg_b = sb("bg_b", [P, NE])
        ordn = sb("ordn", [P, NT, 4], I32)
        deg = sb("deg", [P, NT])
        rowp = sb("rowp", [P, NT])
        small = sb("small", [P, 4, NT])
        ranki = sb("ranki", [P, NT], I32)
        mxrem = sb("mxrem", [P, NT])
        winr = sb("winr", [P, NT], I32)
        starti = sb("starti", [P, NT], I32)
        bits = sb("bits", [P, 4, NT], I32)
        groups = sb("groups", [P, NT], I32)
        ctl = sb("ctl", [P, 5], I32)
        ctlf = sb("ctlf", [P, 7])
        gmask = sb("gmask", [P, NT])
        gcumf = sb("gcumf", [P, 2, NPAIR])
        gbase = sb("gbase", [P, 2, NPAIR], I32)
        gcum = sb("gcum", [P, 2, NPAIR], I32)
        nwin = sb("nwin", [P, 1], I32)
        idx = sb("idx", [P, NT + 2, WIN], I32)
        idxs = sb("idxs", [P, 2, WIN], I32)
        m_all = sb("m_all", [P, NT, H])
        den_all = sb("den_all", [P, NT, H])
        s2_all = sb("s2_all", [P, NT, H])
        stats = sb("stats", [P, 2, 6])
        mv = sb("mv", [P, 2, 2])
        rs = sb("rs", [P, 2, 2])
        kvr = sb("kvr", [P, 2, 2, 8])
        ez = sb("ez", [P, WIN, H])
        pen = sb("pen", [P, WIN])
        es = sb("es", [P, 6, H])
        accf = sb("accf", [P, D])
        wts = sb("wts", [P, 2, NT])
        slotf = sb("slotf", [P, 2, NT])
        sloti = sb("sloti", [P, 2, NT], I32)
        valid = sb("valid", [P, NT])
        cnt = sb("cnt", [P, 4, NE])
        cnti = sb("cnti", [P, NE], I32)
        ebnd = sb("ebnd", [P, 2, NE], I32)

        def carve(area, spans):
            at, parts = spans["start"], []
            for n in spans["sizes"]:
                parts.append(area[:, at:at + n])
                at += n
            assert at <= area.shape[1], at
            return parts

        gb = g.bitcast(BF16)
        oh_b = gb[:, 0:2 * HC * P].rearrange("p (a j c) -> p a j c", a=2, j=HC)
        oh_a = gb[:, 2 * HC * P:2 * HC * (P + NT)].rearrange("p (a j c) -> p a j c", a=2, j=HC)
        oh_d = gb[:, 0:NT * NBUCK].rearrange("p (t c) -> p t c", t=NT)
        r_in, = carve(g, dict(start=1600, sizes=[NT * NBUCK]))
        r_cnt, r_scan = carve(xT_all[:, :, :].rearrange("p k n -> p (k n)"), dict(start=0, sizes=[NT * NBUCK] * 2))
        wina, winb = [a.bitcast(I32).rearrange("p (t w) -> p t w", t=NT)
                      for a in carve(g, dict(start=0, sizes=[NT * WLEN] * 2))]
        xn, xTs, whs, kvs, kvq = carve(g, dict(start=4000, sizes=[2 * D, 2 * D, 2 * WCOL, 4 * D, 4 * D]))
        xn = xn.rearrange("p (b d) -> p b d", b=2)
        xTs = xTs.rearrange("p (k n) -> p k n", k=KD)
        whs = whs.rearrange("p (b c) -> p b c", b=2)
        kvs = kvs.rearrange("p (b c) -> p b c", b=2)
        kvq = kvq.rearrange("p (b c) -> p b c", b=2)
        wkv_, avec_, lngb_, wcat_, bias1 = carve(g, dict(start=7616, sizes=[KD * 2 * D, 3 * D, 4 * MD, KD * WCOL, WCOL]))
        wkv = wkv_.rearrange("p (k c) -> p k c", k=KD)
        avec = avec_.rearrange("p (a c) -> p a c", a=3)
        lngb = lngb_.rearrange("p (a s d) -> p a s d", a=2, s=2)
        wcat = wcat_.rearrange("p (k c) -> p k c", k=KD)
        bcol, acol = [a.bitcast(I32) for a in carve(g, dict(start=10480, sizes=[EC, EC]))]
        wq_s, wo_s, kvd, t1, base_s = carve(shared, dict(start=0, sizes=[2 * D, 2 * D, 2 * P, 2 * D, 2 * D]))
        wq_s = wq_s.rearrange("p (k c) -> p k c", k=2)
        wo_s = wo_s.rearrange("p (k c) -> p k c", k=2)
        kvd = kvd.rearrange("p (k c) -> p k c", k=2)
        t1 = t1.rearrange("p (k c) -> p k c", k=2)
        base_s = base_s.rearrange("p (b c) -> p b c", b=2)
        mxs = g[:, 4000:4000 + 2 * D].rearrange("p (k n) -> p k n", k=KD)
        logit, msk, pos, m01_, tot, tsc = carve(shared, dict(start=0, sizes=[NT * NE, 2 * NT * NE, NT * NE, NT * NE // 2, 0, 0]))
        logit = logit.rearrange("p (t e) -> p t e", t=NT)
        msk = msk.rearrange("p (j t e) -> p j t e", j=2, t=NT)
        pos = pos.rearrange("p (t e) -> p t e", t=NT)
        m01 = m01_.bitcast(BF16)
        cmp8, cmp8b, xTr, baseg, xn2s, tri8, tsc, tex = carve(
            g, dict(start=0, sizes=[NT * 64, NT * 64, 2 * D, 2 * D, 2 * D, 64, NT * NE, NT * NE]))
        cmp8 = cmp8.rearrange("p (t a b) -> p t a b", t=NT, a=NE)
        cmp8b = cmp8b.rearrange("p (t a b) -> p t a b", t=NT, a=NE)
        xTr = xTr.rearrange("p (k n) -> p k n", k=KD)
        baseg = baseg.rearrange("p (b d) -> p b d", b=2)
        xn2s = xn2s.rearrange("p (b d) -> p b d", b=2)
        tri8 = tri8.rearrange("p (a b) -> p a b", a=NE)
        tsc3 = tsc.rearrange("p (e t) -> p e t", e=NE)
        tex3 = tex.rearrange("p (e t) -> p e t", e=NE)
        w1s, w2s, b1s, b2s, xs_s, xTe, hT = carve(
            g, dict(start=0, sizes=[2 * KD * HID, 2 * FC * D, 2 * FC, 2 * D, 2 * D, 2 * KD * TT, FC * TT]))
        w1s = w1s.rearrange("p (s k f) -> p s k f", s=2, k=KD)
        w2s = w2s.rearrange("p (s c n) -> p s c n", s=2, c=FC)
        b1s = b1s.rearrange("p (s c) -> p s c", s=2)
        b2s = b2s.rearrange("p (s n) -> p s n", s=2)
        xs_s = xs_s.rearrange("p (a d) -> p a d", a=2)
        xTe = xTe.rearrange("p (b k n) -> p b k n", b=2, k=KD)
        hT = hT.rearrange("p (c n) -> p c n", c=FC)
        ysb = shared[:, 0:2 * D].rearrange("p (a d) -> p a d", a=2)
        yg = g[:, 0:4 * D].rearrange("p (b j d) -> p b j d", b=2, j=2)
        ob = g[:, 4 * D:6 * D].rearrange("p (b d) -> p b d", b=2)

        bank = [ctx.enter_context(nc.psum_tensor(f"bank{i}", [P, 512], F32)) for i in range(8)]

        S = {}
        for name in """consts pool_step pool_khat dve_step dve_pass passed dve_unit dve_end dve_out act_step weights_in edges_in x_in
            hist_oh hist_used deg_ready rowp_ps ohd_ready cnt_ps cnt_used rank_ready ord_stored ord_in win_done
            mx_ready mx_done whs_free bases_free var_ready rstd_ready xn_ready tp_ready xT_ready wh_ps wh_ready s2_stored
            kv_ps sq_ready kvar_ready krs_ready kn_ready khat_ready kv_done kvd_ready t1_ps t1_ready mix_ps mix_ready
            mw_in mxs_ready base_ps base_ready winr_ready win_in idx_ready idx_step s2_in f_in ex_in f_ready ex_ready
            accf_ready acc_ps acc_used pass_done v2_ready r2_ready xn2_ready xn2_copied tp2_ready xTr_ready lg_ps
            lg_used m01_ready pre_ps gap_ready gexp_ready slot_ready bounds_ready xs_zeroed xs_done xs_in xte_ps xte_ready
            h_ps h_ready y_ps y_ready ys_done ys_free ob_ready""".split():
            S[name] = sem(name)
        for name in """wh_stored base_stored idxs_ready gath_in prod baseg_in baseg_used ew_in ew_used
            yg_in ob_stored""".split():
            S[name] = [sem(name + "_a"), sem(name + "_b")]

        def signal(name, b=None):
            return S[name] if b is None else S[name][b]

        def apart(eng):
            eng.sem_inc(S["passed"], 1)

        block = ctx.enter_context(nc.Block())
        NLOAD = 15
        NZERO = (2 * XT - YMIN) * TT // P
        unit_bound = NPAIR * (EP // WIN)

        @block.sync
        def _(sp):
            sp.dma_start(bcol, dst.rearrange("(p j) -> p j", j=EC)).then_inc(S["edges_in"], 16)
            w = lambda o, i: sp.dma_start(o, i).then_inc(S["weights_in"], 16)
            w(wcat[:, :, 0:D], gW.rearrange("(k p) c -> p k c", p=P))
            w(avec[:, 0, :], gas.partition_broadcast(P))
            w(avec[:, 1, :], gad.partition_broadcast(P))
            w(avec[:, 2, :], gbW.partition_broadcast(P))
            w(abias[:, :], gab.partition_broadcast(P))
            w(wkv, wkvT.rearrange("(k p) c -> p k c", p=P))
            w(bo_b[:, :], bo.partition_broadcast(P))
            w(lngb_[:, 0:2 * MD], lng.partition_broadcast(P))
            w(lngb_[:, 2 * MD:4 * MD], lnb.partition_broadcast(P))
            w(wg_s[:, :, :], Wg.rearrange("(k p) c -> p k c", p=P))
            w(bg_b[:, :], bg.partition_broadcast(P))
            for i in range(4):
                lo, hi = NT * i // 4, NT * (i + 1) // 4
                w(x_all[:, lo:hi, :], x[lo * P:hi * P, :].rearrange("(t p) d -> p t d", p=P))
            sp.dma_start(win_tab, bass.AP(src.tensor, 0, [[WSTEP, NWROW], [1, WLEN]])).then_inc(S["win_done"], 16)
            sp.wait_ge(S["consts"], 1)
            for i in range(XT * TT // P):
                sp.dma_start(xs_tab[i * P:(i + 1) * P, :], zeros[:, :]).then_inc(S["xs_zeroed"], 16)
            for i in range(YMIN * TT // P, XT * TT // P):
                sp.dma_start(ys_tab[i * P:(i + 1) * P, :], zeros[:, :]).then_inc(S["xs_zeroed"], 16)
            sp.sem_inc(S["whs_free"], 1)
            with sp.Fori(0, NPAIR) as i:
                sp.wait_ge(S["wh_ready"], i + 1)
                for b in range(2):
                    sp.dma_start(wh_tab[bass.ds(i * (2 * P) + b * P, P), :], whs[:, b, 0:ROW]).then_inc(S["wh_stored"][b], 16)
                for b in range(2):
                    sp.wait_ge(S["wh_stored"][b], i * 16 + 16)
                sp.sem_inc(S["whs_free"], 1)
            sp.dma_start(s2_tab.rearrange("(t p) h -> p t h", p=P), s2_all[:, :, :]).then_inc(S["s2_stored"], 16)
            sp.wait_ge(S["ord_stored"], 16 * NT)
            sp.dma_start(ordn[:, :, :], ord_tab.rearrange("(t p) c -> p t c", p=P)).then_inc(S["ord_in"], 16)
            sp.dma_start(wq_s, wq.rearrange("(k p) c -> p k c", p=P)).then_inc(S["mw_in"], 16)
            sp.dma_start(wo_s, woT.rearrange("(k p) c -> p k c", p=P)).then_inc(S["mw_in"], 16)
            sp.sem_inc(S["bases_free"], 1)
            with sp.Fori(0, NPAIR) as i:
                sp.wait_ge(S["base_ready"], i + 1)
                for b in range(2):
                    sp.dma_start(base_tab[bass.ds(i * (2 * P) + b * P, P), :], base_s[:, b, :]).then_inc(S["base_stored"][b], 16)
                for b in range(2):
                    sp.wait_ge(S["base_stored"][b], i * 16 + 16)
                sp.sem_inc(S["bases_free"], 1)
            with sp.Fori(0, NE // 2) as ep:
                for s in range(2):
                    sp.wait_ge(S["ew_used"][s], ep + 1)
                    e = ep * 2 + s
                    ew = lambda o, i: sp.dma_start(o, i).then_inc(S["ew_in"][s], 16)
                    ew(w1s[:, s, :, :], W1[bass.ds(e * D, D), :].rearrange("(k p) f -> p k f", p=P))
                    ew(w2s[:, s, :, :], W2[bass.ds(e * HID, HID), :].rearrange("(c p) n -> p c n", p=P))
                    ew(b1s[:, s, :], b1[bass.ds(e * P, P), :])
                    ew(b2s[:, s, :], b2[bass.ds(e, 1), :].to_broadcast([P, D]))
            sp.wait_ge(S["ob_stored"][0], 16 * NPAIR)
            sp.wait_ge(S["ob_stored"][1], 16 * NPAIR)

        @block.gpsimd
        def _(pool):
            pc = Chain(pool, S["pool_step"])
            pc.step(pool.memset(ident[:, :], 0.0))
            pc.step(pool.memset(ltf[:, :], 1.0))
            pc.step(pool.memset(onesf[:, :], 1.0))
            pc.step(pool.memset(onesb[:, :], 1.0))
            pc.step(pool.memset(zeros[:, :], 0.0))
            pc.step(pool.iota(iota_i[:, :], pattern=[[1, P]], base=0, channel_multiplier=0))
            pc.link(pool.iota(node_i[:, :], pattern=[[P, NT]], base=0, channel_multiplier=1))
            pc.step(pool.affine_select(out=ident[:, :], in_=ident[:, :], compare_op=ALU.not_equal, fill=1.0,
                                       base=0, pattern=[[-1, P]], channel_multiplier=1))
            pc.step(pool.affine_select(out=ltf[:, :], in_=ltf[:, :], compare_op=ALU.is_gt, fill=0.0,
                                       base=0, pattern=[[1, P]], channel_multiplier=-1))
            pc.link(pool.tensor_copy(iota_f[:, :], iota_i[:, :]))
            pool.tensor_copy(ltb[:, :], ltf[:, :]).then_inc(S["consts"], 1)

            pool.wait_ge(S["rank_ready"], 1)
            for t in range(NT):
                pool.indirect_dma_start(out=ord_tab, out_offset=bass.IndirectOffsetOnAxis(ap=ranki[:, t:t + 1], axis=0),
                                        in_=ordn[:, t, :], in_offset=None).then_inc(S["ord_stored"], 16)

            def khat(n, first):
                for b in range(2):
                    pool.wait_ge(S["kn_ready"], n + b)
                    v = kvs[:, b, :].rearrange("p (s h d) -> p s h d", s=2, h=MH)
                    for s in range(2):
                        gain = lngb[:, 0, s, :].unsqueeze(1).to_broadcast([P, MH, MD])
                        pool.tensor_tensor(v[:, s], v[:, s], gain, ALU.mult).then_inc(S["pool_khat"], 1)
                    pool.wait_ge(S["pool_khat"], first + 2 * b)
                    for s in range(2):
                        add = lngb[:, 1, s, :].unsqueeze(1).to_broadcast([P, MH, MD])
                        last = pool.tensor_tensor(v[:, s], v[:, s], add, ALU.add)
                    last.then_inc(S["khat_ready"], 1)

            with pool.Fori(0, NPAIR) as i:
                khat(i * 2 + 1, i * 4 + 2)

            pool.wait_ge(S["mx_ready"], 1)
            pool.partition_all_reduce(mxrem[:, :], deg[:, :], P, MAXOP).then_inc(S["mx_done"], 1)
            pool.wait_ge(S["s2_stored"], 16)
            pool.wait_ge(S["ord_in"], 16)
            for t in range(NT):
                pool.indirect_dma_start(out=s2_all[:, t, :], out_offset=None, in_=s2_tab,
                                        in_offset=bass.IndirectOffsetOnAxis(ap=ordn[:, t, 0:1], axis=0)).then_inc(S["s2_in"], 16)

            pool.wait_ge(S["win_done"], 16)
            for b in range(2):
                pool.wait_ge(S["wh_stored"][b], 16 * NPAIR)
            pool.wait_ge(S["winr_ready"], 1)
            nw = pool.value_load(nwin[0:1, 0:1], min_val=1, max_val=EP // WIN)
            with pool.Fori(0, nw) as w:
                pool.wait_ge(S["winr_ready"], w + 1)
                apart(pool)
                lo = pool.value_load(ctl[0:1, 0:1], min_val=0, max_val=unit_bound)
                npr = pool.value_load(ctl[0:1, 3:4], min_val=1, max_val=NPAIR)
                ngr = pool.value_load(ctl[0:1, 2:3], min_val=1, max_val=NT // WT)
                for gr in range(NT // WT):
                    with pool.If(ngr > gr):
                        for t in range(gr * WT, (gr + 1) * WT):
                            pool.indirect_dma_start(out=wina[:, t, :], out_offset=None, in_=win_tab,
                                                    in_offset=bass.IndirectOffsetOnAxis(ap=winr[:, t:t + 1], axis=0)
                                                    ).then_inc(S["win_in"], 16)
                pool.wait_ge(S["idx_ready"], w + 1)
                apart(pool)
                with pool.Fori(0, npr) as i:
                    u = i + lo
                    for b in range(2):
                        pool.wait_ge(S["idxs_ready"][b], u + 1)
                        ng = pool.value_load(groups[0:1, bass.ds(i * 2 + b, 1)], min_val=1, max_val=NG)
                        for q in range(NG):
                            with pool.If(ng > q):
                                for k in range(q * SG, (q + 1) * SG):
                                    pool.indirect_dma_start(
                                        out=gath[:, b, k, :], out_offset=None, in_=wh_tab,
                                        in_offset=bass.IndirectOffsetOnAxis(ap=idxs[:, b, k:k + 1], axis=0)
                                        ).then_inc(S["gath_in"][b], 16)
                pool.wait_ge(S["pass_done"], w + 1)

            for b in range(2):
                pool.wait_ge(S["base_stored"][b], 16 * NPAIR)
            for t in range(NT):
                b = t % 2
                if t >= 2:
                    pool.wait_ge(S["baseg_used"][b], t // 2)
                pool.indirect_dma_start(out=baseg[:, b, :], out_offset=None, in_=base_tab,
                                        in_offset=bass.IndirectOffsetOnAxis(ap=ordn[:, t, 0:1], axis=0)
                                        ).then_inc(S["baseg_in"][b], 16)
            pool.wait_ge(S["slot_ready"], 1)
            pool.wait_ge(S["xs_zeroed"], 16 * NZERO)
            for t in range(NT):
                for j in range(2):
                    pool.indirect_dma_start(out=xs_tab, out_offset=bass.IndirectOffsetOnAxis(ap=sloti[:, j, t:t + 1], axis=0),
                                            in_=xn2_all[:, t, :], in_offset=None,
                                            bounds_check=XT * TT - 1, oob_is_err=False).then_inc(S["xs_done"], 16)
            pool.wait_ge(S["xs_done"], 16 * 2 * NT)
            ntile = pool.value_load(ebnd[0:1, 1, NE - 1:NE], min_val=1, max_val=XT - 1)
            pool.sem_inc(S["ys_free"], 1)

            def load_xs(i):
                pool.dma_start(xs_s, xs_tab[bass.ds(i * TT, TT), :].rearrange("(a p) d -> p a d", p=P)).then_inc(S["xs_in"], 16)

            pool.dma_start(xs_s, xs_tab[0:TT, :].rearrange("(a p) d -> p a d", p=P)).then_inc(S["xs_in"], 16)
            with pool.Fori(0, ntile) as i:
                pool.wait_ge(S["xte_ps"], i + 1)
                load_xs(i + 1)
                pool.wait_ge(S["y_ready"], i + 2)
                pool.dma_start(ys_tab[bass.ds(i * TT, TT), :].rearrange("(a p) d -> p a d", p=P), ysb).then_inc(S["ys_done"], 16)
                pool.wait_ge(S["ys_done"], i * 16 + 16)
                pool.sem_inc(S["ys_free"], 1)
            def gather_y(t):
                for j in range(2):
                    pool.indirect_dma_start(out=yg[:, t % 2, j, :], out_offset=None, in_=ys_tab,
                                            in_offset=bass.IndirectOffsetOnAxis(ap=sloti[:, j, t:t + 1], axis=0),
                                            bounds_check=XT * TT - 1, oob_is_err=False).then_inc(S["yg_in"][t % 2], 16)

            pool.wait_ge(S["ob_ready"], 1)
            gather_y(0)
            gather_y(1)
            for t in range(NT):
                pool.wait_ge(S["ob_ready"], t + 2)
                pool.indirect_dma_start(out=out, out_offset=bass.IndirectOffsetOnAxis(ap=ordn[:, t, 0:1], axis=0),
                                        in_=ob[:, t % 2, :], in_offset=None,
                                        bounds_check=N - 1, oob_is_err=False).then_inc(S["ob_stored"][t % 2], 16)
                if t + 2 < NT:
                    gather_y(t + 2)

        @block.scalar
        def _(act):
            def root(o, i, ready):
                nc.scalar.activation(o, i, ACT.Sqrt).then_inc(ready, 1)

            act.wait_ge(S["var_ready"], 1)
            root(rs[:, :, 1], rs[:, :, 0], S["rstd_ready"])

            def evacuate(i, first=False):
                act.wait_ge(S["tp_ready"], i + 1)
                if not first:
                    act.wait_ge(S["kv_ps"], i * 2)
                nc.scalar.copy(xTs, bank[5][:, :].rearrange("p (k n) -> p k n", k=KD)).then_inc(S["xT_ready"], 1)
                nc.scalar.copy(xT_all[:, :, bass.ds(i * (2 * P), 2 * P)],
                               bank[5][:, :].rearrange("p (k n) -> p k n", k=KD)).then_inc(S["xT_ready"], 1)

            def squares(i):
                for b in range(2):
                    act.wait_ge(S["kv_ps"], i * 2 + (b + 1))
                    nc.scalar.activation(kvq[:, b, :], bank[2 + b][:, :], ACT.Square).then_inc(S["sq_ready"], 1)
                act.wait_ge(S["kvar_ready"], i + 1)
                root(kvr[:, 1, :, :], kvr[:, 0, :, :], S["krs_ready"])

            def first_phase(i, first=False):
                evacuate(i, first)
                act.wait_ge(S["var_ready"], i + 2)
                root(rs[:, :, 1], rs[:, :, 0], S["rstd_ready"])
                squares(i)

            first_phase(0, True)
            with act.Fori(1, NPAIR - 1) as i:
                first_phase(i)
            evacuate(NPAIR - 1)
            squares(NPAIR - 1)

            with act.Fori(0, NPAIR) as i:
                act.wait_ge(S["base_ps"], i + 1)
                nc.scalar.copy(mxs, xT_all[:, :, bass.ds(i * (2 * P), 2 * P)]).then_inc(S["mxs_ready"], 1)

            act.wait_ge(S["winr_ready"], 1)
            nw = act.value_load(nwin[0:1, 0:1], min_val=1, max_val=EP // WIN)
            with act.Fori(0, nw) as w:
                act.wait_ge(S["winr_ready"], w + 1)
                apart(act)
                lo = act.value_load(ctl[0:1, 0:1], min_val=0, max_val=unit_bound)
                npr = act.value_load(ctl[0:1, 3:4], min_val=1, max_val=NPAIR)
                with act.Fori(0, npr) as i:
                    u = i + lo
                    for b in range(2):
                        act.wait_ge(S["f_in"], u * 2 + (b + 1))
                        nc.scalar.activation(es[:, 3, :], es[:, 2, :], ACT.Exp).then_inc(S["f_ready"], 1)
                        act.wait_ge(S["ex_in"], u * 2 + (b + 1))
                        nc.scalar.activation(ez[:, :, :], ez[:, :, :], ACT.Exp).then_inc(S["ex_ready"], 1)
                act.wait_ge(S["pass_done"], w + 1)

            with act.Fori(0, NPAIR) as i:
                act.wait_ge(S["v2_ready"], i + 1)
                root(rs[:, :, 1], rs[:, :, 0], S["r2_ready"])
                act.wait_ge(S["xn2_ready"], i + 1)
                nc.scalar.copy(xn2_all[:, bass.ds(i * 2, 2), :], xn2s).then_inc(S["xn2_copied"], 1)
                act.wait_ge(S["tp2_ready"], i + 1)
                nc.scalar.copy(xTr, bank[5][:, :].rearrange("p (k n) -> p k n", k=KD)).then_inc(S["xTr_ready"], 1)
            act.wait_ge(S["gap_ready"], 1)
            nc.scalar.activation(small[:, 3, :], small[:, 2, :], ACT.Exp).then_inc(S["gexp_ready"], 1)

            act.sem_inc(S["h_ready"], 4)
            act.wait_ge(S["bounds_ready"], 1)
            with act.Fori(0, NE // 2) as ep:
                for s in range(2):
                    lo = act.value_load(ebnd[0:1, 0, bass.ds(ep * 2 + s, 1)], min_val=0, max_val=XT - 2)
                    hi = act.value_load(ebnd[0:1, 1, bass.ds(ep * 2 + s, 1)], min_val=1, max_val=XT - 1)
                    act.wait_ge(S["ew_in"][s], ep * 64 + 64)
                    with act.Fori(lo, hi) as i:
                        for c in range(FC):
                            act.wait_ge(S["h_ps"], i * FC + (c + 1))
                            nc.scalar.activation(hT[:, c, :], bank[c % 4][:, 0:TT], ACT.Gelu,
                                                 bias=b1s[:, s, c:c + 1]).then_inc(S["h_ready"], 1)

        @block.vector
        def _(v):
            ch = Chain(v, S["dve_step"])
            tt, ts = nc.vector.tensor_tensor, nc.vector.tensor_scalar

            def inner_sum(o, i):
                return nc.vector.tensor_reduce(o, i, AX.X, ALU.add)

            v.wait_ge(S["edges_in"], 16)
            v.wait_ge(S["consts"], 1)
            ch.link(ts(acol, bcol, 7, None, ALU.arith_shift_right))
            ch.link(ts(bcol, bcol, P - 1, None, ALU.bitwise_and))
            base = ch.n
            with v.Fori(0, NHIST) as i:
                for a in range(2):
                    v.wait_ge(S["hist_used"], i * 2 + (a + 1))
                    cols = bass.ds(i * (2 * HC) + a * HC, HC)
                    tt(oh_b[:, a], bcol[:, cols].unsqueeze(2).to_broadcast([P, HC, P]),
                       iota_i[:, :].unsqueeze(1).to_broadcast([P, HC, P]), ALU.is_equal)
                    tt(oh_a[:, a], acol[:, cols].unsqueeze(2).to_broadcast([P, HC, NT]),
                       iota_i[:, 0:NT].unsqueeze(1).to_broadcast([P, HC, NT]), ALU.is_equal).then_inc(S["hist_oh"], 1)
            v.wait_ge(S["hist_used"], 2 * NHIST + 3)
            ch.link(nc.vector.tensor_copy(deg[:, :], bank[0][:, 0:NT]))
            v.sem_inc(S["deg_ready"], 1)

            v.wait_ge(S["rowp_ps"], 1)
            ch.link(nc.vector.tensor_tensor_scan(small[:, 0, :], onesf[:, 0:NT], bank[1][:, 64:64 + NT], 0.0, ALU.mult, ALU.add))
            ch.link(tt(small[:, 1, :], small[:, 0, :], bank[1][:, 64:64 + NT], ALU.subtract))
            ch.link(tt(rowp[:, :], small[:, 1, :], bank[1][:, 0:NT], ALU.add))

            ch.link(ts(small[:, 2, :], deg[:, :], float(NBUCK - 1), -1.0, ALU.min, ALU.mult))
            ch.link(ts(small[:, 3, :], small[:, 2, :], float(NBUCK - 1), None, ALU.add))
            ch.step(tt(oh_d, small[:, 3, :].unsqueeze(2).to_broadcast([P, NT, NBUCK]),
                       iota_f[:, 0:NBUCK].unsqueeze(1).to_broadcast([P, NT, NBUCK]), ALU.is_equal))
            ch.wait()
            v.sem_inc(S["ohd_ready"], 1)
            rin = r_in.rearrange("p (t c) -> p t c", t=NT)
            rc = r_cnt.rearrange("p (c t) -> p c t", t=NT)
            rsc = r_scan.rearrange("p (c t) -> p c t", t=NT)
            for n, lo in enumerate(range(0, NT, BT)):
                k = min(BT, NT - lo)
                v.wait_ge(S["cnt_ps"], n + 1)
                bk = 2 + 2 * (n % 2)
                ch.step(nc.vector.tensor_copy(rin[:, lo:lo + k, :], bank[bk][:, 0:k * NBUCK].rearrange("p (t c) -> p t c", t=k)))
                ch.step(nc.vector.tensor_copy(rc[:, :, lo:lo + k], bank[bk + 1][:, 0:k * NBUCK].rearrange("p (t c) -> p c t", t=k)))
                ch.wait()
                v.sem_inc(S["cnt_used"], 1)
            ch.link(nc.vector.tensor_tensor_scan(r_scan, onesf[:, 0:1].to_broadcast([P, NT * NBUCK]), r_cnt, 0.0, ALU.mult, ALU.add))
            ch.link(tt(r_scan, r_scan, r_cnt, ALU.subtract))
            ch.link(tt(rin, rin, rsc.rearrange("p c t -> p t c"), ALU.add))
            ch.link(tt(rin, rin, oh_d, ALU.mult))
            ch.link(inner_sum(small[:, 2, :], rin))
            ch.step(nc.vector.tensor_copy(ranki[:, :], small[:, 2, :]))
            ch.step(nc.vector.tensor_copy(ordn[:, :, 0], node_i[:, :]))
            ch.step(nc.vector.tensor_copy(ordn[:, :, 1], rowp[:, :]))
            ch.step(nc.vector.tensor_copy(ordn[:, :, 2], deg[:, :]))
            ch.step(nc.vector.memset(ordn[:, :, 3], 0))
            ch.wait()
            v.sem_inc(S["rank_ready"], 1)

            v.wait_ge(S["weights_in"], 16 * NLOAD)
            for s in range(2):
                tmp = kvq[:, :, s * D:(s + 1) * D]
                ch.link(tt(tmp, wcat[:, :, 0:D], avec[:, s, :].unsqueeze(1).to_broadcast([P, KD, D]), ALU.mult))
                ch.step(inner_sum(wcat[:, :, D + s * H:D + (s + 1) * H], tmp.rearrange("p k (h d) -> p k h d", h=H)))
                ch.link(tt(whs[:, s, 0:D], avec[:, 2, :], avec[:, s, :], ALU.mult))
                ch.step(inner_sum(bias1[:, D + s * H:D + (s + 1) * H], whs[:, s, 0:D].rearrange("p (h d) -> p h d", h=H)))
            ch.step(nc.vector.tensor_copy(bias1[:, 0:D], avec[:, 2, :]))
            ch.wait()
            ch.link(tt(bias1[:, D + H:WCOL], bias1[:, D + H:WCOL], abias[:, :], ALU.add))
            wk4 = wkv.rearrange("p k (h d) -> p k h d", d=MD)
            ch.link(inner_sum(kvr[:, 0, :, :], wk4))
            ch.link(ts(kvr[:, 1, :, :], kvr[:, 0, :, :], -1.0 / MD, None, ALU.mult))
            for k in range(KD):
                ch.step(tt(wk4[:, k], wk4[:, k], kvr[:, 1, k, :].unsqueeze(2).to_broadcast([P, 8, MD]), ALU.add))
            ch.wait()

            def variance(ch, rows):
                for b in range(2):
                    ch.step(nc.vector.bn_stats(stats[:, b, :], rows(b)))
                ch.wait()
                apart(v)
                for b in range(2):
                    ch.step(nc.vector.bn_aggr(mv[:, b, :], stats[:, b, :]))
                ch.wait()
                ch.link(ts(stats[:, :, 0], mv[:, :, 1], EPS, None, ALU.add))
                ch.link(nc.vector.reciprocal(rs[:, :, 0], stats[:, :, 0]))

            def x_rows(i):
                return lambda b: x_all[:, bass.ds(i * 2 + b, 1), :].rearrange("p o d -> p (o d)")

            def scaled(ch, o, rows):
                for b in range(2):
                    ch.step(ts(o[:, b, :], rows(b), mv[:, b, 0:1], rs[:, b, 1:2], ALU.subtract, ALU.mult))
                ch.wait()

            def products(i):
                v.wait_ge(S["wh_ps"], i + 1)
                v.wait_ge(S["whs_free"], i + 1)
                for b in range(2):
                    ch.step(tt(whs[:, b, :], bank[b][:, 0:WCOL], bias1, ALU.add))
                ch.wait()
                ch.step(nc.vector.tensor_copy(s2_all[:, bass.ds(i * 2, 2), :], whs[:, :, ROW:WCOL]))
                ch.wait()
                v.sem_inc(S["wh_ready"], 1)
                for b in range(2):
                    v.wait_ge(S["sq_ready"], i * 2 + (b + 1))
                    ch.step(inner_sum(kvr[:, 0, b, :], kvq[:, b, :].rearrange("p (h d) -> p h d", d=MD)))
                ch.wait()
                ch.link(ts(kvr[:, 0, :, :], kvr[:, 0, :, :], 1.0 / MD, EPS, ALU.mult, ALU.add))
                ch.link(nc.vector.reciprocal(kvr[:, 0, :, :], kvr[:, 0, :, :]))
                v.sem_inc(S["kvar_ready"], 1)
                v.wait_ge(S["krs_ready"], i + 1)
                v.wait_ge(S["kv_done"], i + 1)
                for b in range(2):
                    tt(kvs[:, b, :].rearrange("p (h d) -> p h d", d=MD), bank[2 + b][:, :].rearrange("p (h d) -> p h d", d=MD),
                       kvr[:, 1, b, :].unsqueeze(2).to_broadcast([P, 8, MD]), ALU.mult).then_inc(S["kn_ready"], 1)

            variance(ch, x_rows(0))
            v.sem_inc(S["var_ready"], 1)
            v.wait_ge(S["rstd_ready"], 1)
            scaled(ch, xn, x_rows(0))
            v.sem_inc(S["xn_ready"], 1)
            start, per = ch.base + ch.n, 15
            with v.Fori(0, NPAIR - 1) as i:
                ch.at(i * per + start)
                variance(ch, x_rows(i + 1))
                v.sem_inc(S["var_ready"], 1)
                v.wait_ge(S["rstd_ready"], i + 2)
                v.wait_ge(S["tp_ready"], i + 1)
                scaled(ch, xn, x_rows(i + 1))
                v.sem_inc(S["xn_ready"], 1)
                products(i)
                assert ch.n == per, ch.n
            ch.at(start + (NPAIR - 1) * per)
            products(NPAIR - 1)

            v.wait_ge(S["ord_in"], 16)
            ch.step(nc.vector.tensor_copy(rowp[:, :], ordn[:, :, 1]))
            ch.step(nc.vector.tensor_copy(deg[:, :], ordn[:, :, 2]))
            ch.step(ts(valid[:, :], ordn[:, :, 0], float(N), None, ALU.is_lt))
            ch.step(nc.vector.memset(m_all[:, :, :], LOW))
            ch.step(nc.vector.memset(den_all[:, :, :], 0.0))
            ch.step(nc.vector.memset(ctlf[:, :], 0.0))
            ch.wait()
            v.sem_inc(S["mx_ready"], 1)
            v.wait_ge(S["mx_done"], 1)
            ch.link(nc.vector.tensor_reduce(ctlf[:, 3:4], mxrem[:, :], AX.X, ALU.max))
            ch.link(ts(ctlf[:, 3:4], ctlf[:, 3:4], (WIN - 1) / 2, 1.0 / WIN, ALU.add, ALU.mult))
            ch.link(nc.vector.tensor_copy(nwin[:, :], ctlf[:, 3:4]))
            ch.link(ts(nwin[:, :], nwin[:, :], 1, None, ALU.max))

            v.wait_ge(S["kv_done"], NPAIR + 2)
            ch.link(nc.vector.memset(kvd, 0.0))
            for j in range(2):
                for q in range(2):
                    r = slice(q * MD, (q + 1) * MD)
                    ch.step(ts(kvd[r, j, r], bank[4][r, j * P + q * MD:j * P + (q + 1) * MD], 1.0 / N, None, ALU.mult))
            ch.wait()
            v.sem_inc(S["kvd_ready"], 1)
            v.wait_ge(S["t1_ps"], 1)
            ch.link(nc.vector.tensor_copy(t1, bank[6][:, :].rearrange("p (k c) -> p k c", k=2)))
            v.sem_inc(S["t1_ready"], 1)
            v.wait_ge(S["mix_ps"], 1)
            ch.link(nc.vector.tensor_copy(mixw[:, :, :], bank[7][:, :].rearrange("p (k c) -> p k c", k=2)))
            v.sem_inc(S["mix_ready"], 1)
            start, per = ch.base + ch.n, 4
            with v.Fori(0, NPAIR) as i:
                ch.at(i * per + start)
                v.wait_ge(S["base_ps"], i + 2)
                v.wait_ge(S["bases_free"], i + 1)
                for b in range(2):
                    ch.step(tt(base_s[:, b, :], bank[b][:, 0:D], bo_b[:, :], ALU.add))
                ch.wait()
                for b in range(2):
                    ch.step(tt(base_s[:, b, :], base_s[:, b, :], x_rows(i)(b), ALU.add))
                ch.wait()
                v.sem_inc(S["base_ready"], 1)
                assert ch.n == per, ch.n
            ch.at(start + NPAIR * per)
            ch.step(nc.vector.memset(x_all[:, :, :], 0.0))
            ch.wait()

            cp, ci, cu = Chain(v, S["dve_pass"]), Chain(v, S["idx_step"]), Chain(v, S["dve_unit"])
            PASS, IDX, UNIT = 32, 9, 14
            nw = v.value_load(nwin[0:1, 0:1], min_val=1, max_val=EP // WIN)
            with v.Fori(0, nw) as w:
                cp.at(w * (PASS + 4))
                cp.link(ts(small[:, 0, :], mxrem[:, :], float(SG - 1), None, ALU.add))
                cp.link(nc.vector.tensor_copy(groups[:, :], small[:, 0, :]))
                cp.link(ts(groups[:, :], groups[:, :], SG.bit_length() - 1, None, ALU.arith_shift_right))
                cp.step(ts(groups[:, :], groups[:, :], 1, NG, ALU.max, ALU.min))
                cp.link(ts(small[:, 1, :], mxrem[:, :], 0.0, None, ALU.is_gt))
                cp.link(inner_sum(ctlf[:, 1:2], small[:, 1, :]))
                cp.step(ts(ctl[:, 1:2], ctlf[:, 1:2], 1.0, None, ALU.add))
                cp.link(ts(ctlf[:, 2:3], ctlf[:, 1:2], float(WT - 1), None, ALU.add))
                cp.step(ts(ctl[:, 1:2], ctl[:, 1:2], 1, None, ALU.arith_shift_right))
                cp.link(ts(ctlf[:, 2:3], ctlf[:, 2:3], -(WT - 1) / 2, 1.0 / WT, ALU.add, ALU.mult))
                cp.step(nc.vector.tensor_copy(ctl[:, 2:3], ctlf[:, 2:3]))
                cp.link(nc.vector.tensor_copy(ctl[:, 0:1], ctlf[:, 0:1]))
                cp.link(ts(ctl[:, 1:3], ctl[:, 1:3], 1, None, ALU.max))
                cp.link(nc.vector.tensor_copy(ctl[:, 3:4], ctl[:, 1:2]))
                cp.step(tt(ctlf[:, 4:5], ctlf[:, 4:5], ctl[:, 2:3], ALU.add))
                cp.link(ts(ctlf[:, 1:2], ctl[:, 3:4], 2.0, None, ALU.mult))
                cp.step(nc.vector.tensor_copy(ctl[:, 4:5], ctlf[:, 4:5]))
                cp.link(ts(gmask[:, :], iota_f[:, 0:NT], ctlf[:, 1:2], None, ALU.is_lt))
                cp.link(tt(gmask[:, :], gmask[:, :], groups[:, :], ALU.mult))
                for b in range(2):
                    cp.step(nc.vector.tensor_tensor_scan(gcumf[:, b, :], onesf[:, 0:NPAIR], gmask[:, :].rearrange("p (i b) -> p b i", b=2)[:, b, :],
                                                         ctlf[:, 5 + b:6 + b], ALU.mult, ALU.add))
                cp.wait()
                cp.step(nc.vector.tensor_copy(ctlf[:, 5:7], gcumf[:, :, NPAIR - 1]))
                cp.step(nc.vector.tensor_copy(gcum[:, :, :], gcumf[:, :, :]))
                cp.step(tt(gbase[:, :, :], gcumf[:, :, :], groups[:, :].rearrange("p (i b) -> p b i", b=2), ALU.subtract))
                cp.link(ts(ctl[:, 1:2], ctl[:, 1:2], ctlf[:, 0:1], None, ALU.add))
                cp.link(nc.vector.tensor_copy(starti[:, :], rowp[:, :]))
                cp.step(ts(winr[:, :], starti[:, :], WSTEP.bit_length() - 1, None, ALU.arith_shift_right))
                for n in range(4):
                    cp.step(ts(bits[:, n, :], starti[:, :], n, 1, ALU.arith_shift_right, ALU.bitwise_and))
                cp.wait()
                cp.step(ts(winr[:, :], winr[:, :], NWROW - 1, None, ALU.min))
                cp.wait()
                assert cp.n == PASS, cp.n
                v.sem_inc(S["winr_ready"], 1)
                lo = v.value_load(ctl[0:1, 0:1], min_val=0, max_val=unit_bound)
                npr = v.value_load(ctl[0:1, 3:4], min_val=1, max_val=NPAIR)
                ngr = v.value_load(ctl[0:1, 2:3], min_val=1, max_val=NT // WT)
                nwt = v.value_load(ctl[0:1, 4:5], min_val=1, max_val=NT * EP)
                v.wait_ge(S["win_in"], nwt * (16 * WT))
                ci.at(w * (IDX * NT // WT))
                for gr in range(NT // WT):
                    tiles = slice(gr * WT, (gr + 1) * WT)
                    with v.If(ngr > gr):
                        n0, cur, other, width = ci.n, wina, winb, WLEN
                        for n in (3, 2, 1, 0):
                            width -= 1 << n
                            o = other[:, tiles, 0:width] if n else idx[:, tiles, 0:WIN]
                            take = width if n else WIN
                            ci.link(nc.vector.tensor_copy(o, cur[:, tiles, 0:take]))
                            apart(v)
                            ci.link(nc.vector.copy_predicated(o, bits[:, n, tiles].unsqueeze(2).to_broadcast([P, WT, take]),
                                                              cur[:, tiles, (1 << n):(1 << n) + take]))
                            cur, other = other, cur
                        ci.link(nc.vector.tensor_copy(small[:, 0, tiles], small[:, 1, tiles]))
                        apart(v)
                        assert ci.n - n0 == IDX, ci.n - n0
                    with v.Else():
                        v.sem_inc(S["idx_step"], IDX)
                v.sem_inc(S["idx_ready"], 1)

                def stage(i, b):
                    nc.vector.tensor_copy(idxs[:, b, :], idx[:, bass.ds(i * 2 + b, 1), :].rearrange("p o k -> p (o k)")
                                          ).then_inc(S["idxs_ready"][b], 1)

                for b in range(2):
                    stage(0, b)
                with v.Fori(0, npr) as i:
                    u = i + lo
                    for b in range(2):
                        cu.at(u * (2 * UNIT) + b * UNIT)
                        t = i * 2 + b
                        one = lambda a: a[:, bass.ds(t, 1), :].rearrange("p o h -> p (o h)")
                        ngath = v.value_load(gcum[0:1, b, bass.ds(i, 1)], min_val=1, max_val=NT * EP)
                        v.wait_ge(S["gath_in"][b], ngath * (16 * SG))
                        cu.step(ts(pen[:, :], iota_f[:, 0:WIN], deg[:, bass.ds(t, 1)], LOWER, ALU.is_ge, ALU.mult))
                        cu.link(tt(ez[:, :, :], gath[:, b, :, D:ROW], s2_all[:, bass.ds(t, 1), :].to_broadcast([P, WIN, H]), ALU.add))
                        cu.link(nc.vector.scalar_tensor_tensor(ez[:, :, :], ez[:, :, :], ALPHA, ez[:, :, :], ALU.mult, ALU.max))
                        cu.link(tt(ez[:, :, :], ez[:, :, :], pen[:, :].unsqueeze(2).to_broadcast([P, WIN, H]), ALU.add))
                        cu.link(nc.vector.tensor_reduce(es[:, 0, :], ez[:, :, :].rearrange("p k h -> p h k"), AX.X, ALU.max))
                        cu.link(tt(es[:, 1, :], es[:, 0, :], one(m_all), ALU.max))
                        cu.link(tt(es[:, 2, :], one(m_all), es[:, 1, :], ALU.subtract))
                        v.sem_inc(S["f_in"], 1)
                        cu.step(nc.vector.tensor_copy(one(m_all), es[:, 1, :]))
                        cu.link(tt(ez[:, :, :], ez[:, :, :], es[:, 1, :].unsqueeze(1).to_broadcast([P, WIN, H]), ALU.subtract))
                        v.sem_inc(S["ex_in"], 1)
                        v.wait_ge(S["f_ready"], u * 2 + (b + 1))
                        cu.step(tt(accf[:, :].rearrange("p (h d) -> p h d", h=H), one(x_all).rearrange("p (h d) -> p h d", h=H),
                                   es[:, 3, :].unsqueeze(2).to_broadcast([P, H, DH]), ALU.mult))
                        cu.step(tt(es[:, 4, :], one(den_all), es[:, 3, :], ALU.mult))
                        cu.wait()
                        v.sem_inc(S["accf_ready"], 1)
                        v.wait_ge(S["ex_ready"], u * 2 + (b + 1))
                        ng = v.value_load(groups[0:1, bass.ds(t, 1)], min_val=1, max_val=NG)
                        for q in range(NG):
                            ks = slice(q * SG, (q + 1) * SG)
                            rows = gath[:, b, ks, 0:D].rearrange("p k (h d) -> p k h d", h=H)
                            with v.If(ng > q):
                                tt(rows, rows, ez[:, ks, :].unsqueeze(3).to_broadcast([P, SG, H, DH]), ALU.mult).then_inc(S["prod"][b], 1)
                        cu.link(nc.vector.tensor_reduce(es[:, 5, :], ez[:, :, :].rearrange("p k h -> p h k"), AX.X, ALU.add))
                        cu.step(tt(one(den_all), es[:, 4, :], es[:, 5, :], ALU.add))
                        v.wait_ge(S["acc_ps"], u * 2 + (b + 1))
                        apart(v)
                        cu.step(nc.vector.tensor_copy(one(x_all), bank[b][:, 0:D]))
                        cu.wait()
                        apart(v)
                        assert cu.n == UNIT, cu.n
                        with v.If(i < npr - 1):
                            stage(i + 1, b)
                v.wait_ge(S["dve_unit"], (lo + npr) * (2 * UNIT))
                apart(v)
                cp.step(ts(deg[:, :], deg[:, :], -float(WIN), None, ALU.add))
                cp.step(ts(rowp[:, :], rowp[:, :], float(WIN), None, ALU.add))
                cp.step(ts(mxrem[:, :], mxrem[:, :], -float(WIN), None, ALU.add))
                cp.step(nc.vector.tensor_copy(ctlf[:, 0:1], ctl[:, 1:2]))
                cp.wait()
                assert cp.n == PASS + 4
                v.sem_inc(S["pass_done"], 1)

            ce = Chain(v, S["dve_end"])
            ce.link(ts(den_all[:, :, :], den_all[:, :, :], 1e-30, None, ALU.max))
            ce.link(nc.vector.reciprocal(den_all[:, :, :], den_all[:, :, :]))
            start, per = ce.n, 14
            with v.Fori(0, NPAIR) as i:
                ce.at(i * per + start)
                heads = lambda a: a.rearrange("p (h d) -> p h d", h=H)
                for b in range(2):
                    ce.step(tt(heads(x_rows(i)(b)), heads(x_rows(i)(b)),
                               den_all[:, bass.ds(i * 2 + b, 1), :].rearrange("p o h -> p (o h)").unsqueeze(2).to_broadcast([P, H, DH]), ALU.mult))
                ce.wait()
                for b in range(2):
                    v.wait_ge(S["baseg_in"][b], i * 16 + 16)
                    ins = tt(x_rows(i)(b), x_rows(i)(b), baseg[:, b, :], ALU.add)
                    ce.step(ins)
                ce.wait()
                for b in range(2):
                    v.sem_inc(S["baseg_used"][b], 1)
                variance(ce, x_rows(i))
                v.sem_inc(S["v2_ready"], 1)
                v.wait_ge(S["r2_ready"], i + 1)
                scaled(ce, xn2s, x_rows(i))
                v.sem_inc(S["xn2_ready"], 1)
                v.wait_ge(S["lg_ps"], i + 1)
                ce.step(tt(logit[:, bass.ds(i * 2, 2), :], bank[6][:, 0:2 * NE].rearrange("p (b e) -> p b e", b=2),
                           bg_b[:, :].unsqueeze(1).to_broadcast([P, 2, NE]), ALU.add))
                ce.step(nc.vector.memset(tri8[:, 0, 0:1], 0.0))
                ce.wait()
                assert ce.n == per, ce.n
            ce.at(start + NPAIR * per)

            bt = lambda a: a.unsqueeze(2).to_broadcast([P, NT, NE, NE])
            be = lambda a: a.unsqueeze(3).to_broadcast([P, NT, NE, NE])
            ce.step(tt(cmp8, bt(logit), be(logit), ALU.is_gt))
            ce.step(tt(cmp8b, bt(logit), be(logit), ALU.is_equal))
            ce.step(tt(tri8, iota_f[:, 0:NE].unsqueeze(1).to_broadcast([P, NE, NE]),
                       iota_f[:, 0:NE].unsqueeze(2).to_broadcast([P, NE, NE]), ALU.is_lt))
            ce.wait()
            ce.link(tt(cmp8b, cmp8b, tri8.unsqueeze(1).to_broadcast([P, NT, NE, NE]), ALU.mult))
            ce.link(tt(cmp8, cmp8, cmp8b, ALU.add))
            ce.link(inner_sum(pos, cmp8))
            for j in range(2):
                ce.step(ts(msk[:, j], pos, float(j), None, ALU.is_equal))
            ce.wait()
            for j in range(2):
                ce.step(tt(cmp8[:, :, j, :], msk[:, j], logit, ALU.mult))
            ce.wait()
            for j in range(2):
                ce.step(inner_sum(small[:, j, :], cmp8[:, :, j, :]))
            ce.wait()
            ce.link(tt(small[:, 2, :], small[:, 1, :], small[:, 0, :], ALU.subtract))
            v.sem_inc(S["gap_ready"], 1)
            for j in range(2):
                ce.step(tt(msk[:, j], msk[:, j], valid[:, :].unsqueeze(2).to_broadcast([P, NT, NE]), ALU.mult))
            ce.wait()
            ce.link(tt(m01.rearrange("p (t e) -> p t e", t=NT), msk[:, 0], msk[:, 1], ALU.add))
            v.sem_inc(S["m01_ready"], 1)
            v.wait_ge(S["pre_ps"], 1)
            ce.step(nc.vector.tensor_copy(pos, bank[0][:, 0:NT * NE].rearrange("p (t e) -> p t e", t=NT)))
            ce.step(nc.vector.tensor_copy(tex3, bank[1][:, 0:NT * NE].rearrange("p (t e) -> p e t", t=NT)))
            ce.wait()
            for e in range(NE):
                ce.step(nc.vector.tensor_tensor_scan(tsc3[:, e, :], onesf[:, 0:NT], tex3[:, e, :], 0.0, ALU.mult, ALU.add))
            ce.wait()
            ce.step(nc.vector.tensor_copy(cnt[:, 0, :], tsc3[:, :, NT - 1]))
            ce.link(tt(tex3, tsc3, tex3, ALU.subtract))
            ce.link(ts(cnt[:, 0, :], cnt[:, 0, :], float(TT - 1), None, ALU.add))
            ce.link(nc.vector.tensor_copy(cnti[:, :], cnt[:, 0, :]))
            ce.link(ts(cnti[:, :], cnti[:, :], TT.bit_length() - 1, None, ALU.arith_shift_right))
            ce.link(ts(cnti[:, :], cnti[:, :], 1, None, ALU.max))
            ce.link(nc.vector.tensor_copy(cnt[:, 1, :], cnti[:, :]))
            ce.link(nc.vector.tensor_tensor_scan(cnt[:, 2, :], onesf[:, 0:NE], cnt[:, 1, :], 0.0, ALU.mult, ALU.add))
            ce.link(tt(cnt[:, 3, :], cnt[:, 2, :], cnt[:, 1, :], ALU.subtract))
            ce.step(nc.vector.tensor_copy(ebnd[:, 0, :], cnt[:, 3, :]))
            ce.step(nc.vector.tensor_copy(ebnd[:, 1, :], cnt[:, 2, :]))
            ce.link(ts(cnt[:, 0, :], cnt[:, 3, :], float(TT), None, ALU.mult))
            v.sem_inc(S["bounds_ready"], 1)
            ce.link(tt(pos, pos, tex3.rearrange("p e t -> p t e"), ALU.add))
            ce.link(tt(pos, pos, cnt[:, 0, :].unsqueeze(1).to_broadcast([P, NT, NE]), ALU.add))
            for j in range(2):
                ce.step(tt(cmp8[:, :, j, :], msk[:, j], pos, ALU.mult))
            ce.link(ts(small[:, 0, :], valid[:, :], 1.0, -1e6, ALU.subtract, ALU.mult))
            for j in range(2):
                ce.step(inner_sum(slotf[:, j, :], cmp8[:, :, j, :]))
            ce.wait()
            for j in range(2):
                ce.step(tt(slotf[:, j, :], slotf[:, j, :], small[:, 0, :], ALU.add))
            ce.wait()
            ce.link(nc.vector.tensor_copy(sloti[:, :, :], slotf[:, :, :]))
            v.wait_ge(S["gexp_ready"], 1)
            ce.link(ts(small[:, 1, :], small[:, 3, :], 1.0, None, ALU.add))
            ce.link(nc.vector.reciprocal(wts[:, 0, :], small[:, 1, :]))
            ce.link(tt(wts[:, 1, :], wts[:, 0, :], small[:, 3, :], ALU.mult))
            v.sem_inc(S["slot_ready"], 1)
            for s in range(2):
                v.sem_inc(S["ew_used"][s], 1)

            v.sem_inc(S["y_ready"], 1)

            def tokens_in(i, par):
                v.wait_ge(S["xte_ps"], i + 1)
                nc.vector.tensor_copy(xTe[:, bass.ds(par, 1), :, :].rearrange("p o k n -> p (o k) n"),
                                      bank[6][:, :].rearrange("p (k n) -> p k n", k=KD)).then_inc(S["xte_ready"], 1)

            tokens_in(0, 0)
            with v.Fori(0, NE // 2) as ep:
                for s in range(2):
                    lo = v.value_load(ebnd[0:1, 0, bass.ds(ep * 2 + s, 1)], min_val=0, max_val=XT - 2)
                    hi = v.value_load(ebnd[0:1, 1, bass.ds(ep * 2 + s, 1)], min_val=1, max_val=XT - 1)
                    v.wait_ge(S["ew_in"][s], ep * 64 + 64)
                    apart(v)
                    with v.Fori(lo, hi) as i:
                        tokens_in(i + 1, (i + 1) % 2)
                        v.wait_ge(S["ys_free"], i + 1)
                        v.wait_ge(S["y_ps"], i + 1)
                        for a in range(2):
                            ins = tt(ysb[:, a, :], bank[4 + a][:, 0:D], b2s[:, s, :], ALU.add)
                        ins.then_inc(S["y_ready"], 1)
                    v.wait_ge(S["y_ready"], hi + 1)
                    v.sem_inc(S["ew_used"][s], 1)

            cf = Chain(v, S["dve_out"])
            cf.link(nc.vector.memset(yg, 0.0))
            v.sem_inc(S["ob_ready"], 1)

            def combine(i, first=False):
                for b in range(2):
                    cf.at(i * 2 + (b + 1))
                    v.wait_ge(S["yg_in"][b], i * 32 + 32)
                    if not first:
                        v.wait_ge(S["ob_stored"][b], i * 16)
                    wt = lambda j: wts[:, j, bass.ds(i * 2 + b, 1)]
                    cf.link(nc.vector.scalar_tensor_tensor(ob[:, b, :], yg[:, b, 0, :], wt(0), x_rows(i)(b), ALU.mult, ALU.add))
                    nc.vector.scalar_tensor_tensor(ob[:, b, :], yg[:, b, 1, :], wt(1), ob[:, b, :], ALU.mult, ALU.add
                                                   ).then_inc(S["ob_ready"], 1)

            combine(0, True)
            with v.Fori(1, NPAIR) as i:
                combine(i)

        @block.tensor
        def _(pe):
            mm = nc.tensor.matmul

            pe.wait_ge(S["consts"], 1)
            mm(bank[0][:, 0:NT], onesb[:, :], zeros[:, :].bitcast(BF16)[:, 0:NT], start=True, stop=False)
            pe.sem_inc(S["hist_used"], 2)
            with pe.Fori(0, NHIST) as i:
                for a in range(2):
                    pe.wait_ge(S["hist_oh"], i * 2 + (a + 1))
                    for j in range(HC):
                        last = mm(bank[0][:, 0:NT], oh_b[:, a, j, :], oh_a[:, a, j, :], start=False, stop=False)
                    last.then_inc(S["hist_used"], 1)
            mm(bank[0][:, 0:NT], onesb[:, :], zeros[:, :].bitcast(BF16)[:, 0:NT], start=False, stop=True).then_inc(S["hist_used"], 1)
            pe.wait_ge(S["deg_ready"], 1)
            mm(bank[1][:, 0:NT], ltf[:, :], deg[:, :], start=True, stop=True)
            mm(bank[1][:, 64:64 + NT], onesf[:, :], deg[:, :], start=True, stop=True).then_inc(S["rowp_ps"], 1)
            pe.wait_ge(S["ohd_ready"], 1)
            for n, lo in enumerate(range(0, NT, BT)):
                k = min(BT, NT - lo)
                if n >= 2:
                    pe.wait_ge(S["cnt_used"], n - 1)
                bk = 2 + 2 * (n % 2)
                oh = oh_d[:, lo:lo + k, :].rearrange("p t c -> p (t c)")
                mm(bank[bk][:, 0:k * NBUCK], ltb[:, :], oh, start=True, stop=True)
                mm(bank[bk + 1][:, 0:k * NBUCK], onesb[:, :], oh, start=True, stop=True).then_inc(S["cnt_ps"], 1)

            pe.wait_ge(S["cnt_used"], (NT + BT - 1) // BT)
            mm(bank[4][:, 0:D], ident[:, :], zeros[:, :], start=True, stop=False)
            pe.sem_inc(S["kv_done"], 1)

            def kv_outer(i, rows=(P, P)):
                for b in range(2):
                    if rows[b]:
                        pe.wait_ge(S["khat_ready"], i * 2 + (b + 1))
                        for j in range(2):
                            last = mm(bank[4][:, j * P:(j + 1) * P], kvs[0:rows[b], b, j * P:(j + 1) * P],
                                      kvs[0:rows[b], b, D + j * P:D + (j + 1) * P], start=False, stop=False)
                last.then_inc(S["kv_done"], 1)

            def first_phase(i, first=False):
                pe.wait_ge(S["xn_ready"], i + 1)
                if not first:
                    pe.wait_ge(S["xT_ready"], i * 2)
                for k in range(KD):
                    for b in range(2):
                        last = nc.tensor.transpose(bank[5][:, k * 2 * P + b * P:k * 2 * P + (b + 1) * P],
                                                   xn[:, b, k * P:(k + 1) * P], ident[:, :])
                last.then_inc(S["tp_ready"], 1)
                pe.wait_ge(S["xT_ready"], i * 2 + 1)
                if not first:
                    pe.wait_ge(S["wh_ready"], i)
                for b in range(2):
                    for k in range(KD):
                        last = mm(bank[b][:, 0:WCOL], xTs[:, k, b * P:(b + 1) * P], wcat[:, k, :], start=(k == 0), stop=(k == KD - 1))
                last.then_inc(S["wh_ps"], 1)
                if not first:
                    pe.wait_ge(S["kn_ready"], i * 2)
                for b in range(2):
                    for k in range(KD):
                        last = mm(bank[2 + b][:, :], xTs[:, k, b * P:(b + 1) * P], wkv[:, k, :], start=(k == 0), stop=(k == KD - 1))
                    last.then_inc(S["kv_ps"], 1)

            first_phase(0, True)
            with pe.Fori(1, NPAIR) as i:
                first_phase(i)
                kv_outer(i - 1)
            kv_outer(NPAIR - 1, (TAIL, 0))
            mm(bank[4][:, 0:D], ident[:, :], zeros[:, :], start=False, stop=True).then_inc(S["kv_done"], 1)

            pe.wait_ge(S["mw_in"], 32)
            pe.wait_ge(S["kvd_ready"], 1)
            for j in range(2):
                last = mm(bank[6][:, j * D:(j + 1) * D], kvd[:, j, :], wq_s[:, j, :], start=True, stop=True)
            last.then_inc(S["t1_ps"], 1)
            pe.wait_ge(S["t1_ready"], 1)
            for k in range(KD):
                for j in range(2):
                    last = mm(bank[7][:, k * D:(k + 1) * D], t1[:, j, k * P:(k + 1) * P], wo_s[:, j, :], start=(j == 0), stop=(j == 1))
            last.then_inc(S["mix_ps"], 1)
            pe.wait_ge(S["mix_ready"], 1)
            pe.sem_inc(S["base_ps"], 1)

            def mixed(i, first=False):
                pe.wait_ge(S["mxs_ready"], i + 1)
                if not first:
                    pe.wait_ge(S["base_ready"], i)
                for b in range(2):
                    for k in range(KD):
                        last = mm(bank[b][:, 0:D], mxs[:, k, b * P:(b + 1) * P], mixw[:, k, :], start=(k == 0), stop=(k == KD - 1))
                last.then_inc(S["base_ps"], 1)

            mixed(0, True)
            with pe.Fori(1, NPAIR) as i:
                mixed(i)

            pe.wait_ge(S["winr_ready"], 1)
            nw = pe.value_load(nwin[0:1, 0:1], min_val=1, max_val=EP // WIN)
            with pe.Fori(0, nw) as w:
                pe.wait_ge(S["winr_ready"], w + 1)
                apart(pe)
                lo = pe.value_load(ctl[0:1, 0:1], min_val=0, max_val=unit_bound)
                npr = pe.value_load(ctl[0:1, 3:4], min_val=1, max_val=NPAIR)
                with pe.Fori(0, npr) as i:
                    u = i + lo
                    for b in range(2):
                        ng = pe.value_load(groups[0:1, bass.ds(i * 2 + b, 1)], min_val=1, max_val=NG)
                        nprod = pe.value_load(gbase[0:1, b, bass.ds(i, 1)], min_val=0, max_val=NT * EP)
                        pe.wait_ge(S["accf_ready"], u * 2 + (b + 1))
                        mm(bank[b][:, 0:D], ident[:, :], accf[:, :], start=True, stop=False)
                        for q in range(NG):
                            with pe.If(ng > q):
                                pe.wait_ge(S["prod"][b], nprod + (q + 1))
                                for k in range(q * SG, (q + 1) * SG):
                                    mm(bank[b][:, 0:D], ident[:, :], gath[:, b, k, 0:D], start=False, stop=False)
                        mm(bank[b][:, 0:D], ident[:, :], zeros[:, :], start=False, stop=True).then_inc(S["acc_ps"], 1)
                pe.wait_ge(S["pass_done"], w + 1)

            with pe.Fori(0, NPAIR) as i:
                pe.wait_ge(S["xn2_ready"], i + 1)
                for k in range(KD):
                    for b in range(2):
                        last = nc.tensor.transpose(bank[5][:, k * 2 * P + b * P:k * 2 * P + (b + 1) * P],
                                                   xn2s[:, b, k * P:(k + 1) * P], ident[:, :])
                last.then_inc(S["tp2_ready"], 1)
                pe.wait_ge(S["xTr_ready"], i + 1)
                for b in range(2):
                    for k in range(KD):
                        last = mm(bank[6][:, b * NE:(b + 1) * NE], xTr[:, k, b * P:(b + 1) * P], wg_s[:, k, :], start=(k == 0), stop=(k == KD - 1))
                last.then_inc(S["lg_ps"], 1)
            pe.wait_ge(S["m01_ready"], 1)
            mm(bank[0][:, 0:NT * NE], ltb[:, :], m01, start=True, stop=True)
            mm(bank[1][:, 0:NT * NE], onesb[:, :], m01, start=True, stop=True).then_inc(S["pre_ps"], 1)

            def tokens_in(i, first=False):
                pe.wait_ge(S["xs_in"], i * 16 + 16)
                if not first:
                    pe.wait_ge(S["xte_ready"], i)
                for k in range(KD):
                    for a in range(2):
                        last = nc.tensor.transpose(bank[6][:, k * TT + a * P:k * TT + (a + 1) * P],
                                                   xs_s[:, a, k * P:(k + 1) * P], ident[:, :])
                last.then_inc(S["xte_ps"], 1)

            pe.wait_ge(S["bounds_ready"], 1)
            tokens_in(0, True)
            with pe.Fori(0, NE // 2) as ep:
                for s in range(2):
                    lo = pe.value_load(ebnd[0:1, 0, bass.ds(ep * 2 + s, 1)], min_val=0, max_val=XT - 2)
                    hi = pe.value_load(ebnd[0:1, 1, bass.ds(ep * 2 + s, 1)], min_val=1, max_val=XT - 1)
                    pe.wait_ge(S["ew_in"][s], ep * 64 + 64)
                    apart(pe)

                    def up(i, c):
                        pe.wait_ge(S["h_ready"], i * FC + (c + 1))
                        for k in range(KD):
                            last = mm(bank[c % 4][:, 0:TT], w1s[:, s, k, c * P:(c + 1) * P],
                                      xTe[:, bass.ds(i % 2, 1), k, :].rearrange("p o n -> p (o n)"), start=(k == 0), stop=(k == KD - 1))
                        last.then_inc(S["h_ps"], 1)

                    def down(i, c):
                        pe.wait_ge(S["h_ready"], i * FC + (c + 5))
                        for a in range(2):
                            last = mm(bank[4 + a][:, 0:D], hT[:, c, a * P:(a + 1) * P], w2s[:, s, c, :], start=(c == 0), stop=(c == FC - 1))
                        if c == FC - 1:
                            last.then_inc(S["y_ps"], 1)

                    with pe.Fori(lo, hi) as i:
                        pe.wait_ge(S["xte_ready"], i + 1)
                        for c in range(FC):
                            up(i, c)
                            if c == 2:
                                pe.wait_ge(S["y_ready"], i + 1)
                            if c >= 2:
                                down(i, c - 2)
                            if c == FC // 2:
                                tokens_in(i + 1)
                        down(i, FC - 2)
                        down(i, FC - 1)


def kernel(x, src, dst, L0_gnn_W, L0_gnn_bW, L0_gnn_a_src, L0_gnn_a_dst, L0_gnn_a_bias, L0_mix_wq, L0_mix_wk, L0_mix_wv,
           L0_mix_wo, L0_mix_bo, L0_mix_ln_k_g, L0_mix_ln_k_b, L0_mix_ln_v_g, L0_mix_ln_v_b, L0_ffn_Wg, L0_ffn_bg,
           L0_ffn_W1, L0_ffn_b1, L0_ffn_W2, L0_ffn_b2):
    import numpy as np
    import concourse.bacc as bacc
    from concourse.bass_utils import run_bass_kernel_spmd as run

    a = lambda v: np.ascontiguousarray(np.asarray(v))
    src_, dst_ = a(src), a(dst)
    arrays = {
        "x": np.pad(a(x), ((0, NP - N), (0, 0))),
        "src": np.pad(src_, (0, EP - E_REAL)),
        "dst": np.pad(dst_, (0, EP - E_REAL), constant_values=NP),
        "dst_next": np.pad(dst_[1:], (0, EP - E_REAL + 1), constant_values=NP),
        "gW": a(np.asarray(L0_gnn_W).transpose(1, 0, 2).reshape(D, D)),
        "gbW": a(L0_gnn_bW).reshape(-1),
        "gas": a(L0_gnn_a_src).reshape(-1),
        "gad": a(L0_gnn_a_dst).reshape(-1),
        "gab": a(L0_gnn_a_bias),
        "wkvT": a(np.concatenate([np.asarray(L0_mix_wk).T, np.asarray(L0_mix_wv).T], axis=1)),
        "wq": a(L0_mix_wq),
        "woT": a(np.asarray(L0_mix_wo).T),
        "bo": a(L0_mix_bo),
        "lng": a(np.concatenate([np.asarray(L0_mix_ln_k_g), np.asarray(L0_mix_ln_v_g)])),
        "lnb": a(np.concatenate([np.asarray(L0_mix_ln_k_b), np.asarray(L0_mix_ln_v_b)])),
        "Wg": a(L0_ffn_Wg),
        "bg": a(L0_ffn_bg),
        "W1": a(L0_ffn_W1).reshape(NE * D, HID),
        "b1": a(np.asarray(L0_ffn_b1).reshape(NE, FC, P).transpose(0, 2, 1)).reshape(NE * P, FC),
        "W2": a(L0_ffn_W2).reshape(NE * HID, D),
        "b2": a(L0_ffn_b2),
    }
    nc = bacc.Bacc("TRN2", target_bir_lowering=False, num_devices=1)
    args = [nc.dram_tensor(f"in_{n}", v.shape, mybir.dt.from_np(v.dtype), kind="ExternalInput").ap() for n, v in arrays.items()]
    out = nc.dram_tensor("out", (N, D), F32, kind="ExternalOutput").ap()
    gps_layer(nc, *args, out)
    r = run(nc, [{f"in_{n}": v for n, v in arrays.items()}], core_ids=[0])
    return r.results[0]["out"]
```

```python
from contextlib import ExitStack

import concourse.bass as bass
from concourse import mybir

F32 = mybir.dt.float32
BF16 = mybir.dt.bfloat16
I32 = mybir.dt.int32
ALU = mybir.AluOpType
ACT = mybir.ActivationFunctionType
AX = mybir.AxisListType
MAXOP = bass.bass_isa.ReduceOp.max

P = 128
N = 6250
D = 256
KD = D // P
NT = 50
NP = NT * P
NPAIR = NT // 2
H, DH = 8, 32
ROW = D + H
WCOL = D + 2 * H
MH, MD = 4, 64
E_REAL = 2 * 50000 + N
EC = 832
EP = EC * P
HC = 32
NHIST = EC // (2 * HC)
WIN = 24
SG = 2
NG = WIN // SG
WSTEP, WLEN = 16, 40
NWROW = (EP - WLEN) // WSTEP + 1
WT = 10
NBUCK = 64
BT = 512 // NBUCK
NE, HID = 8, 1024
XROW = D + NE + 1
NOWHERE = 1 << 20
SPLIT = 9
FC = HID // P
TT = 256
XT = 58
TAIL = N - (N // P) * P
TAIL_T = N // P
EPS = 1e-5
ALPHA = 0.2
LOW, LOWER = -1e29, -1e30
assert NPAIR * 2 == NT and E_REAL <= EP and EC == NHIST * 2 * HC and TAIL_T == NT - 2


class Chain:

    def __init__(self, eng, sem):
        self.eng, self.sem, self.base, self.n = eng, sem, 0, 0

    def step(self, ins):
        self.n += 1
        ins.then_inc(self.sem, 1)

    def wait(self, upto=None):
        self.eng.wait_ge(self.sem, self.base + (self.n if upto is None else upto))

    def link(self, ins):
        self.step(ins)
        self.wait()

    def at(self, base):
        self.base, self.n = base, 0


def gps_layer(nc, x, src, dst, dst_next, gW, gbW, gas, gad, gab, wkvT, wq, woT, bo, lng, lnb,
              Wg, bg, W1, b1, W2, b2, out):
    ctx = ExitStack()

    def sb(name, shape, dt=F32):
        return ctx.enter_context(nc.sbuf_tensor(name, shape, dt))

    def sem(name):
        return ctx.enter_context(nc.semaphore(name))

    def dram(name, shape, dt=F32):
        return nc.dram_tensor(name, shape, dt, kind="Internal").ap()

    with ctx:
        win_tab = dram("win_tab", (NWROW, WLEN), I32)
        wh_tab = dram("wh_tab", (NP, ROW))
        s2_tab = dram("s2_tab", (NP, H))
        base_tab = dram("base_tab", (NP, D))
        ord_tab = dram("ord_tab", (NP, 4), I32)
        xs_tab = dram("xs_tab", (XT * TT, XROW))

        x_all = sb("x_all", [P, NT, D])
        xT_flat = sb("xT_flat", [P, NT * XROW])
        xT_all = xT_flat[:, 0:KD * NP].rearrange("p (k n) -> p k n", k=KD)
        xrow_all = xT_flat[:, :].rearrange("p (t c) -> p t c", t=NT)
        gath = sb("gath", [P, 2, WIN, ROW])
        g = gath[:, :, :, :].rearrange("p a k r -> p (a k r)")
        shared = sb("shared", [P, 2900])
        ident = sb("ident", [P, P])
        ltf = sb("ltf", [P, P])
        ltb = sb("ltb", [P, P], BF16)
        onesf = sb("onesf", [P, P])
        onesb = sb("onesb", [P, P], BF16)
        zeros = sb("zeros", [P, D])
        blank = sb("blank", [P, XROW])
        iota_f = sb("iota_f", [P, P])
        iota_i = sb("iota_i", [P, P], I32)
        node_i = sb("node_i", [P, NT], I32)
        abias = sb("abias", [P, H])
        bo_b = sb("bo_b", [P, D])
        mixw = sb("mixw", [P, KD, D])
        wg_s = sb("wg_s", [P, KD, NE])
        bg_b = sb("bg_b", [P, NE])
        ordn = sb("ordn", [P, NT, 4], I32)
        deg = sb("deg", [P, NT])
        rowp = sb("rowp", [P, NT])
        small = sb("small", [P, 4, NT])
        ranki = sb("ranki", [P, NT], I32)
        mxrem = sb("mxrem", [P, NT])
        winr = sb("winr", [P, NT], I32)
        starti = sb("starti", [P, NT], I32)
        bits = sb("bits", [P, 4, NT], I32)
        groups = sb("groups", [P, NT], I32)
        ctl = sb("ctl", [P, 5], I32)
        ctlf = sb("ctlf", [P, 7])
        gmask = sb("gmask", [P, NT])
        gcumf = sb("gcumf", [P, 2, NPAIR])
        gbase = sb("gbase", [P, 2, NPAIR], I32)
        gcum = sb("gcum", [P, 2, NPAIR], I32)
        nextra = sb("nextra", [P, 1], I32)
        vare = sb("vare", [P, 2])
        idx = sb("idx", [P, NT + 2, WIN], I32)
        idx_x = sb("idx_x", [P, NT + 2, WIN], I32)
        idxs = sb("idxs", [P, 2, WIN], I32)
        basei = sb("basei", [P, 2], I32)
        s2st = sb("s2st", [P, 2, H])
        rankst = sb("rankst", [P, 2], I32)
        meta = sb("meta", [P, 2, NE + 1])
        metao = sb("metao", [P, 2, NE + 1])
        m_all = sb("m_all", [P, NT, H])
        den_all = sb("den_all", [P, NT, H])
        s2_all = sb("s2_all", [P, NT, H])
        stats = sb("stats", [P, 2, 6])
        mv = sb("mv", [P, 2, 2])
        rs = sb("rs", [P, 2, 2])
        kvr = sb("kvr", [P, 2, 2, 8])
        ez = sb("ez", [P, WIN, H])
        pen = sb("pen", [P, WIN])
        es = sb("es", [P, 6, H])
        accf = sb("accf", [P, D])
        wts = sb("wts", [P, 2, NT])
        slotf = sb("slotf", [P, 2, NT])
        sloti = sb("sloti", [P, 2, NT], I32)
        valid = sb("valid", [P, NT])
        cnt = sb("cnt", [P, 4, NE])
        cnti = sb("cnti", [P, NE], I32)
        ebnd = sb("ebnd", [P, 2, NE], I32)

        def carve(area, spans):
            at, parts = spans["start"], []
            for n in spans["sizes"]:
                parts.append(area[:, at:at + n])
                at += n
            assert at <= area.shape[1], at
            return parts

        gb = g.bitcast(BF16)
        oh_b = gb[:, 0:2 * HC * P].rearrange("p (a j c) -> p a j c", a=2, j=HC)
        oh_a = gb[:, 2 * HC * P:2 * HC * (P + NT)].rearrange("p (a j c) -> p a j c", a=2, j=HC)
        oh_d = gb[:, 0:NT * NBUCK].rearrange("p (t c) -> p t c", t=NT)
        r_in, = carve(g, dict(start=1600, sizes=[NT * NBUCK]))
        r_cnt, r_scan = carve(xT_flat, dict(start=0, sizes=[NT * NBUCK] * 2))
        wina, winb = [a.bitcast(I32).rearrange("p (t w) -> p t w", t=NT)
                      for a in carve(g, dict(start=0, sizes=[NT * WLEN] * 2))]
        xn, xTs, whs, kvs, kvq = carve(g, dict(start=4000, sizes=[2 * D, 2 * D, 2 * WCOL, 4 * D, 4 * D]))
        xn = xn.rearrange("p (b d) -> p b d", b=2)
        xTs = xTs.rearrange("p (k n) -> p k n", k=KD)
        whs = whs.rearrange("p (b c) -> p b c", b=2)
        kvs = kvs.rearrange("p (b c) -> p b c", b=2)
        kvq = kvq.rearrange("p (b c) -> p b c", b=2)
        wkv_, avec_, lngb_, wcat_, bias1 = carve(g, dict(start=7616, sizes=[KD * 2 * D, 3 * D, 4 * MD, KD * WCOL, WCOL]))
        wkv = wkv_.rearrange("p (k c) -> p k c", k=KD)
        avec = avec_.rearrange("p (a c) -> p a c", a=3)
        lngb = lngb_.rearrange("p (a s d) -> p a s d", a=2, s=2)
        wcat = wcat_.rearrange("p (k c) -> p k c", k=KD)
        bcol, acol = [a.bitcast(I32) for a in carve(g, dict(start=10480, sizes=[EC, EC]))]
        wq_s, wo_s, kvd, t1, base_s, mxs = carve(shared, dict(start=0, sizes=[2 * D, 2 * D, 2 * P, 2 * D, 2 * D, 2 * D]))
        mxs = mxs.rearrange("p (k n) -> p k n", k=KD)
        wq_s = wq_s.rearrange("p (k c) -> p k c", k=2)
        wo_s = wo_s.rearrange("p (k c) -> p k c", k=2)
        kvd = kvd.rearrange("p (k c) -> p k c", k=2)
        t1 = t1.rearrange("p (k c) -> p k c", k=2)
        base_s = base_s.rearrange("p (b c) -> p b c", b=2)
        msk, pos, m01_ = carve(shared, dict(start=0, sizes=[2 * NT * NE, NT * NE, NT * NE // 2]))
        logit = sb("logit", [P, NT, NE])[:, :, :]
        baseg = sb("baseg", [P, 2, D])[:, :, :]
        xn2s = sb("xn2s", [P, 2, D])[:, :, :]
        xTr = sb("xTr", [P, KD, 2 * P])[:, :, :]
        msk = msk.rearrange("p (j t e) -> p j t e", j=2, t=NT)
        pos = pos.rearrange("p (t e) -> p t e", t=NT)
        m01 = m01_.bitcast(BF16)
        cmp8, cmp8b, tri8, tsc, tex = carve(g, dict(start=0, sizes=[NT * 64, NT * 64, 64, NT * NE, NT * NE]))
        cmp8 = cmp8.rearrange("p (t a b) -> p t a b", t=NT, a=NE)
        cmp8b = cmp8b.rearrange("p (t a b) -> p t a b", t=NT, a=NE)
        tri8 = tri8.rearrange("p (a b) -> p a b", a=NE)
        tsc3 = tsc.rearrange("p (e t) -> p e t", e=NE)
        tex3 = tex.rearrange("p (e t) -> p e t", e=NE)
        w1s, w2s, b1s, b2s, xs_s, xTe, hT = carve(
            g, dict(start=0, sizes=[2 * KD * HID, 2 * FC * D, 2 * FC, 2 * D, 2 * XROW, 2 * KD * TT, FC * TT]))
        w1s = w1s.rearrange("p (s k f) -> p s k f", s=2, k=KD)
        w2s = w2s.rearrange("p (s c n) -> p s c n", s=2, c=FC)
        b1s = b1s.rearrange("p (s c) -> p s c", s=2)
        b2s = b2s.rearrange("p (s n) -> p s n", s=2)
        xs_s = xs_s.rearrange("p (a d) -> p a d", a=2)
        xTe = xTe.rearrange("p (b k n) -> p b k n", b=2, k=KD)
        hT = hT.rearrange("p (c n) -> p c n", c=FC)
        ysb = shared[:, 0:2 * D].rearrange("p (a d) -> p a d", a=2)

        bank = [ctx.enter_context(nc.psum_tensor(f"bank{i}", [P, 512], F32)) for i in range(8)]

        S = {}
        for name in """consts pool_step pool_khat dve_step dve_end passed act_step weights_in edges_in
            hist_oh hist_used deg_ready rowp_ps ohd_ready cnt_ps cnt_used rank_ready ord_stored ord_in win_done
            mx_ready mx_done whs_free bases_free var_ready rstd_ready xn_ready tp_ready xT_ready wh_ps wh_ready
            s2_ready s2_sent s2_free s2_in kv_ps sq_ready kvar_ready krs_ready kn_ready khat_ready kv_done kvd_ready t1_ps t1_ready
            mix_ps mix_ready mw_in mxs_ready base_ps base_ready tables_ready lwin_ready lwin_in idx_step
            x_ready x_win_in x_idx_ready x_pass x_done l_ready basei_ready g_blank slots_filled
            y_step lg_done v2_ready r2_ready xn2_ready xn2_copied tp2_ready xTr_ready lg_ps x1_sent
            m01_ready pre_ps gap_ready gexp_ready slot_ready bounds_ready xs_blank xs_done xs_in xte_ps xte_ready
            h_ps h_ready y_ps y_ready ys_done ys_free""".split():
            S[name] = sem(name)
        for pass_ in ("x", "l"):
            for name in "f_in ex_in f_ready ex_ready accf_ready acc_ps unit".split():
                S[pass_, name] = sem(f"{pass_}_{name}")
            for name in "idxs_ready gath_in prod".split():
                S[pass_, name] = [sem(f"{pass_}_{name}_a"), sem(f"{pass_}_{name}_b")]
        for name in """wh_stored base_stored baseg_in ew_in ew_used""".split():
            S[name] = [sem(name + "_a"), sem(name + "_b")]

        def apart(eng):
            eng.sem_inc(S["passed"], 1)

        block = ctx.enter_context(nc.Block())
        NLOAD = 15
        unit_bound = NPAIR * (EP // WIN)

        @block.sync
        def _(sp):
            sp.dma_start(bcol, dst.rearrange("(p j) -> p j", j=EC)).then_inc(S["edges_in"], 16)
            w = lambda o, i: sp.dma_start(o, i).then_inc(S["weights_in"], 16)
            w(wcat[:, :, 0:D], gW.rearrange("(k p) c -> p k c", p=P))
            w(avec[:, 0, :], gas.partition_broadcast(P))
            w(avec[:, 1, :], gad.partition_broadcast(P))
            w(avec[:, 2, :], gbW.partition_broadcast(P))
            w(abias[:, :], gab.partition_broadcast(P))
            w(wkv, wkvT.rearrange("(k p) c -> p k c", p=P))
            w(bo_b[:, :], bo.partition_broadcast(P))
            w(lngb_[:, 0:2 * MD], lng.partition_broadcast(P))
            w(lngb_[:, 2 * MD:4 * MD], lnb.partition_broadcast(P))
            w(wg_s[:, :, :], Wg.rearrange("(k p) c -> p k c", p=P))
            w(bg_b[:, :], bg.partition_broadcast(P))
            for i in range(4):
                lo, hi = NT * i // 4, NT * (i + 1) // 4
                w(x_all[:, lo:hi, :], x[lo * P:hi * P, :].rearrange("(t p) d -> p t d", p=P))
            sp.dma_start(win_tab, bass.AP(src.tensor, 0, [[WSTEP, NWROW], [1, WLEN]])).then_inc(S["win_done"], 16)
            sp.dma_start(wq_s, wq.rearrange("(k p) c -> p k c", p=P)).then_inc(S["mw_in"], 16)
            sp.dma_start(wo_s, woT.rearrange("(k p) c -> p k c", p=P)).then_inc(S["mw_in"], 16)
            sp.wait_ge(S["consts"], 1)
            for i in range(XT // 2):
                sp.dma_start(xs_tab[i * 2 * TT:(i + 1) * 2 * TT, :].rearrange("(a p) c -> p a c", p=P),
                             blank[:, :].unsqueeze(1).to_broadcast([P, 2 * TT // P, XROW])).then_inc(S["xs_blank"], 16)
            sp.wait_ge(S["ord_stored"], 16 * NT)
            sp.dma_start(ordn[:, :, :], ord_tab.rearrange("(t p) c -> p t c", p=P)).then_inc(S["ord_in"], 16)
            sp.sem_inc(S["whs_free"], 1)
            with sp.Fori(0, NPAIR) as i:
                sp.wait_ge(S["wh_ready"], i + 1)
                for b in range(2):
                    sp.dma_start(wh_tab[bass.ds(i * (2 * P) + b * P, P), :], whs[:, b, 0:ROW]).then_inc(S["wh_stored"][b], 16)
                for b in range(2):
                    sp.wait_ge(S["wh_stored"][b], i * 16 + 16)
                sp.sem_inc(S["whs_free"], 1)
            sp.wait_ge(S["s2_sent"], 16 * NT)
            sp.dma_start(s2_all[:, :, :], s2_tab.rearrange("(t p) h -> p t h", p=P)).then_inc(S["s2_in"], 16)
            sp.sem_inc(S["bases_free"], 1)
            with sp.Fori(0, NPAIR) as i:
                sp.wait_ge(S["base_ready"], i + 1)
                for b in range(2):
                    sp.dma_start(base_tab[bass.ds(i * (2 * P) + b * P, P), :], base_s[:, b, :]).then_inc(S["base_stored"][b], 16)
                for b in range(2):
                    sp.wait_ge(S["base_stored"][b], i * 16 + 16)
                sp.sem_inc(S["bases_free"], 1)
            sp.wait_ge(S["bounds_ready"], 1)
            sp.wait_ge(S["slots_filled"], 1)
            ntile = sp.value_load(ebnd[0:1, 1, NE - 1:NE], min_val=1, max_val=XT - 1)
            sp.dma_start(xs_s, xs_tab[0:TT, :].rearrange("(a p) c -> p a c", p=P)).then_inc(S["xs_in"], 16)
            with sp.Fori(0, ntile) as i:
                sp.wait_ge(S["xte_ready"], i + 1)
                sp.dma_start(xs_s, xs_tab[bass.ds(i * TT + TT, TT), :].rearrange("(a p) c -> p a c", p=P)).then_inc(S["xs_in"], 16)

        @block.gpsimd
        def _(pool):
            def gather(o, table, index):
                return pool.indirect_dma_start(out=o, out_offset=None, in_=table,
                                               in_offset=bass.IndirectOffsetOnAxis(ap=index, axis=0))

            def scatter(table, index, i, **more):
                return pool.indirect_dma_start(out=table, out_offset=bass.IndirectOffsetOnAxis(ap=index, axis=0),
                                               in_=i, in_offset=None, **more)

            pc = Chain(pool, S["pool_step"])
            pc.step(pool.memset(ident[:, :], 0.0))
            pc.step(pool.memset(ltf[:, :], 1.0))
            pc.step(pool.memset(onesf[:, :], 1.0))
            pc.step(pool.memset(onesb[:, :], 1.0))
            pc.step(pool.memset(zeros[:, :], 0.0))
            pc.step(pool.memset(blank[:, 0:XROW - 1], 0.0))
            pc.step(pool.memset(blank[:, XROW - 1:XROW].bitcast(I32), NOWHERE))
            pc.step(pool.iota(iota_i[:, :], pattern=[[1, P]], base=0, channel_multiplier=0))
            pc.link(pool.iota(node_i[:, :], pattern=[[P, NT]], base=0, channel_multiplier=1))
            pc.step(pool.affine_select(out=ident[:, :], in_=ident[:, :], compare_op=ALU.not_equal, fill=1.0,
                                       base=0, pattern=[[-1, P]], channel_multiplier=1))
            pc.step(pool.affine_select(out=ltf[:, :], in_=ltf[:, :], compare_op=ALU.is_gt, fill=0.0,
                                       base=0, pattern=[[1, P]], channel_multiplier=-1))
            pc.link(pool.tensor_copy(iota_f[:, :], iota_i[:, :]))
            pool.tensor_copy(ltb[:, :], ltf[:, :]).then_inc(S["consts"], 1)

            pool.wait_ge(S["rank_ready"], 1)
            for t in range(NT):
                scatter(ord_tab, ranki[:, t:t + 1], ordn[:, t, :]).then_inc(S["ord_stored"], 16)

            def first_phase(i):
                pool.wait_ge(S["s2_ready"], i + 1)
                apart(pool)
                for b in range(2):
                    scatter(s2_tab, rankst[:, b:b + 1], s2st[:, b, :]).then_inc(S["s2_sent"], 16)
                for b in range(2):
                    pool.wait_ge(S["kn_ready"], i * 2 + (b + 1))
                    v = kvs[:, b, :].rearrange("p (s h d) -> p s h d", s=2, h=MH)
                    for s in range(2):
                        gain = lngb[:, 0, s, :].unsqueeze(1).to_broadcast([P, MH, MD])
                        pool.tensor_tensor(v[:, s], v[:, s], gain, ALU.mult).then_inc(S["pool_khat"], 1)
                    pool.wait_ge(S["pool_khat"], i * 4 + 2 * (b + 1))
                    for s in range(2):
                        add = lngb[:, 1, s, :].unsqueeze(1).to_broadcast([P, MH, MD])
                        last = pool.tensor_tensor(v[:, s], v[:, s], add, ALU.add)
                    last.then_inc(S["khat_ready"], 1)
                pool.wait_ge(S["s2_sent"], i * 32 + 32)
                pool.sem_inc(S["s2_free"], 1)

            pool.sem_inc(S["s2_free"], 1)
            with pool.Fori(0, SPLIT) as i:
                first_phase(i)
            pool.wait_ge(S["mx_ready"], 1)
            pool.partition_all_reduce(mxrem[:, :], deg[:, :], P, MAXOP).then_inc(S["mx_done"], 1)
            pool.wait_ge(S["win_done"], 16)
            pool.wait_ge(S["lwin_ready"], 1)
            for t in range(NT):
                gather(wina[:, t, :], win_tab, winr[:, t:t + 1]).then_inc(S["lwin_in"], 16)
            with pool.Fori(SPLIT, NPAIR) as i:
                first_phase(i)

            for b in range(2):
                pool.wait_ge(S["wh_stored"][b], 16 * NPAIR)

            def rows(p, i, b):
                ng = pool.value_load(groups[0:1, bass.ds(i * 2 + b, 1)], min_val=1, max_val=NG)
                for q in range(NG):
                    with pool.If(ng > q):
                        for k in range(q * SG, (q + 1) * SG):
                            gather(gath[:, b, k, :], wh_tab, idxs[:, b, k:k + 1]).then_inc(S[p, "gath_in"][b], 16)

            pool.wait_ge(S["tables_ready"], 1)
            pool.wait_ge(S["kv_done"], NPAIR + 2)
            pool.wait_ge(S["khat_ready"], NT)
            pool.memset(g, 0.0).then_inc(S["g_blank"], 1)
            pool.wait_ge(S["g_blank"], 1)
            nx = pool.value_load(nextra[0:1, 0:1], min_val=0, max_val=EP // WIN)
            with pool.If(nx > 0):
                with pool.Fori(0, nx) as w:
                    pool.wait_ge(S["x_ready"], w + 1)
                    apart(pool)
                    lo = pool.value_load(ctl[0:1, 0:1], min_val=0, max_val=unit_bound)
                    npr = pool.value_load(ctl[0:1, 3:4], min_val=1, max_val=NPAIR)
                    ngr = pool.value_load(ctl[0:1, 2:3], min_val=1, max_val=NT // WT)
                    for gr in range(NT // WT):
                        with pool.If(ngr > gr):
                            for t in range(gr * WT, (gr + 1) * WT):
                                gather(wina[:, t, :], win_tab, winr[:, t:t + 1]).then_inc(S["x_win_in"], 16)
                    pool.wait_ge(S["x_idx_ready"], w + 1)
                    apart(pool)
                    with pool.Fori(0, npr) as i:
                        for b in range(2):
                            pool.wait_ge(S["x", "idxs_ready"][b], i + lo + 1)
                            rows("x", i, b)
                    pool.wait_ge(S["x_done"], w + 1)
                    apart(pool)
            pool.wait_ge(S["l_ready"], 1)
            for b in range(2):
                pool.wait_ge(S["base_stored"][b], 16 * NPAIR)
            with pool.Fori(0, NPAIR) as i:
                for b in range(2):
                    pool.wait_ge(S["l", "idxs_ready"][b], i + 1)
                    rows("l", i, b)
                pool.wait_ge(S["basei_ready"], i + 1)
                apart(pool)
                for b in range(2):
                    gather(baseg[:, b, :], base_tab, basei[:, b:b + 1]).then_inc(S["baseg_in"][b], 16)

            def x1_out(lo, hi):
                for t in range(lo, hi):
                    scatter(out, ordn[:, t, 0:1], x_all[:, t, :], bounds_check=N - 1, oob_is_err=False).then_inc(S["x1_sent"], 16)

            pool.wait_ge(S["lg_done"], 1)
            x1_out(0, NT // 3)
            pool.wait_ge(S["slot_ready"], 1)
            pool.wait_ge(S["xs_blank"], 16 * (XT // 2))
            for t in range(NT):
                for j in range(2):
                    scatter(xs_tab, sloti[:, j, t:t + 1], xrow_all[:, t, :],
                            bounds_check=XT * TT - 1, oob_is_err=False).then_inc(S["xs_done"], 16)
            pool.wait_ge(S["xs_done"], 16 * 2 * NT)
            ntile = pool.value_load(ebnd[0:1, 1, NE - 1:NE], min_val=1, max_val=XT - 1)
            pool.sem_inc(S["ys_free"], 1)
            pool.sem_inc(S["slots_filled"], 1)
            x1_out(NT // 3, NT)
            pool.wait_ge(S["x1_sent"], 16 * NT)
            with pool.Fori(0, ntile) as i:
                pool.wait_ge(S["y_ready"], i + 2)
                apart(pool)
                for a in range(2):
                    scatter(out, metao[:, a, NE:NE + 1].bitcast(I32), ysb[:, a, :], bounds_check=N - 1, oob_is_err=False,
                            compute_op=ALU.add).then_inc(S["ys_done"], 16)
                pool.wait_ge(S["ys_done"], i * 32 + 32)
                pool.sem_inc(S["ys_free"], 1)

        @block.scalar
        def _(act):
            def root(o, i, ready):
                nc.scalar.activation(o, i, ACT.Sqrt).then_inc(ready, 1)

            act.wait_ge(S["var_ready"], 1)
            root(rs[:, :, 1], rs[:, :, 0], S["rstd_ready"])

            def evacuate(i, first=False):
                act.wait_ge(S["tp_ready"], i + 1)
                if not first:
                    act.wait_ge(S["kv_ps"], i * 2)
                pair = bank[5][:, :].rearrange("p (k n) -> p k n", k=KD)
                nc.scalar.copy(xTs, pair).then_inc(S["xT_ready"], 1)
                nc.scalar.copy(xT_all[:, :, bass.ds(i * (2 * P), 2 * P)], pair).then_inc(S["xT_ready"], 1)

            def spreads(i, more=True):
                for b in range(2):
                    act.wait_ge(S["kv_ps"], i * 2 + (b + 1))
                    nc.scalar.activation(kvq[:, b, :], bank[2 + b][:, :], ACT.Square).then_inc(S["sq_ready"], 1)
                if more:
                    act.wait_ge(S["var_ready"], i + 2)
                    root(rs[:, :, 1], rs[:, :, 0], S["rstd_ready"])
                act.wait_ge(S["kvar_ready"], i + 1)
                root(kvr[:, 1, :, :], kvr[:, 0, :, :], S["krs_ready"])

            evacuate(0, True)
            spreads(0)
            with act.Fori(1, NPAIR - 1) as i:
                evacuate(i)
                spreads(i)
            evacuate(NPAIR - 1)
            spreads(NPAIR - 1, False)

            with act.Fori(0, NPAIR) as i:
                act.wait_ge(S["base_ps"], i + 1)
                nc.scalar.copy(mxs, xT_all[:, :, bass.ds(i * (2 * P), 2 * P)]).then_inc(S["mxs_ready"], 1)

            def exponentials(p, u, b):
                act.wait_ge(S[p, "f_in"], u * 2 + (b + 1))
                nc.scalar.activation(es[:, 3, :], es[:, 2, :], ACT.Exp).then_inc(S[p, "f_ready"], 1)
                act.wait_ge(S[p, "ex_in"], u * 2 + (b + 1))
                nc.scalar.activation(ez[:, :, :], ez[:, :, :], ACT.Exp).then_inc(S[p, "ex_ready"], 1)

            act.wait_ge(S["tables_ready"], 1)
            nx = act.value_load(nextra[0:1, 0:1], min_val=0, max_val=EP // WIN)
            with act.If(nx > 0):
                with act.Fori(0, nx) as w:
                    act.wait_ge(S["x_ready"], w + 1)
                    apart(act)
                    lo = act.value_load(ctl[0:1, 0:1], min_val=0, max_val=unit_bound)
                    npr = act.value_load(ctl[0:1, 3:4], min_val=1, max_val=NPAIR)
                    with act.Fori(0, npr) as i:
                        for b in range(2):
                            exponentials("x", i + lo, b)
                    act.wait_ge(S["x_done"], w + 1)
                    apart(act)
            act.wait_ge(S["l_ready"], 1)
            with act.Fori(0, NPAIR) as i:
                for b in range(2):
                    exponentials("l", i, b)
                act.wait_ge(S["v2_ready"], i + 1)
                root(rs[:, :, 1], rs[:, :, 0], S["r2_ready"])
                act.wait_ge(S["xn2_ready"], i + 1)
                nc.scalar.copy(xrow_all[:, bass.ds(i * 2, 2), 0:D], xn2s).then_inc(S["xn2_copied"], 1)
                act.wait_ge(S["tp2_ready"], i + 1)
                nc.scalar.copy(xTr, bank[5][:, :].rearrange("p (k n) -> p k n", k=KD)).then_inc(S["xTr_ready"], 1)
            act.wait_ge(S["gap_ready"], 1)
            nc.scalar.activation(small[:, 3, :], small[:, 2, :], ACT.Exp).then_inc(S["gexp_ready"], 1)

            def weights(e, s):
                ew = lambda o, i: act.dma_start(o, i).then_inc(S["ew_in"][s], 16)
                ew(w1s[:, s, :, :], W1[bass.ds(e * D, D), :].rearrange("(k p) f -> p k f", p=P))
                ew(w2s[:, s, :, :], W2[bass.ds(e * HID, HID), :].rearrange("(c p) n -> p c n", p=P))
                ew(b1s[:, s, :], b1[bass.ds(e * P, P), :])
                ew(b2s[:, s, :], b2[bass.ds(e, 1), :].to_broadcast([P, D]))

            act.sem_inc(S["h_ready"], 4)
            act.wait_ge(S["slot_ready"], 1)
            weights(0, 0)
            weights(1, 1)

            def expert(ep, s):
                lo = act.value_load(ebnd[0:1, 0, bass.ds(ep * 2 + s, 1)], min_val=0, max_val=XT - 2)
                hi = act.value_load(ebnd[0:1, 1, bass.ds(ep * 2 + s, 1)], min_val=1, max_val=XT - 1)
                act.wait_ge(S["ew_in"][s], ep * 64 + 64)
                with act.Fori(lo, hi) as i:
                    for c in range(FC):
                        act.wait_ge(S["h_ps"], i * FC + (c + 1))
                        nc.scalar.activation(hT[:, c, :], bank[c % 4][:, 0:TT], ACT.Gelu,
                                             bias=b1s[:, s, c:c + 1]).then_inc(S["h_ready"], 1)

            with act.Fori(0, NE // 2 - 1) as ep:
                for s in range(2):
                    expert(ep, s)
                    act.wait_ge(S["ew_used"][s], ep + 1)
                    weights(ep * 2 + (2 + s), s)
            for s in range(2):
                expert(NE // 2 - 1, s)

        @block.vector
        def _(v):
            ch = Chain(v, S["dve_step"])
            tt, ts, copy = nc.vector.tensor_tensor, nc.vector.tensor_scalar, nc.vector.tensor_copy
            scan, reduce = nc.vector.tensor_tensor_scan, nc.vector.tensor_reduce

            def inner_sum(o, i):
                return reduce(o, i, AX.X, ALU.add)

            v.wait_ge(S["edges_in"], 16)
            v.wait_ge(S["consts"], 1)
            ch.link(ts(acol, bcol, 7, None, ALU.arith_shift_right))
            ch.link(ts(bcol, bcol, P - 1, None, ALU.bitwise_and))
            with v.Fori(0, NHIST) as i:
                for a in range(2):
                    v.wait_ge(S["hist_used"], i * 2 + (a + 1))
                    cols = bass.ds(i * (2 * HC) + a * HC, HC)
                    tt(oh_b[:, a], bcol[:, cols].unsqueeze(2).to_broadcast([P, HC, P]),
                       iota_i[:, :].unsqueeze(1).to_broadcast([P, HC, P]), ALU.is_equal)
                    tt(oh_a[:, a], acol[:, cols].unsqueeze(2).to_broadcast([P, HC, NT]),
                       iota_i[:, 0:NT].unsqueeze(1).to_broadcast([P, HC, NT]), ALU.is_equal).then_inc(S["hist_oh"], 1)
            v.wait_ge(S["hist_used"], 2 * NHIST + 3)
            ch.link(copy(deg[:, :], bank[0][:, 0:NT]))
            v.sem_inc(S["deg_ready"], 1)

            v.wait_ge(S["rowp_ps"], 1)
            ch.link(scan(small[:, 0, :], onesf[:, 0:NT], bank[1][:, 64:64 + NT], 0.0, ALU.mult, ALU.add))
            ch.link(tt(small[:, 1, :], small[:, 0, :], bank[1][:, 64:64 + NT], ALU.subtract))
            ch.link(tt(rowp[:, :], small[:, 1, :], bank[1][:, 0:NT], ALU.add))

            ch.link(ts(small[:, 2, :], deg[:, :], float(NBUCK - 1), -1.0, ALU.min, ALU.mult))
            ch.link(ts(small[:, 3, :], small[:, 2, :], float(NBUCK - 1), None, ALU.add))
            ch.link(tt(oh_d, small[:, 3, :].unsqueeze(2).to_broadcast([P, NT, NBUCK]),
                       iota_f[:, 0:NBUCK].unsqueeze(1).to_broadcast([P, NT, NBUCK]), ALU.is_equal))
            v.sem_inc(S["ohd_ready"], 1)
            rin = r_in.rearrange("p (t c) -> p t c", t=NT)
            rc = r_cnt.rearrange("p (c t) -> p c t", t=NT)
            rsc = r_scan.rearrange("p (c t) -> p c t", t=NT)
            for n, lo in enumerate(range(0, NT, BT)):
                k = min(BT, NT - lo)
                v.wait_ge(S["cnt_ps"], n + 1)
                bk = 2 + 2 * (n % 2)
                ch.step(copy(rin[:, lo:lo + k, :], bank[bk][:, 0:k * NBUCK].rearrange("p (t c) -> p t c", t=k)))
                ch.step(copy(rc[:, :, lo:lo + k], bank[bk + 1][:, 0:k * NBUCK].rearrange("p (t c) -> p c t", t=k)))
                ch.wait()
                v.sem_inc(S["cnt_used"], 1)
            ch.link(scan(r_scan, onesf[:, 0:1].to_broadcast([P, NT * NBUCK]), r_cnt, 0.0, ALU.mult, ALU.add))
            ch.link(tt(r_scan, r_scan, r_cnt, ALU.subtract))
            ch.link(tt(rin, rin, rsc.rearrange("p c t -> p t c"), ALU.add))
            ch.link(tt(rin, rin, oh_d, ALU.mult))
            ch.link(inner_sum(small[:, 2, :], rin))
            ch.step(copy(ranki[:, :], small[:, 2, :]))
            ch.step(copy(ordn[:, :, 0], node_i[:, :]))
            ch.step(copy(ordn[:, :, 1], rowp[:, :]))
            ch.step(copy(ordn[:, :, 2], deg[:, :]))
            ch.step(nc.vector.memset(ordn[:, :, 3], 0))
            ch.wait()
            v.sem_inc(S["rank_ready"], 1)

            v.wait_ge(S["weights_in"], 16 * NLOAD)
            for s in range(2):
                tmp = kvq[:, :, s * D:(s + 1) * D]
                ch.link(tt(tmp, wcat[:, :, 0:D], avec[:, s, :].unsqueeze(1).to_broadcast([P, KD, D]), ALU.mult))
                ch.step(inner_sum(wcat[:, :, D + s * H:D + (s + 1) * H], tmp.rearrange("p k (h d) -> p k h d", h=H)))
                ch.link(tt(whs[:, s, 0:D], avec[:, 2, :], avec[:, s, :], ALU.mult))
                ch.step(inner_sum(bias1[:, D + s * H:D + (s + 1) * H], whs[:, s, 0:D].rearrange("p (h d) -> p h d", h=H)))
            ch.step(copy(bias1[:, 0:D], avec[:, 2, :]))
            ch.wait()
            ch.link(tt(bias1[:, D + H:WCOL], bias1[:, D + H:WCOL], abias[:, :], ALU.add))
            wk4 = wkv.rearrange("p k (h d) -> p k h d", d=MD)
            ch.link(inner_sum(kvr[:, 0, :, :], wk4))
            ch.link(ts(kvr[:, 1, :, :], kvr[:, 0, :, :], -1.0 / MD, None, ALU.mult))
            for k in range(KD):
                ch.step(tt(wk4[:, k], wk4[:, k], kvr[:, 1, k, :].unsqueeze(2).to_broadcast([P, 8, MD]), ALU.add))
            ch.wait()

            def x_rows(i):
                return lambda b: x_all[:, bass.ds(i * 2 + b, 1), :].rearrange("p o d -> p (o d)")

            def first_phase(i, now=True, ahead=True):
                if ahead:
                    for b in range(2):
                        ch.step(nc.vector.bn_stats(stats[:, b, :], x_rows(i + 1)(b)))
                    stats_in = ch.n
                if now:
                    v.wait_ge(S["wh_ps"], i + 1)
                    v.wait_ge(S["whs_free"], i + 1)
                    for b in range(2):
                        ch.step(tt(whs[:, b, :], bank[b][:, 0:WCOL], bias1, ALU.add))
                    wh_out = ch.n
                if ahead:
                    ch.wait(stats_in)
                    apart(v)
                    for b in range(2):
                        ch.step(nc.vector.bn_aggr(mv[:, b, :], stats[:, b, :]))
                    aggregated = ch.n
                if now:
                    for b in range(2):
                        v.wait_ge(S["sq_ready"], i * 2 + (b + 1))
                        ch.step(inner_sum(kvr[:, 0, b, :], kvq[:, b, :].rearrange("p (h d) -> p h d", d=MD)))
                    summed = ch.n
                if ahead:
                    ch.wait(aggregated)
                    ch.step(ts(vare[:, :], mv[:, :, 1], EPS, None, ALU.add))
                    var_in = ch.n
                if now:
                    ch.wait(wh_out)
                    v.sem_inc(S["wh_ready"], 1)
                    v.wait_ge(S["s2_free"], i + 1)
                    ch.step(copy(s2st[:, :, :], whs[:, :, ROW:WCOL]))
                    copy(rankst[:, :], ranki[:, bass.ds(i * 2, 2)]).then_inc(S["s2_ready"], 1)
                    ch.wait(summed)
                    ch.step(ts(kvr[:, 0, :, :], kvr[:, 0, :, :], 1.0 / MD, EPS, ALU.mult, ALU.add))
                    kvar_in = ch.n
                if ahead:
                    ch.wait(var_in)
                    nc.vector.reciprocal(rs[:, :, 0], vare[:, :]).then_inc(S["var_ready"], 1)
                if now:
                    ch.wait(kvar_in)
                    nc.vector.reciprocal(kvr[:, 0, :, :], kvr[:, 0, :, :]).then_inc(S["kvar_ready"], 1)
                if ahead:
                    v.wait_ge(S["rstd_ready"], i + 2)
                    if now:
                        v.wait_ge(S["tp_ready"], i + 1)
                    for b in range(2):
                        last = ts(xn[:, b, :], x_rows(i + 1)(b), mv[:, b, 0:1], rs[:, b, 1:2], ALU.subtract, ALU.mult)
                    last.then_inc(S["xn_ready"], 1)
                if now:
                    v.wait_ge(S["krs_ready"], i + 1)
                    v.wait_ge(S["kv_done"], i + 1)
                    for b in range(2):
                        tt(kvs[:, b, :].rearrange("p (h d) -> p h d", d=MD), bank[2 + b][:, :].rearrange("p (h d) -> p h d", d=MD),
                           kvr[:, 1, b, :].unsqueeze(2).to_broadcast([P, 8, MD]), ALU.mult).then_inc(S["kn_ready"], 1)

            first_phase(-1, now=False)
            start, per = ch.base + ch.n, 11
            with v.Fori(0, SPLIT) as i:
                ch.at(i * per + start)
                first_phase(i)
                assert ch.n == per, ch.n
            ch.at(start + SPLIT * per)

            v.wait_ge(S["ord_in"], 16)
            ch.step(copy(rowp[:, :], ordn[:, :, 1]))
            ch.step(copy(deg[:, :], ordn[:, :, 2]))
            ch.step(ts(valid[:, :], ordn[:, :, 0], float(N), None, ALU.is_lt))
            ch.step(nc.vector.memset(m_all[:, :, :], LOW))
            ch.step(nc.vector.memset(den_all[:, :, :], 0.0))
            ch.step(nc.vector.memset(ctlf[:, :], 0.0))
            ch.wait()
            v.sem_inc(S["mx_ready"], 1)

            def windows(c):
                c.link(copy(starti[:, :], rowp[:, :]))
                c.step(ts(winr[:, :], starti[:, :], WSTEP.bit_length() - 1, None, ALU.arith_shift_right))
                for n in range(4):
                    c.step(ts(bits[:, n, :], starti[:, :], n, 1, ALU.arith_shift_right, ALU.bitwise_and))
                c.wait()
                c.link(ts(winr[:, :], winr[:, :], NWROW - 1, None, ALU.min))

            def shifted(c, gr, o):
                tiles = slice(gr * WT, (gr + 1) * WT)
                cur, other, width = wina, winb, WLEN
                for n in (3, 2, 1, 0):
                    width -= 1 << n
                    to = other[:, tiles, 0:width] if n else o[:, tiles, 0:WIN]
                    take = width if n else WIN
                    c.link(copy(to, cur[:, tiles, 0:take]))
                    apart(v)
                    c.link(nc.vector.copy_predicated(to, bits[:, n, tiles].unsqueeze(2).to_broadcast([P, WT, take]),
                                                     cur[:, tiles, (1 << n):(1 << n) + take]))
                    cur, other = other, cur
                apart(v)

            def slot_groups(c):
                c.link(ts(small[:, 0, :], mxrem[:, :], float(SG - 1), None, ALU.add))
                c.link(copy(groups[:, :], small[:, 0, :]))
                c.link(ts(groups[:, :], groups[:, :], SG.bit_length() - 1, None, ALU.arith_shift_right))
                c.step(ts(groups[:, :], groups[:, :], 1, NG, ALU.max, ALU.min))

            def group_sums(c, mask):
                for b in range(2):
                    c.step(scan(gcumf[:, b, :], onesf[:, 0:NPAIR], mask.rearrange("p (i b) -> p b i", b=2)[:, b, :],
                                ctlf[:, 5 + b:6 + b], ALU.mult, ALU.add))
                c.wait()
                c.step(copy(ctlf[:, 5:7], gcumf[:, :, NPAIR - 1]))
                c.step(copy(gcum[:, :, :], gcumf[:, :, :]))
                c.step(tt(gbase[:, :, :], gcumf[:, :, :], groups[:, :].rearrange("p (i b) -> p b i", b=2), ALU.subtract))

            windows(ch)
            v.sem_inc(S["lwin_ready"], 1)
            v.wait_ge(S["mx_done"], 1)
            ch.link(reduce(ctlf[:, 3:4], mxrem[:, :], AX.X, ALU.max))
            ch.link(ts(ctlf[:, 3:4], ctlf[:, 3:4], (WIN - 1) / 2 - WIN, 1.0 / WIN, ALU.add, ALU.mult))
            ch.link(ts(ctlf[:, 3:4], ctlf[:, 3:4], 0.0, None, ALU.max))
            ch.link(copy(nextra[:, :], ctlf[:, 3:4]))
            start = ch.base + ch.n
            with v.Fori(SPLIT, NPAIR - 1) as i:
                ch.at(i * per + (start - SPLIT * per))
                first_phase(i)
            ch.at(start + (NPAIR - 1 - SPLIT) * per)
            first_phase(NPAIR - 1, ahead=False)
            v.wait_ge(S["lwin_in"], 16 * NT)
            for gr in range(NT // WT):
                shifted(ch, gr, idx)
            v.wait_ge(S["s2_in"], 16)
            ch.wait()
            v.sem_inc(S["tables_ready"], 1)

            v.wait_ge(S["mw_in"], 32)
            v.wait_ge(S["kv_done"], NPAIR + 2)
            ch.link(nc.vector.memset(kvd, 0.0))
            for j in range(2):
                for q in range(2):
                    r = slice(q * MD, (q + 1) * MD)
                    ch.step(ts(kvd[r, j, r], bank[4][r, j * P + q * MD:j * P + (q + 1) * MD], 1.0 / N, None, ALU.mult))
            ch.wait()
            v.sem_inc(S["kvd_ready"], 1)
            v.wait_ge(S["t1_ps"], 1)
            ch.link(copy(t1, bank[6][:, :].rearrange("p (k c) -> p k c", k=2)))
            v.sem_inc(S["t1_ready"], 1)
            v.wait_ge(S["mix_ps"], 1)
            ch.link(copy(mixw[:, :, :], bank[7][:, :].rearrange("p (k c) -> p k c", k=2)))
            v.sem_inc(S["mix_ready"], 1)
            start, per = ch.base + ch.n, 5
            with v.Fori(0, NPAIR) as i:
                ch.at(i * per + start)
                v.wait_ge(S["base_ps"], i + 2)
                v.wait_ge(S["bases_free"], i + 1)
                for b in range(2):
                    ch.step(tt(base_s[:, b, :], bank[b][:, 0:D], bo_b[:, :], ALU.add))
                ch.wait()
                for b in range(2):
                    ch.step(tt(base_s[:, b, :], base_s[:, b, :], x_rows(i)(b), ALU.add))
                ch.wait()
                v.sem_inc(S["base_ready"], 1)
                ch.step(copy(x_all[:, bass.ds(i * 2, 2), :], zeros[:, :].unsqueeze(1).to_broadcast([P, 2, D])))
                assert ch.n == per, ch.n
            ch.at(start + NPAIR * per)

            UNIT = 14

            def stage(p, i, b, index):
                copy(idxs[:, b, :], index[:, bass.ds(i * 2 + b, 1), :].rearrange("p o k -> p (o k)")
                     ).then_inc(S[p, "idxs_ready"][b], 1)

            def attend(p, cu, i, u, b):
                cu.at(u * (2 * UNIT) + b * UNIT)
                t = i * 2 + b
                one = lambda a: a[:, bass.ds(t, 1), :].rearrange("p o h -> p (o h)")
                ngath = v.value_load(gcum[0:1, b, bass.ds(i, 1)], min_val=1, max_val=NT * EP)
                v.wait_ge(S[p, "gath_in"][b], ngath * (16 * SG))
                cu.step(ts(pen[:, :], iota_f[:, 0:WIN], deg[:, bass.ds(t, 1)], LOWER, ALU.is_ge, ALU.mult))
                cu.link(tt(ez[:, :, :], gath[:, b, :, D:ROW], s2_all[:, bass.ds(t, 1), :].to_broadcast([P, WIN, H]), ALU.add))
                cu.link(nc.vector.scalar_tensor_tensor(ez[:, :, :], ez[:, :, :], ALPHA, ez[:, :, :], ALU.mult, ALU.max))
                cu.link(tt(ez[:, :, :], ez[:, :, :], pen[:, :].unsqueeze(2).to_broadcast([P, WIN, H]), ALU.add))
                cu.link(reduce(es[:, 0, :], ez[:, :, :].rearrange("p k h -> p h k"), AX.X, ALU.max))
                cu.link(tt(es[:, 1, :], es[:, 0, :], one(m_all), ALU.max))
                cu.link(tt(es[:, 2, :], one(m_all), es[:, 1, :], ALU.subtract))
                v.sem_inc(S[p, "f_in"], 1)
                cu.step(copy(one(m_all), es[:, 1, :]))
                cu.link(tt(ez[:, :, :], ez[:, :, :], es[:, 1, :].unsqueeze(1).to_broadcast([P, WIN, H]), ALU.subtract))
                v.sem_inc(S[p, "ex_in"], 1)
                v.wait_ge(S[p, "f_ready"], u * 2 + (b + 1))
                cu.step(tt(accf[:, :].rearrange("p (h d) -> p h d", h=H), one(x_all).rearrange("p (h d) -> p h d", h=H),
                           es[:, 3, :].unsqueeze(2).to_broadcast([P, H, DH]), ALU.mult))
                cu.step(tt(es[:, 4, :], one(den_all), es[:, 3, :], ALU.mult))
                cu.wait()
                v.sem_inc(S[p, "accf_ready"], 1)
                v.wait_ge(S[p, "ex_ready"], u * 2 + (b + 1))
                ng = v.value_load(groups[0:1, bass.ds(t, 1)], min_val=1, max_val=NG)
                for q in range(NG):
                    ks = slice(q * SG, (q + 1) * SG)
                    rows = gath[:, b, ks, 0:D].rearrange("p k (h d) -> p k h d", h=H)
                    with v.If(ng > q):
                        tt(rows, rows, ez[:, ks, :].unsqueeze(3).to_broadcast([P, SG, H, DH]), ALU.mult).then_inc(S[p, "prod"][b], 1)
                cu.link(reduce(es[:, 5, :], ez[:, :, :].rearrange("p k h -> p h k"), AX.X, ALU.add))
                cu.step(tt(one(den_all), es[:, 4, :], es[:, 5, :], ALU.add))
                v.wait_ge(S[p, "acc_ps"], u * 2 + (b + 1))
                apart(v)
                cu.step(copy(one(x_all), bank[b][:, 0:D]))
                cu.wait()
                apart(v)
                assert cu.n == UNIT, cu.n

            def next_stage(p, i, b, n, index):
                with v.If(i < n - 1):
                    stage(p, i + 1, b, index)

            cx, ci, cu = Chain(v, S["x_pass"]), Chain(v, S["idx_step"]), Chain(v, S["x", "unit"])
            PASS, IDX = 33, 8
            nx = v.value_load(nextra[0:1, 0:1], min_val=0, max_val=EP // WIN)
            for a, f in ((deg, -float(WIN)), (rowp, float(WIN)), (mxrem, -float(WIN))):
                ch.link(ts(ctlf[:, 2:3], nextra[:, 0:1], f, None, ALU.mult))
                ch.link(ts(a[:, :], a[:, :], ctlf[:, 2:3], None, ALU.add))
            with v.If(nx > 0):
                with v.Fori(0, nx) as w:
                    cx.at(w * PASS)
                    slot_groups(cx)
                    cx.link(ts(small[:, 1, :], mxrem[:, :], 0.0, None, ALU.is_gt))
                    cx.link(inner_sum(ctlf[:, 1:2], small[:, 1, :]))
                    cx.step(ts(ctl[:, 3:4], ctlf[:, 1:2], 1.0, None, ALU.add))
                    cx.link(ts(ctlf[:, 2:3], ctlf[:, 1:2], (WT - 1) / 2, 1.0 / WT, ALU.add, ALU.mult))
                    cx.step(ts(ctl[:, 3:4], ctl[:, 3:4], 1, None, ALU.arith_shift_right))
                    cx.step(copy(ctl[:, 2:3], ctlf[:, 2:3]))
                    cx.link(copy(ctl[:, 0:1], ctlf[:, 0:1]))
                    cx.link(ts(ctl[:, 2:4], ctl[:, 2:4], 1, None, ALU.max))
                    cx.step(tt(ctlf[:, 0:1], ctlf[:, 0:1], ctl[:, 3:4], ALU.add))
                    cx.step(tt(ctlf[:, 4:5], ctlf[:, 4:5], ctl[:, 2:3], ALU.add))
                    cx.link(ts(ctlf[:, 1:2], ctl[:, 3:4], 2.0, None, ALU.mult))
                    cx.step(copy(ctl[:, 4:5], ctlf[:, 4:5]))
                    cx.link(ts(gmask[:, :], iota_f[:, 0:NT], ctlf[:, 1:2], None, ALU.is_lt))
                    cx.link(tt(gmask[:, :], gmask[:, :], groups[:, :], ALU.mult))
                    group_sums(cx, gmask[:, :])
                    windows(cx)
                    v.sem_inc(S["x_ready"], 1)
                    npr = v.value_load(ctl[0:1, 3:4], min_val=1, max_val=NPAIR)
                    lo = v.value_load(ctl[0:1, 0:1], min_val=0, max_val=unit_bound)
                    ngr = v.value_load(ctl[0:1, 2:3], min_val=1, max_val=NT // WT)
                    nwt = v.value_load(ctl[0:1, 4:5], min_val=1, max_val=NT * EP)
                    v.wait_ge(S["x_win_in"], nwt * (16 * WT))
                    ci.at(w * (IDX * NT // WT))
                    for gr in range(NT // WT):
                        with v.If(ngr > gr):
                            n0 = ci.n
                            shifted(ci, gr, idx_x)
                            assert ci.n - n0 == IDX, ci.n - n0
                        with v.Else():
                            v.sem_inc(S["idx_step"], IDX)
                    v.sem_inc(S["x_idx_ready"], 1)
                    for b in range(2):
                        stage("x", 0, b, idx_x)
                    with v.Fori(0, npr) as i:
                        for b in range(2):
                            attend("x", cu, i, i + lo, b)
                            next_stage("x", i, b, npr, idx_x)
                    v.wait_ge(S["x", "unit"], (lo + npr) * (2 * UNIT))
                    apart(v)
                    cx.step(ts(deg[:, :], deg[:, :], float(WIN), None, ALU.add))
                    cx.step(ts(rowp[:, :], rowp[:, :], -float(WIN), None, ALU.add))
                    cx.step(ts(mxrem[:, :], mxrem[:, :], float(WIN), None, ALU.add))
                    cx.wait()
                    apart(v)
                    assert cx.n == PASS, cx.n
                    v.sem_inc(S["x_done"], 1)

            slot_groups(ch)
            ch.link(nc.vector.memset(ctlf[:, :], 0.0))
            group_sums(ch, groups[:, :])
            ch.wait()
            v.sem_inc(S["l_ready"], 1)
            for b in range(2):
                stage("l", 0, b, idx)
            cl, ce = Chain(v, S["l", "unit"]), Chain(v, S["dve_end"])
            per = 14
            with v.Fori(0, NPAIR) as i:
                copy(basei[:, :], ordn[:, bass.ds(i * 2, 2), 0]).then_inc(S["basei_ready"], 1)
                for b in range(2):
                    attend("l", cl, i, i, b)
                    next_stage("l", i, b, NPAIR, idx)
                ce.at(i * per)
                heads = lambda a: a.rearrange("p (h d) -> p h d", h=H)
                one = lambda a, b: a[:, bass.ds(i * 2 + b, 1), :].rearrange("p o h -> p (o h)")
                pair = den_all[:, bass.ds(i * 2, 2), :]
                ce.link(ts(pair, pair, 1e-30, None, ALU.max))
                apart(v)
                ce.link(nc.vector.reciprocal(pair, pair))
                for b in range(2):
                    ce.step(tt(heads(x_rows(i)(b)), heads(x_rows(i)(b)), one(den_all, b).unsqueeze(2).to_broadcast([P, H, DH]), ALU.mult))
                ce.wait()
                for b in range(2):
                    v.wait_ge(S["baseg_in"][b], i * 16 + 16)
                    ce.step(tt(x_rows(i)(b), x_rows(i)(b), baseg[:, b, :], ALU.add))
                ce.wait()
                apart(v)
                for b in range(2):
                    ce.step(nc.vector.bn_stats(stats[:, b, :], x_rows(i)(b)))
                ce.wait()
                apart(v)
                for b in range(2):
                    ce.step(nc.vector.bn_aggr(mv[:, b, :], stats[:, b, :]))
                ce.wait()
                ce.link(ts(vare[:, :], mv[:, :, 1], EPS, None, ALU.add))
                nc.vector.reciprocal(rs[:, :, 0], vare[:, :]).then_inc(S["v2_ready"], 1)
                v.wait_ge(S["r2_ready"], i + 1)
                for b in range(2):
                    ce.step(ts(xn2s[:, b, :], x_rows(i)(b), mv[:, b, 0:1], rs[:, b, 1:2], ALU.subtract, ALU.mult))
                ce.wait()
                v.sem_inc(S["xn2_ready"], 1)
                v.wait_ge(S["lg_ps"], i + 1)
                ce.link(tt(logit[:, bass.ds(i * 2, 2), :], bank[6][:, 0:2 * NE].rearrange("p (b e) -> p b e", b=2),
                           bg_b[:, :].unsqueeze(1).to_broadcast([P, 2, NE]), ALU.add))
                assert ce.n == per, ce.n
            ce.at(NPAIR * per)
            v.sem_inc(S["lg_done"], 1)

            bt = lambda a: a.unsqueeze(2).to_broadcast([P, NT, NE, NE])
            be = lambda a: a.unsqueeze(3).to_broadcast([P, NT, NE, NE])
            ce.step(tt(cmp8, bt(logit), be(logit), ALU.is_gt))
            ce.step(tt(cmp8b, bt(logit), be(logit), ALU.is_equal))
            ce.step(tt(tri8, iota_f[:, 0:NE].unsqueeze(1).to_broadcast([P, NE, NE]),
                       iota_f[:, 0:NE].unsqueeze(2).to_broadcast([P, NE, NE]), ALU.is_lt))
            ce.wait()
            ce.link(tt(cmp8b, cmp8b, tri8.unsqueeze(1).to_broadcast([P, NT, NE, NE]), ALU.mult))
            ce.link(tt(cmp8, cmp8, cmp8b, ALU.add))
            ce.link(inner_sum(pos, cmp8))
            for j in range(2):
                ce.step(ts(msk[:, j], pos, float(j), None, ALU.is_equal))
            ce.wait()
            for j in range(2):
                ce.step(tt(cmp8[:, :, j, :], msk[:, j], logit, ALU.mult))
            ce.wait()
            for j in range(2):
                ce.step(inner_sum(small[:, j, :], cmp8[:, :, j, :]))
            ce.wait()
            ce.link(tt(small[:, 2, :], small[:, 1, :], small[:, 0, :], ALU.subtract))
            v.sem_inc(S["gap_ready"], 1)
            for j in range(2):
                ce.step(tt(msk[:, j], msk[:, j], valid[:, :].unsqueeze(2).to_broadcast([P, NT, NE]), ALU.mult))
            ce.wait()
            ce.link(tt(m01.rearrange("p (t e) -> p t e", t=NT), msk[:, 0], msk[:, 1], ALU.add))
            v.sem_inc(S["m01_ready"], 1)
            v.wait_ge(S["pre_ps"], 1)
            ce.step(copy(pos, bank[0][:, 0:NT * NE].rearrange("p (t e) -> p t e", t=NT)))
            ce.step(copy(tex3, bank[1][:, 0:NT * NE].rearrange("p (t e) -> p e t", t=NT)))
            ce.wait()
            for e in range(NE):
                ce.step(scan(tsc3[:, e, :], onesf[:, 0:NT], tex3[:, e, :], 0.0, ALU.mult, ALU.add))
            ce.wait()
            ce.step(copy(cnt[:, 0, :], tsc3[:, :, NT - 1]))
            ce.link(tt(tex3, tsc3, tex3, ALU.subtract))
            ce.link(ts(cnt[:, 0, :], cnt[:, 0, :], float(TT - 1), None, ALU.add))
            ce.link(copy(cnti[:, :], cnt[:, 0, :]))
            ce.link(ts(cnti[:, :], cnti[:, :], TT.bit_length() - 1, None, ALU.arith_shift_right))
            ce.link(ts(cnti[:, :], cnti[:, :], 1, None, ALU.max))
            ce.link(copy(cnt[:, 1, :], cnti[:, :]))
            ce.link(scan(cnt[:, 2, :], onesf[:, 0:NE], cnt[:, 1, :], 0.0, ALU.mult, ALU.add))
            ce.link(tt(cnt[:, 3, :], cnt[:, 2, :], cnt[:, 1, :], ALU.subtract))
            ce.step(copy(ebnd[:, 0, :], cnt[:, 3, :]))
            ce.step(copy(ebnd[:, 1, :], cnt[:, 2, :]))
            ce.link(ts(cnt[:, 0, :], cnt[:, 3, :], float(TT), None, ALU.mult))
            v.sem_inc(S["bounds_ready"], 1)
            ce.link(tt(pos, pos, tex3.rearrange("p e t -> p t e"), ALU.add))
            ce.link(tt(pos, pos, cnt[:, 0, :].unsqueeze(1).to_broadcast([P, NT, NE]), ALU.add))
            for j in range(2):
                ce.step(tt(cmp8[:, :, j, :], msk[:, j], pos, ALU.mult))
            ce.link(ts(small[:, 0, :], valid[:, :], 1.0, -float(NOWHERE), ALU.subtract, ALU.mult))
            for j in range(2):
                ce.step(inner_sum(slotf[:, j, :], cmp8[:, :, j, :]))
            ce.wait()
            for j in range(2):
                ce.step(tt(slotf[:, j, :], slotf[:, j, :], small[:, 0, :], ALU.add))
            ce.wait()
            ce.link(copy(sloti[:, :, :], slotf[:, :, :]))
            v.wait_ge(S["gexp_ready"], 1)
            ce.link(ts(small[:, 1, :], small[:, 3, :], 1.0, None, ALU.add))
            ce.link(nc.vector.reciprocal(wts[:, 0, :], small[:, 1, :]))
            ce.link(tt(wts[:, 1, :], wts[:, 0, :], small[:, 3, :], ALU.mult))
            for j in range(2):
                ce.step(tt(msk[:, j], msk[:, j], wts[:, j, :].unsqueeze(2).to_broadcast([P, NT, NE]), ALU.mult))
            ce.wait()
            v.wait_ge(S["xn2_copied"], NPAIR)
            ce.step(tt(xrow_all[:, :, D:D + NE], msk[:, 0], msk[:, 1], ALU.add))
            ce.link(copy(xrow_all[:, :, D + NE:XROW].bitcast(I32), ordn[:, :, 0:1]))
            v.sem_inc(S["slot_ready"], 1)

            v.sem_inc(S["y_ready"], 1)
            cy = Chain(v, S["y_step"])

            def tokens_in(i, par):
                v.wait_ge(S["xs_in"], i * 16 + 16)
                copy(meta[:, :, :], xs_s[:, :, D:XROW])
                v.wait_ge(S["xte_ps"], i + 1)
                copy(xTe[:, bass.ds(par, 1), :, :].rearrange("p o k n -> p (o k) n"),
                     bank[6][:, :].rearrange("p (k n) -> p k n", k=KD)).then_inc(S["xte_ready"], 1)

            tokens_in(0, 0)
            with v.Fori(0, NE // 2) as ep:
                for s in range(2):
                    e = ep * 2 + s
                    lo = v.value_load(ebnd[0:1, 0, bass.ds(e, 1)], min_val=0, max_val=XT - 2)
                    hi = v.value_load(ebnd[0:1, 1, bass.ds(e, 1)], min_val=1, max_val=XT - 1)
                    v.wait_ge(S["ew_in"][s], ep * 64 + 64)
                    apart(v)
                    with v.Fori(lo, hi) as i:
                        cy.at(i * 3)
                        v.wait_ge(S["ys_free"], i + 1)
                        v.wait_ge(S["xte_ready"], i + 1)
                        cy.link(copy(metao[:, :, :], meta[:, :, :]))
                        tokens_in(i + 1, (i + 1) % 2)
                        v.wait_ge(S["y_ps"], i + 1)
                        for a in range(2):
                            cy.step(tt(ysb[:, a, :], bank[4 + a][:, 0:D], b2s[:, s, :], ALU.add))
                        cy.wait()
                        for a in range(2):
                            last = ts(ysb[:, a, :], ysb[:, a, :], metao[:, a, bass.ds(e, 1)], None, ALU.mult)
                        last.then_inc(S["y_ready"], 1)
                    v.wait_ge(S["y_ready"], hi + 1)
                    v.sem_inc(S["ew_used"][s], 1)

        @block.tensor
        def _(pe):
            mm = nc.tensor.matmul

            pe.wait_ge(S["consts"], 1)
            zb = zeros[:, :].bitcast(BF16)[:, 0:NT]
            mm(bank[0][:, 0:NT], onesb[:, :], zb, start=True, stop=False)
            pe.sem_inc(S["hist_used"], 2)
            with pe.Fori(0, NHIST) as i:
                for a in range(2):
                    pe.wait_ge(S["hist_oh"], i * 2 + (a + 1))
                    for j in range(HC):
                        last = mm(bank[0][:, 0:NT], oh_b[:, a, j, :], oh_a[:, a, j, :], start=False, stop=False)
                    last.then_inc(S["hist_used"], 1)
            mm(bank[0][:, 0:NT], onesb[:, :], zb, start=False, stop=True).then_inc(S["hist_used"], 1)
            pe.wait_ge(S["deg_ready"], 1)
            mm(bank[1][:, 0:NT], ltf[:, :], deg[:, :], start=True, stop=True)
            mm(bank[1][:, 64:64 + NT], onesf[:, :], deg[:, :], start=True, stop=True).then_inc(S["rowp_ps"], 1)
            pe.wait_ge(S["ohd_ready"], 1)
            for n, lo in enumerate(range(0, NT, BT)):
                k = min(BT, NT - lo)
                if n >= 2:
                    pe.wait_ge(S["cnt_used"], n - 1)
                bk = 2 + 2 * (n % 2)
                oh = oh_d[:, lo:lo + k, :].rearrange("p t c -> p (t c)")
                mm(bank[bk][:, 0:k * NBUCK], ltb[:, :], oh, start=True, stop=True)
                mm(bank[bk + 1][:, 0:k * NBUCK], onesb[:, :], oh, start=True, stop=True).then_inc(S["cnt_ps"], 1)

            pe.wait_ge(S["cnt_used"], (NT + BT - 1) // BT)
            mm(bank[4][:, 0:D], ident[:, :], zeros[:, :], start=True, stop=False)
            pe.sem_inc(S["kv_done"], 1)

            def kv_outer(i, rows=(P, P)):
                for b in range(2):
                    if rows[b]:
                        pe.wait_ge(S["khat_ready"], i * 2 + (b + 1))
                        for j in range(2):
                            last = mm(bank[4][:, j * P:(j + 1) * P], kvs[0:rows[b], b, j * P:(j + 1) * P],
                                      kvs[0:rows[b], b, D + j * P:D + (j + 1) * P], start=False, stop=False)
                last.then_inc(S["kv_done"], 1)

            def first_phase(i, first=False):
                pe.wait_ge(S["xn_ready"], i + 1)
                if not first:
                    pe.wait_ge(S["xT_ready"], i * 2)
                for k in range(KD):
                    for b in range(2):
                        last = nc.tensor.transpose(bank[5][:, k * 2 * P + b * P:k * 2 * P + (b + 1) * P],
                                                   xn[:, b, k * P:(k + 1) * P], ident[:, :])
                last.then_inc(S["tp_ready"], 1)
                pe.wait_ge(S["xT_ready"], i * 2 + 1)
                if not first:
                    pe.wait_ge(S["wh_ready"], i)
                for b in range(2):
                    for k in range(KD):
                        last = mm(bank[b][:, 0:WCOL], xTs[:, k, b * P:(b + 1) * P], wcat[:, k, :], start=(k == 0), stop=(k == KD - 1))
                last.then_inc(S["wh_ps"], 1)
                if not first:
                    pe.wait_ge(S["kn_ready"], i * 2)
                for b in range(2):
                    for k in range(KD):
                        last = mm(bank[2 + b][:, :], xTs[:, k, b * P:(b + 1) * P], wkv[:, k, :], start=(k == 0), stop=(k == KD - 1))
                    last.then_inc(S["kv_ps"], 1)

            first_phase(0, True)
            with pe.Fori(1, NPAIR) as i:
                first_phase(i)
                kv_outer(i - 1)
            kv_outer(NPAIR - 1, (TAIL, 0))
            mm(bank[4][:, 0:D], ident[:, :], zeros[:, :], start=False, stop=True).then_inc(S["kv_done"], 1)

            pe.wait_ge(S["mw_in"], 32)
            pe.wait_ge(S["kvd_ready"], 1)
            for j in range(2):
                last = mm(bank[6][:, j * D:(j + 1) * D], kvd[:, j, :], wq_s[:, j, :], start=True, stop=True)
            last.then_inc(S["t1_ps"], 1)
            pe.wait_ge(S["t1_ready"], 1)
            for k in range(KD):
                for j in range(2):
                    last = mm(bank[7][:, k * D:(k + 1) * D], t1[:, j, k * P:(k + 1) * P], wo_s[:, j, :], start=(j == 0), stop=(j == 1))
            last.then_inc(S["mix_ps"], 1)
            pe.wait_ge(S["mix_ready"], 1)
            pe.sem_inc(S["base_ps"], 1)

            def mixed(i, first=False):
                pe.wait_ge(S["mxs_ready"], i + 1)
                if not first:
                    pe.wait_ge(S["base_ready"], i)
                for b in range(2):
                    for k in range(KD):
                        last = mm(bank[b][:, 0:D], mxs[:, k, b * P:(b + 1) * P], mixw[:, k, :], start=(k == 0), stop=(k == KD - 1))
                last.then_inc(S["base_ps"], 1)

            mixed(0, True)
            with pe.Fori(1, NPAIR) as i:
                mixed(i)

            def slot_sums(p, i, u, b):
                ng = pe.value_load(groups[0:1, bass.ds(i * 2 + b, 1)], min_val=1, max_val=NG)
                nprod = pe.value_load(gbase[0:1, b, bass.ds(i, 1)], min_val=0, max_val=NT * EP)
                pe.wait_ge(S[p, "accf_ready"], u * 2 + (b + 1))
                mm(bank[b][:, 0:D], ident[:, :], accf[:, :], start=True, stop=False)
                for q in range(NG):
                    with pe.If(ng > q):
                        pe.wait_ge(S[p, "prod"][b], nprod + (q + 1))
                        for k in range(q * SG, (q + 1) * SG):
                            mm(bank[b][:, 0:D], ident[:, :], gath[:, b, k, 0:D], start=False, stop=False)
                mm(bank[b][:, 0:D], ident[:, :], zeros[:, :], start=False, stop=True).then_inc(S[p, "acc_ps"], 1)

            pe.wait_ge(S["tables_ready"], 1)
            nx = pe.value_load(nextra[0:1, 0:1], min_val=0, max_val=EP // WIN)
            with pe.If(nx > 0):
                with pe.Fori(0, nx) as w:
                    pe.wait_ge(S["x_ready"], w + 1)
                    apart(pe)
                    lo = pe.value_load(ctl[0:1, 0:1], min_val=0, max_val=unit_bound)
                    npr = pe.value_load(ctl[0:1, 3:4], min_val=1, max_val=NPAIR)
                    with pe.Fori(0, npr) as i:
                        for b in range(2):
                            slot_sums("x", i, i + lo, b)
                    pe.wait_ge(S["x_done"], w + 1)
                    apart(pe)
            pe.wait_ge(S["l_ready"], 1)
            with pe.Fori(0, NPAIR) as i:
                for b in range(2):
                    slot_sums("l", i, i, b)
                pe.wait_ge(S["xn2_ready"], i + 1)
                for k in range(KD):
                    for b in range(2):
                        last = nc.tensor.transpose(bank[5][:, k * 2 * P + b * P:k * 2 * P + (b + 1) * P],
                                                   xn2s[:, b, k * P:(k + 1) * P], ident[:, :])
                last.then_inc(S["tp2_ready"], 1)
                pe.wait_ge(S["xTr_ready"], i + 1)
                for b in range(2):
                    for k in range(KD):
                        last = mm(bank[6][:, b * NE:(b + 1) * NE], xTr[:, k, b * P:(b + 1) * P], wg_s[:, k, :], start=(k == 0), stop=(k == KD - 1))
                last.then_inc(S["lg_ps"], 1)
            pe.wait_ge(S["m01_ready"], 1)
            mm(bank[0][:, 0:NT * NE], ltb[:, :], m01, start=True, stop=True)
            mm(bank[1][:, 0:NT * NE], onesb[:, :], m01, start=True, stop=True).then_inc(S["pre_ps"], 1)

            def tokens_in(i, first=False):
                pe.wait_ge(S["xs_in"], i * 16 + 16)
                if not first:
                    pe.wait_ge(S["xte_ready"], i)
                for k in range(KD):
                    for a in range(2):
                        last = nc.tensor.transpose(bank[6][:, k * TT + a * P:k * TT + (a + 1) * P],
                                                   xs_s[:, a, k * P:(k + 1) * P], ident[:, :])
                last.then_inc(S["xte_ps"], 1)

            pe.wait_ge(S["bounds_ready"], 1)
            tokens_in(0, True)
            with pe.Fori(0, NE // 2) as ep:
                for s in range(2):
                    lo = pe.value_load(ebnd[0:1, 0, bass.ds(ep * 2 + s, 1)], min_val=0, max_val=XT - 2)
                    hi = pe.value_load(ebnd[0:1, 1, bass.ds(ep * 2 + s, 1)], min_val=1, max_val=XT - 1)
                    pe.wait_ge(S["ew_in"][s], ep * 64 + 64)
                    apart(pe)

                    def up(i, c):
                        pe.wait_ge(S["h_ready"], i * FC + (c + 1))
                        for k in range(KD):
                            last = mm(bank[c % 4][:, 0:TT], w1s[:, s, k, c * P:(c + 1) * P],
                                      xTe[:, bass.ds(i % 2, 1), k, :].rearrange("p o n -> p (o n)"), start=(k == 0), stop=(k == KD - 1))
                        last.then_inc(S["h_ps"], 1)

                    def down(i, c):
                        pe.wait_ge(S["h_ready"], i * FC + (c + 5))
                        for a in range(2):
                            last = mm(bank[4 + a][:, 0:D], hT[:, c, a * P:(a + 1) * P], w2s[:, s, c, :], start=(c == 0), stop=(c == FC - 1))
                        if c == FC - 1:
                            last.then_inc(S["y_ps"], 1)

                    with pe.Fori(lo, hi) as i:
                        pe.wait_ge(S["xte_ready"], i + 1)
                        for c in range(FC):
                            up(i, c)
                            if c == 2:
                                pe.wait_ge(S["y_ready"], i + 1)
                            if c >= 2:
                                down(i, c - 2)
                            if c == FC // 2:
                                tokens_in(i + 1)
                        down(i, FC - 2)
                        down(i, FC - 1)


def kernel(x, src, dst, L0_gnn_W, L0_gnn_bW, L0_gnn_a_src, L0_gnn_a_dst, L0_gnn_a_bias, L0_mix_wq, L0_mix_wk, L0_mix_wv,
           L0_mix_wo, L0_mix_bo, L0_mix_ln_k_g, L0_mix_ln_k_b, L0_mix_ln_v_g, L0_mix_ln_v_b, L0_ffn_Wg, L0_ffn_bg,
           L0_ffn_W1, L0_ffn_b1, L0_ffn_W2, L0_ffn_b2):
    import numpy as np
    import concourse.bacc as bacc
    from concourse.bass_utils import run_bass_kernel_spmd as run

    a = lambda v: np.ascontiguousarray(np.asarray(v))
    src_, dst_ = a(src), a(dst)
    arrays = {
        "x": np.pad(a(x), ((0, NP - N), (0, 0))),
        "src": np.pad(src_, (0, EP - E_REAL)),
        "dst": np.pad(dst_, (0, EP - E_REAL), constant_values=NP),
        "dst_next": np.pad(dst_[1:], (0, EP - E_REAL + 1), constant_values=NP),
        "gW": a(np.asarray(L0_gnn_W).transpose(1, 0, 2).reshape(D, D)),
        "gbW": a(L0_gnn_bW).reshape(-1),
        "gas": a(L0_gnn_a_src).reshape(-1),
        "gad": a(L0_gnn_a_dst).reshape(-1),
        "gab": a(L0_gnn_a_bias),
        "wkvT": a(np.concatenate([np.asarray(L0_mix_wk).T, np.asarray(L0_mix_wv).T], axis=1)),
        "wq": a(L0_mix_wq),
        "woT": a(np.asarray(L0_mix_wo).T),
        "bo": a(L0_mix_bo),
        "lng": a(np.concatenate([np.asarray(L0_mix_ln_k_g), np.asarray(L0_mix_ln_v_g)])),
        "lnb": a(np.concatenate([np.asarray(L0_mix_ln_k_b), np.asarray(L0_mix_ln_v_b)])),
        "Wg": a(L0_ffn_Wg),
        "bg": a(L0_ffn_bg),
        "W1": a(L0_ffn_W1).reshape(NE * D, HID),
        "b1": a(np.asarray(L0_ffn_b1).reshape(NE, FC, P).transpose(0, 2, 1)).reshape(NE * P, FC),
        "W2": a(L0_ffn_W2).reshape(NE * HID, D),
        "b2": a(L0_ffn_b2),
    }
    nc = bacc.Bacc("TRN2", target_bir_lowering=False, num_devices=1)
    args = [nc.dram_tensor(f"in_{n}", v.shape, mybir.dt.from_np(v.dtype), kind="ExternalInput").ap() for n, v in arrays.items()]
    out = nc.dram_tensor("out", (N, D), F32, kind="ExternalOutput").ap()
    gps_layer(nc, *args, out)
    r = run(nc, [{f"in_{n}": v for n, v in arrays.items()}], core_ids=[0])
    return r.results[0]["out"]
```

```python
from contextlib import ExitStack

import concourse.bass as bass
from concourse import mybir

F32 = mybir.dt.float32
BF16 = mybir.dt.bfloat16
I32 = mybir.dt.int32
ALU = mybir.AluOpType
ACT = mybir.ActivationFunctionType
AX = mybir.AxisListType
MAXOP = bass.bass_isa.ReduceOp.max

P = 128
N = 6250
D = 256
KD = D // P
NT = 50
NP = NT * P
NPAIR = NT // 2
H, DH = 8, 32
ROW = D + H
WCOL = D + 2 * H
MH, MD = 4, 64
E_REAL = 2 * 50000 + N
EC = 832
EP = EC * P
HC = 32
NHIST = EC // (2 * HC)
WIN = 24
SG = 2
NG = WIN // SG
WSTEP, WLEN = 16, 40
NWROW = (EP - WLEN) // WSTEP + 1
WT = 10
NBUCK = 64
BT = 512 // NBUCK
NE, HID = 8, 1024
XROW = D + NE + 1
NOWHERE = 1 << 20
SPLIT = 9
FC = HID // P
TT = 256
XT = 58
TAIL = N - (N // P) * P
TAIL_T = N // P
EPS = 1e-5
ALPHA = 0.2
LOW, LOWER = -1e29, -1e30
assert NPAIR * 2 == NT and E_REAL <= EP and EC == NHIST * 2 * HC and TAIL_T == NT - 2


class Chain:

    def __init__(self, eng, sem):
        self.eng, self.sem, self.base, self.n = eng, sem, 0, 0

    def step(self, ins):
        self.n += 1
        ins.then_inc(self.sem, 1)

    def wait(self, upto=None):
        self.eng.wait_ge(self.sem, self.base + (self.n if upto is None else upto))

    def link(self, ins):
        self.step(ins)
        self.wait()

    def at(self, base):
        self.base, self.n = base, 0


def gps_layer(nc, x, src, dst, dst_next, gW, gbW, gas, gad, gab, wkvT, wq, woT, bo, lng, lnb, lncol,
              Wg, bg, W1, b1, W2, b2, out):
    ctx = ExitStack()

    def sb(name, shape, dt=F32):
        return ctx.enter_context(nc.sbuf_tensor(name, shape, dt))

    def sem(name):
        return ctx.enter_context(nc.semaphore(name))

    def dram(name, shape, dt=F32):
        return nc.dram_tensor(name, shape, dt, kind="Internal").ap()

    with ctx:
        win_tab = dram("win_tab", (NWROW, WLEN), I32)
        next_tab = dram("next_tab", (NP + 1, 4), I32)
        src_tab = dram("src_tab", (EP, 1), I32)
        wh_tab = dram("wh_tab", (NP, ROW))
        s2_tab = dram("s2_tab", (NP, H))
        base_tab = dram("base_tab", (NP, D))
        ord_tab = dram("ord_tab", (NP, 4), I32)
        xs_tab = dram("xs_tab", (XT * TT, XROW))

        x_all = sb("x_all", [P, NT, D])
        xT_flat = sb("xT_flat", [P, NT * XROW])
        xT_all = xT_flat[:, 0:KD * NP].rearrange("p (k n) -> p k n", k=KD)
        xrow_all = xT_flat[:, :].rearrange("p (t c) -> p t c", t=NT)
        gath = sb("gath", [P, 2, WIN, ROW])
        g = gath[:, :, :, :].rearrange("p a k r -> p (a k r)")
        shared = sb("shared", [P, 2900])
        ident = sb("ident", [P, P])
        ltf = sb("ltf", [P, P])
        ltb = sb("ltb", [P, P], BF16)
        onesf = sb("onesf", [P, P])
        onesb = sb("onesb", [P, P], BF16)
        zeros = sb("zeros", [P, D])
        blank = sb("blank", [P, XROW])
        iota_f = sb("iota_f", [P, P])
        iota_i = sb("iota_i", [P, P], I32)
        node_i = sb("node_i", [P, NT], I32)
        abias = sb("abias", [P, H])
        bo_b = sb("bo_b", [P, D])
        mixw = sb("mixw", [P, KD, D])
        lngb = sb("lngb", [P, 2, 2, MD])
        kcol = sb("kcol", [P, 2])
        ksum = sb("ksum", [P, 2])
        wg_s = sb("wg_s", [P, KD, NE])
        bg_b = sb("bg_b", [P, NE])
        ordn = sb("ordn", [P, NT, 4], I32)
        deg = sb("deg", [P, NT])
        rowp = sb("rowp", [P, NT])
        small = sb("small", [P, 4, NT])
        ranki = sb("ranki", [P, NT], I32)
        mxrem = sb("mxrem", [P, NT])
        winr = sb("winr", [P, NT], I32)
        starti = sb("starti", [P, NT], I32)
        bits = sb("bits", [P, 4, NT], I32)
        groups = sb("groups", [P, NT], I32)
        ctl = sb("ctl", [P, 5], I32)
        ctlf = sb("ctlf", [P, 9])
        gmask = sb("gmask", [P, NT])
        gcumf = sb("gcumf", [P, 2, NPAIR])
        gbase = sb("gbase", [P, 2, NPAIR], I32)
        slots = sb("slots", [P, NT], I32)
        scumf = sb("scumf", [P, 2, NPAIR])
        scum = sb("scum", [P, 2, NPAIR], I32)
        nextra = sb("nextra", [P, 1], I32)
        vare = sb("vare", [P, 2])
        idx = sb("idx", [P, NT + 2, WIN], I32)
        idx_x = sb("idx_x", [P, NT + 2, WIN], I32)
        idxs = sb("idxs", [P, 2, WIN], I32)
        basei = sb("basei", [P, 2], I32)
        fallf = sb("fallf", [P, 2])
        falls = sb("falls", [P, 1], I32)
        meta = sb("meta", [P, 2, NE + 1])
        metao = sb("metao", [P, 2, NE + 1])
        m_all = sb("m_all", [P, NT, H])
        den_all = sb("den_all", [P, NT, H])
        s2_all = sb("s2_all", [P, NT, H])
        stats = sb("stats", [P, 2, 6])
        mv = sb("mv", [P, 2, 2])
        rs = sb("rs", [P, 2, 2])
        kvr = sb("kvr", [P, 2, 2, 8])
        ez = sb("ez", [P, WIN, H])
        pen = sb("pen", [P, WIN])
        es = sb("es", [P, 6, H])
        accf = sb("accf", [P, D])
        wts = sb("wts", [P, 2, NT])
        slotf = sb("slotf", [P, 2, NT])
        sloti = sb("sloti", [P, 2, NT], I32)
        valid = sb("valid", [P, NT])
        cnt = sb("cnt", [P, 4, NE])
        cnti = sb("cnti", [P, NE], I32)
        ebnd = sb("ebnd", [P, 2, NE], I32)

        def carve(area, spans):
            at, parts = spans["start"], []
            for n in spans["sizes"]:
                parts.append(area[:, at:at + n])
                at += n
            assert at <= area.shape[1], at
            return parts

        gb = g.bitcast(BF16)
        oh_b = gb[:, 0:2 * HC * P].rearrange("p (a j c) -> p a j c", a=2, j=HC)
        oh_a = gb[:, 2 * HC * P:2 * HC * (P + NT)].rearrange("p (a j c) -> p a j c", a=2, j=HC)
        oh_d = gb[:, 0:NT * NBUCK].rearrange("p (t c) -> p t c", t=NT)
        r_in, = carve(g, dict(start=1600, sizes=[NT * NBUCK]))
        r_cnt, r_scan = carve(xT_flat, dict(start=0, sizes=[NT * NBUCK] * 2))
        srcc_, dstc_, key_b, key_eq, key_lt, key_, place_ = carve(g, dict(start=0, sizes=[EC, EC, P, P, P, 5, 8]))
        srcc, dstc = srcc_.bitcast(I32), dstc_.bitcast(I32)
        keyf, total, later, placef = key_[:, 0:1], key_[:, 1:2], key_[:, 2:3], key_[:, 3:5]
        key, edge_src, place, cur = [place_[:, i:j].bitcast(I32) for i, j in ((0, 1), (1, 2), (2, 3), (3, 7))]
        curf = place_[:, 7:8]
        dnext, dfall = [xT_flat[:, i * EC:(i + 1) * EC] for i in range(2)]
        dnext = dnext.bitcast(I32)
        wina, winb = [a.bitcast(I32).rearrange("p (t w) -> p t w", t=NT)
                      for a in carve(g, dict(start=0, sizes=[NT * WLEN] * 2))]
        xn, xTs, whs, kvs, kvq = carve(g, dict(start=4000, sizes=[2 * D, 2 * D, 2 * WCOL, 4 * D, 4 * D]))
        xn = xn.rearrange("p (b d) -> p b d", b=2)
        xTs = xTs.rearrange("p (k n) -> p k n", k=KD)
        whs = whs.rearrange("p (b c) -> p b c", b=2)
        kvs = kvs.rearrange("p (b c) -> p b c", b=2)
        kvq = kvq.rearrange("p (b c) -> p b c", b=2)
        wkv_, avec_, wcat_, bias1 = carve(g, dict(start=7616, sizes=[KD * 2 * D, 3 * D, KD * WCOL, WCOL]))
        wkv = wkv_.rearrange("p (k c) -> p k c", k=KD)
        avec = avec_.rearrange("p (a c) -> p a c", a=3)
        wcat = wcat_.rearrange("p (k c) -> p k c", k=KD)
        bcol, acol = [a.bitcast(I32) for a in carve(g, dict(start=10480, sizes=[EC, EC]))]
        wq_s, wo_s, kvd, t1, base_s, mxs = carve(shared, dict(start=0, sizes=[2 * D, 2 * D, 2 * P, 2 * D, 2 * D, 2 * D]))
        mxs = mxs.rearrange("p (k n) -> p k n", k=KD)
        wq_s = wq_s.rearrange("p (k c) -> p k c", k=2)
        wo_s = wo_s.rearrange("p (k c) -> p k c", k=2)
        kvd = kvd.rearrange("p (k c) -> p k c", k=2)
        t1 = t1.rearrange("p (k c) -> p k c", k=2)
        base_s = base_s.rearrange("p (b c) -> p b c", b=2)
        msk, pos, m01_ = carve(shared, dict(start=0, sizes=[2 * NT * NE, NT * NE, NT * NE // 2]))
        logit = sb("logit", [P, NT, NE])[:, :, :]
        baseg = sb("baseg", [P, 2, D])[:, :, :]
        xn2s = sb("xn2s", [P, 2, D])[:, :, :]
        xTr = sb("xTr", [P, KD, 2 * P])[:, :, :]
        msk = msk.rearrange("p (j t e) -> p j t e", j=2, t=NT)
        pos = pos.rearrange("p (t e) -> p t e", t=NT)
        m01 = m01_.bitcast(BF16)
        cmp8, cmp8b, tri8, tsc, tex = carve(g, dict(start=0, sizes=[NT * 64, NT * 64, 64, NT * NE, NT * NE]))
        cmp8 = cmp8.rearrange("p (t a b) -> p t a b", t=NT, a=NE)
        cmp8b = cmp8b.rearrange("p (t a b) -> p t a b", t=NT, a=NE)
        tri8 = tri8.rearrange("p (a b) -> p a b", a=NE)
        tsc3 = tsc.rearrange("p (e t) -> p e t", e=NE)
        tex3 = tex.rearrange("p (e t) -> p e t", e=NE)
        w1s, w2s, b1s, b2s, xs_s, xTe, hT = carve(
            g, dict(start=0, sizes=[2 * KD * HID, 2 * FC * D, 2 * FC, 2 * D, 2 * XROW, 2 * KD * TT, FC * TT]))
        w1s = w1s.rearrange("p (s k f) -> p s k f", s=2, k=KD)
        w2s = w2s.rearrange("p (s c n) -> p s c n", s=2, c=FC)
        b1s = b1s.rearrange("p (s c) -> p s c", s=2)
        b2s = b2s.rearrange("p (s n) -> p s n", s=2)
        xs_s = xs_s.rearrange("p (a d) -> p a d", a=2)
        xTe = xTe.rearrange("p (b k n) -> p b k n", b=2, k=KD)
        hT = hT.rearrange("p (c n) -> p c n", c=FC)
        ysb = shared[:, 0:2 * D].rearrange("p (a d) -> p a d", a=2)

        bank = [ctx.enter_context(nc.psum_tensor(f"bank{i}", [P, 512], F32)) for i in range(8)]

        S = {}
        for name in """consts pool_step dve_step dve_end passed weights_in edges_in
            order_seen order_red order_known sort_in next_in sort_step sort_free sort_key sort_ps cur_in sort_placed sort_sent sorted
            hist_oh hist_used deg_ready rowp_ps ohd_ready cnt_ps cnt_used rank_ready ord_stored ord_in win_done
            mx_ready mx_done whs_free bases_free var_ready rstd_ready xn_ready tp_ready xT_ready wh_ps wh_ready
            s2_in kv_ps sq_ready kvar_ready krs_ready kn_ready kv_done kvd_ready t1_ps t1_ready
            mix_ps mix_ready mw_in mxs_ready base_ps base_copied base_ready tables_ready lwin_ready lwin_in idx_step
            x_ready x_win_in x_idx_ready x_pass x_done l_ready basei_ready g_blank slots_filled
            y_step lg_done lg_copied v2_ready r2_ready xn2_ready xn2_copied tp2_ready xTr_ready lg_ps x1_sent
            m01_ready pre_ps gap_ready gexp_ready slot_ready bounds_ready xs_blank xs_done xs_in xte_ps xte_ready
            h_ps h_ready y_ps y_ready ys_done ys_free""".split():
            S[name] = sem(name)
        for pass_ in ("x", "l"):
            for name in "f_in ex_in f_ready ex_ready accf_ready acc_ps unit".split():
                S[pass_, name] = sem(f"{pass_}_{name}")
            for name in "idxs_ready gath_in prod".split():
                S[pass_, name] = [sem(f"{pass_}_{name}_a"), sem(f"{pass_}_{name}_b")]
        for name in """wh_stored base_stored baseg_in ew_in ew_used""".split():
            S[name] = [sem(name + "_a"), sem(name + "_b")]

        def apart(eng):
            eng.sem_inc(S["passed"], 1)

        block = ctx.enter_context(nc.Block())
        NLOAD = 16
        unit_bound = NPAIR * (EP // WIN)

        @block.sync
        def _(sp):
            sp.dma_start(bcol, dst.rearrange("(p j) -> p j", j=EC)).then_inc(S["edges_in"], 16)
            sp.dma_start(dnext, dst_next.rearrange("(p j) -> p j", j=EC)).then_inc(S["edges_in"], 16)
            w = lambda o, i: sp.dma_start(o, i).then_inc(S["weights_in"], 16)
            w(wcat[:, :, 0:D], gW.rearrange("(k p) c -> p k c", p=P))
            w(avec[:, 0, :], gas.partition_broadcast(P))
            w(avec[:, 1, :], gad.partition_broadcast(P))
            w(avec[:, 2, :], gbW.partition_broadcast(P))
            w(abias[:, :], gab.partition_broadcast(P))
            w(wkv, wkvT.rearrange("(k p) c -> p k c", p=P))
            w(bo_b[:, :], bo.partition_broadcast(P))
            w(lngb[:, 0, :, :].rearrange("p s d -> p (s d)"), lng.partition_broadcast(P))
            w(lngb[:, 1, :, :].rearrange("p s d -> p (s d)"), lnb.partition_broadcast(P))
            w(kcol[:, :], lncol)
            w(wg_s[:, :, :], Wg.rearrange("(k p) c -> p k c", p=P))
            w(bg_b[:, :], bg.partition_broadcast(P))
            for i in range(4):
                lo, hi = NT * i // 4, NT * (i + 1) // 4
                w(x_all[:, lo:hi, :], x[lo * P:hi * P, :].rearrange("(t p) d -> p t d", p=P))
            sp.dma_start(win_tab, bass.AP(src.tensor, 0, [[WSTEP, NWROW], [1, WLEN]])).then_inc(S["win_done"], 16)
            sp.dma_start(wq_s, wq.rearrange("(k p) c -> p k c", p=P)).then_inc(S["mw_in"], 16)
            sp.dma_start(wo_s, woT.rearrange("(k p) c -> p k c", p=P)).then_inc(S["mw_in"], 16)
            sp.wait_ge(S["consts"], 1)
            for i in range(XT // 2):
                sp.dma_start(xs_tab[i * 2 * TT:(i + 1) * 2 * TT, :].rearrange("(a p) c -> p a c", p=P),
                             blank[:, :].unsqueeze(1).to_broadcast([P, 2 * TT // P, XROW])).then_inc(S["xs_blank"], 16)
            sp.wait_ge(S["order_known"], 1)
            unsorted = sp.value_load(falls[0:1, 0:1], min_val=0, max_val=1)
            with sp.If(unsorted > 0):
                sp.dma_start(srcc, src.rearrange("(p j) -> p j", j=EC)).then_inc(S["sort_in"], 16)
                sp.dma_start(dstc, dst.rearrange("(p j) -> p j", j=EC)).then_inc(S["sort_in"], 16)
                sp.dma_start(next_tab[0:NP, :].rearrange("(t p) c -> p t c", p=P), ordn[:, :, :]).then_inc(S["next_in"], 16)
                sp.dma_start(next_tab[NP:NP + 1, :], winr[0:1, 0:4]).then_inc(S["next_in"], 16)
                sp.wait_ge(S["win_done"], 16)
                sp.wait_ge(S["sorted"], 1)
                sp.dma_start(win_tab, bass.AP(src_tab.tensor, 0, [[WSTEP, NWROW], [1, WLEN]])).then_inc(S["win_done"], 16)
            sp.sem_inc(S["whs_free"], 1)
            with sp.Fori(0, NPAIR) as i:
                sp.wait_ge(S["wh_ready"], i + 1)
                for b in range(2):
                    sp.dma_start(wh_tab[bass.ds(i * (2 * P) + b * P, P), :], whs[:, b, 0:ROW]).then_inc(S["wh_stored"][b], 16)
                    sp.dma_start(s2_tab[bass.ds(i * (2 * P) + b * P, P), :], whs[:, b, ROW:WCOL]).then_inc(S["wh_stored"][b], 16)
                for b in range(2):
                    sp.wait_ge(S["wh_stored"][b], i * 32 + 32)
                sp.sem_inc(S["whs_free"], 1)
            sp.sem_inc(S["bases_free"], 1)
            with sp.Fori(0, NPAIR) as i:
                sp.wait_ge(S["base_ready"], i + 1)
                for b in range(2):
                    sp.dma_start(base_tab[bass.ds(i * (2 * P) + b * P, P), :], base_s[:, b, :]).then_inc(S["base_stored"][b], 16)
                for b in range(2):
                    sp.wait_ge(S["base_stored"][b], i * 16 + 16)
                sp.sem_inc(S["bases_free"], 1)
            sp.wait_ge(S["bounds_ready"], 1)
            sp.wait_ge(S["slots_filled"], 1)
            ntile = sp.value_load(ebnd[0:1, 1, NE - 1:NE], min_val=1, max_val=XT - 1)
            sp.dma_start(xs_s, xs_tab[0:TT, :].rearrange("(a p) c -> p a c", p=P)).then_inc(S["xs_in"], 16)
            with sp.Fori(0, ntile) as i:
                sp.wait_ge(S["xte_ready"], i + 1)
                sp.dma_start(xs_s, xs_tab[bass.ds(i * TT + TT, TT), :].rearrange("(a p) c -> p a c", p=P)).then_inc(S["xs_in"], 16)

        @block.gpsimd
        def _(pool):
            def gather(o, table, index):
                return pool.indirect_dma_start(out=o, out_offset=None, in_=table,
                                               in_offset=bass.IndirectOffsetOnAxis(ap=index, axis=0))

            def scatter(table, index, i, **more):
                return pool.indirect_dma_start(out=table, out_offset=bass.IndirectOffsetOnAxis(ap=index, axis=0),
                                               in_=i, in_offset=None, **more)

            pc = Chain(pool, S["pool_step"])
            pc.step(pool.memset(ident[:, :], 0.0))
            pc.step(pool.memset(ltf[:, :], 1.0))
            pc.step(pool.memset(onesf[:, :], 1.0))
            pc.step(pool.memset(onesb[:, :], 1.0))
            pc.step(pool.memset(zeros[:, :], 0.0))
            pc.step(pool.memset(blank[:, 0:XROW - 1], 0.0))
            pc.step(pool.memset(blank[:, XROW - 1:XROW].bitcast(I32), NOWHERE))
            pc.step(pool.iota(iota_i[:, :], pattern=[[1, P]], base=0, channel_multiplier=0))
            pc.link(pool.iota(node_i[:, :], pattern=[[P, NT]], base=0, channel_multiplier=1))
            pc.step(pool.affine_select(out=ident[:, :], in_=ident[:, :], compare_op=ALU.not_equal, fill=1.0,
                                       base=0, pattern=[[-1, P]], channel_multiplier=1))
            pc.step(pool.affine_select(out=ltf[:, :], in_=ltf[:, :], compare_op=ALU.is_gt, fill=0.0,
                                       base=0, pattern=[[1, P]], channel_multiplier=-1))
            pc.link(pool.tensor_copy(iota_f[:, :], iota_i[:, :]))
            pool.tensor_copy(ltb[:, :], ltf[:, :]).then_inc(S["consts"], 1)

            pool.wait_ge(S["order_seen"], 1)
            pool.partition_all_reduce(fallf[:, 1:2], fallf[:, 0:1], P, MAXOP).then_inc(S["order_red"], 1)
            pool.wait_ge(S["order_known"], 1)
            unsorted = pool.value_load(falls[0:1, 0:1], min_val=0, max_val=1)
            with pool.If(unsorted > 0):
                pool.wait_ge(S["next_in"], 32)
                pool.sem_inc(S["sort_free"], 1)
                with pool.Fori(0, EC) as j:
                    pool.wait_ge(S["sort_key"], j + 1)
                    apart(pool)
                    gather(cur, next_tab, key).then_inc(S["cur_in"], 16)
                    pool.wait_ge(S["sort_placed"], j + 1)
                    apart(pool)
                    scatter(next_tab, key, cur).then_inc(S["sort_sent"], 16)
                    scatter(src_tab, place, edge_src).then_inc(S["sort_sent"], 16)
                    pool.wait_ge(S["sort_sent"], j * 32 + 32)
                    pool.sem_inc(S["sort_free"], 1)
                pool.sem_inc(S["sorted"], 1)

            pool.wait_ge(S["rank_ready"], 1)
            for t in range(NT):
                scatter(ord_tab, ranki[:, t:t + 1], ordn[:, t, :]).then_inc(S["ord_stored"], 16)

            pool.wait_ge(S["ord_stored"], 16 * NT)
            pool.dma_start(ordn[:, :, :], ord_tab.rearrange("(t p) c -> p t c", p=P)).then_inc(S["ord_in"], 16)
            pool.wait_ge(S["mx_ready"], 1)
            pool.partition_all_reduce(mxrem[:, :], deg[:, :], P, MAXOP).then_inc(S["mx_done"], 1)


            def rows(p, i, b):
                n = pool.value_load(slots[0:1, bass.ds(i * 2 + b, 1)], min_val=1, max_val=WIN)
                for k in range(WIN):
                    with pool.If(n > k):
                        gather(gath[:, b, k, :], wh_tab, idxs[:, b, k:k + 1]).then_inc(S[p, "gath_in"][b], 16)

            pool.wait_ge(S["tables_ready"], 1)
            pool.wait_ge(S["kv_done"], NPAIR + 2)
            pool.wait_ge(S["kn_ready"], NT)
            for b in range(2):
                pool.wait_ge(S["wh_stored"][b], 32 * NPAIR)
            pool.memset(g, 0.0).then_inc(S["g_blank"], 1)
            pool.wait_ge(S["g_blank"], 1)
            with pool.If(unsorted > 0):
                pool.wait_ge(S["win_done"], 32)
                apart(pool)
            pool.wait_ge(S["win_done"], 16)
            pool.wait_ge(S["lwin_ready"], 1)
            for t in range(NT):
                gather(wina[:, t, :], win_tab, winr[:, t:t + 1]).then_inc(S["lwin_in"], 16)
            for t in range(NT):
                gather(s2_all[:, t, :], s2_tab, ordn[:, t, 0:1]).then_inc(S["s2_in"], 16)
            nx = pool.value_load(nextra[0:1, 0:1], min_val=0, max_val=EP // WIN)
            with pool.If(nx > 0):
                with pool.Fori(0, nx) as w:
                    pool.wait_ge(S["x_ready"], w + 1)
                    apart(pool)
                    lo = pool.value_load(ctl[0:1, 0:1], min_val=0, max_val=unit_bound)
                    npr = pool.value_load(ctl[0:1, 3:4], min_val=1, max_val=NPAIR)
                    ngr = pool.value_load(ctl[0:1, 2:3], min_val=1, max_val=NT // WT)
                    for gr in range(NT // WT):
                        with pool.If(ngr > gr):
                            for t in range(gr * WT, (gr + 1) * WT):
                                gather(wina[:, t, :], win_tab, winr[:, t:t + 1]).then_inc(S["x_win_in"], 16)
                    pool.wait_ge(S["x_idx_ready"], w + 1)
                    apart(pool)
                    with pool.Fori(0, npr) as i:
                        for b in range(2):
                            pool.wait_ge(S["x", "idxs_ready"][b], i + lo + 1)
                            rows("x", i, b)
                    pool.wait_ge(S["x_done"], w + 1)
                    apart(pool)
            pool.wait_ge(S["l_ready"], 1)
            for b in range(2):
                pool.wait_ge(S["base_stored"][b], 16 * NPAIR)
            with pool.Fori(0, NPAIR) as i:
                for b in range(2):
                    pool.wait_ge(S["l", "idxs_ready"][b], i + 1)
                    rows("l", i, b)
                pool.wait_ge(S["basei_ready"], i + 1)
                apart(pool)
                for b in range(2):
                    gather(baseg[:, b, :], base_tab, basei[:, b:b + 1]).then_inc(S["baseg_in"][b], 16)

            def x1_out(lo, hi):
                for t in range(lo, hi):
                    scatter(out, ordn[:, t, 0:1], x_all[:, t, :], bounds_check=N - 1, oob_is_err=False).then_inc(S["x1_sent"], 16)

            pool.wait_ge(S["lg_done"], 1)
            x1_out(0, NT // 3)
            pool.wait_ge(S["slot_ready"], 1)
            pool.wait_ge(S["xs_blank"], 16 * (XT // 2))
            for t in range(NT):
                for j in range(2):
                    scatter(xs_tab, sloti[:, j, t:t + 1], xrow_all[:, t, :],
                            bounds_check=XT * TT - 1, oob_is_err=False).then_inc(S["xs_done"], 16)
            pool.wait_ge(S["xs_done"], 16 * 2 * NT)
            ntile = pool.value_load(ebnd[0:1, 1, NE - 1:NE], min_val=1, max_val=XT - 1)
            pool.sem_inc(S["ys_free"], 1)
            pool.sem_inc(S["slots_filled"], 1)
            x1_out(NT // 3, NT)
            pool.wait_ge(S["x1_sent"], 16 * NT)
            with pool.Fori(0, ntile) as i:
                pool.wait_ge(S["y_ready"], i + 2)
                apart(pool)
                for a in range(2):
                    scatter(out, metao[:, a, NE:NE + 1].bitcast(I32), ysb[:, a, :], bounds_check=N - 1, oob_is_err=False,
                            compute_op=ALU.add).then_inc(S["ys_done"], 16)
                pool.wait_ge(S["ys_done"], i * 32 + 32)
                pool.sem_inc(S["ys_free"], 1)

        @block.scalar
        def _(act):
            def root(o, i, ready):
                nc.scalar.activation(o, i, ACT.Sqrt).then_inc(ready, 1)

            act.wait_ge(S["var_ready"], 1)
            root(rs[:, :, 1], rs[:, :, 0], S["rstd_ready"])

            def evacuate(i, first=False):
                act.wait_ge(S["tp_ready"], i + 1)
                if not first:
                    act.wait_ge(S["kv_ps"], i * 2)
                pair = bank[5][:, :].rearrange("p (k n) -> p k n", k=KD)
                nc.scalar.copy(xTs, pair).then_inc(S["xT_ready"], 1)
                nc.scalar.copy(xT_all[:, :, bass.ds(i * (2 * P), 2 * P)], pair).then_inc(S["xT_ready"], 1)

            def spreads(i, more=True):
                for b in range(2):
                    act.wait_ge(S["kv_ps"], i * 2 + (b + 1))
                    nc.scalar.activation(kvq[:, b, :], bank[2 + b][:, :], ACT.Square).then_inc(S["sq_ready"], 1)
                if more:
                    act.wait_ge(S["var_ready"], i + 2)
                    root(rs[:, :, 1], rs[:, :, 0], S["rstd_ready"])
                act.wait_ge(S["kvar_ready"], i + 1)
                root(kvr[:, 1, :, :], kvr[:, 0, :, :], S["krs_ready"])

            evacuate(0, True)
            spreads(0)
            with act.Fori(1, NPAIR - 1) as i:
                evacuate(i)
                spreads(i)
            evacuate(NPAIR - 1)
            spreads(NPAIR - 1, False)

            with act.Fori(0, NPAIR) as i:
                act.wait_ge(S["base_ps"], i + 1)
                nc.scalar.copy(mxs, xT_all[:, :, bass.ds(i * (2 * P), 2 * P)]).then_inc(S["mxs_ready"], 1)

            def exponentials(p, u, b):
                act.wait_ge(S[p, "f_in"], u * 2 + (b + 1))
                nc.scalar.activation(es[:, 3, :], es[:, 2, :], ACT.Exp).then_inc(S[p, "f_ready"], 1)
                act.wait_ge(S[p, "ex_in"], u * 2 + (b + 1))
                nc.scalar.activation(ez[:, :, :], ez[:, :, :], ACT.Exp).then_inc(S[p, "ex_ready"], 1)

            act.wait_ge(S["tables_ready"], 1)
            nx = act.value_load(nextra[0:1, 0:1], min_val=0, max_val=EP // WIN)
            with act.If(nx > 0):
                with act.Fori(0, nx) as w:
                    act.wait_ge(S["x_ready"], w + 1)
                    apart(act)
                    lo = act.value_load(ctl[0:1, 0:1], min_val=0, max_val=unit_bound)
                    npr = act.value_load(ctl[0:1, 3:4], min_val=1, max_val=NPAIR)
                    with act.Fori(0, npr) as i:
                        for b in range(2):
                            exponentials("x", i + lo, b)
                    act.wait_ge(S["x_done"], w + 1)
                    apart(act)
            act.wait_ge(S["l_ready"], 1)
            act.sem_inc(S["lg_copied"], 1)

            def x1_root(i):
                act.wait_ge(S["v2_ready"], i + 1)
                root(rs[:, :, 1], rs[:, :, 0], S["r2_ready"])

            def x1_out(i):
                act.wait_ge(S["xn2_ready"], i + 1)
                nc.scalar.copy(xrow_all[:, bass.ds(i * 2, 2), 0:D], xn2s).then_inc(S["xn2_copied"], 1)
                act.wait_ge(S["tp2_ready"], i + 1)
                nc.scalar.copy(xTr, bank[5][:, :].rearrange("p (k n) -> p k n", k=KD)).then_inc(S["xTr_ready"], 1)
                act.wait_ge(S["xn2_copied"], i + 1)
                act.wait_ge(S["lg_ps"], i + 1)
                nc.scalar.copy(logit[:, bass.ds(i * 2, 2), :], bank[6][:, 0:2 * NE].rearrange("p (b e) -> p b e", b=2)
                               ).then_inc(S["lg_copied"], 1)

            for b in range(2):
                exponentials("l", 0, b)
            with act.Fori(1, NPAIR) as i:
                exponentials("l", i, 0)
                x1_root(i - 1)
                exponentials("l", i, 1)
                x1_out(i - 1)
            x1_root(NPAIR - 1)
            x1_out(NPAIR - 1)
            act.wait_ge(S["gap_ready"], 1)
            nc.scalar.activation(small[:, 3, :], small[:, 2, :], ACT.Exp).then_inc(S["gexp_ready"], 1)

            def weights(e, s):
                ew = lambda o, i: act.dma_start(o, i).then_inc(S["ew_in"][s], 16)
                ew(w1s[:, s, :, :], W1[bass.ds(e * D, D), :].rearrange("(k p) f -> p k f", p=P))
                ew(w2s[:, s, :, :], W2[bass.ds(e * HID, HID), :].rearrange("(c p) n -> p c n", p=P))
                ew(b1s[:, s, :], b1[bass.ds(e * P, P), :])
                ew(b2s[:, s, :], b2[bass.ds(e, 1), :].to_broadcast([P, D]))

            act.sem_inc(S["h_ready"], 4)
            act.wait_ge(S["slot_ready"], 1)
            weights(0, 0)
            weights(1, 1)

            def expert(ep, s):
                lo = act.value_load(ebnd[0:1, 0, bass.ds(ep * 2 + s, 1)], min_val=0, max_val=XT - 2)
                hi = act.value_load(ebnd[0:1, 1, bass.ds(ep * 2 + s, 1)], min_val=1, max_val=XT - 1)
                act.wait_ge(S["ew_in"][s], ep * 64 + 64)
                with act.Fori(lo, hi) as i:
                    for c in range(FC):
                        act.wait_ge(S["h_ps"], i * FC + (c + 1))
                        nc.scalar.activation(hT[:, c, :], bank[c % 4][:, 0:TT], ACT.Gelu,
                                             bias=b1s[:, s, c:c + 1]).then_inc(S["h_ready"], 1)

            with act.Fori(0, NE // 2 - 1) as ep:
                for s in range(2):
                    expert(ep, s)
                    act.wait_ge(S["ew_used"][s], ep + 1)
                    weights(ep * 2 + (2 + s), s)
            for s in range(2):
                expert(NE // 2 - 1, s)

        @block.vector
        def _(v):
            ch = Chain(v, S["dve_step"])
            tt, ts, copy = nc.vector.tensor_tensor, nc.vector.tensor_scalar, nc.vector.tensor_copy
            scan, reduce = nc.vector.tensor_tensor_scan, nc.vector.tensor_reduce

            def inner_sum(o, i):
                return reduce(o, i, AX.X, ALU.add)

            v.wait_ge(S["edges_in"], 32)
            ch.link(tt(dfall, bcol, dnext, ALU.is_gt))
            ch.link(reduce(fallf[:, 0:1], dfall, AX.X, ALU.max))
            v.sem_inc(S["order_seen"], 1)
            v.wait_ge(S["consts"], 1)
            ch.link(ts(acol, bcol, 7, None, ALU.arith_shift_right))
            ch.link(ts(bcol, bcol, P - 1, None, ALU.bitwise_and))
            with v.Fori(0, NHIST) as i:
                for a in range(2):
                    v.wait_ge(S["hist_used"], i * 2 + (a + 1))
                    cols = bass.ds(i * (2 * HC) + a * HC, HC)
                    tt(oh_b[:, a], bcol[:, cols].unsqueeze(2).to_broadcast([P, HC, P]),
                       iota_i[:, :].unsqueeze(1).to_broadcast([P, HC, P]), ALU.is_equal)
                    tt(oh_a[:, a], acol[:, cols].unsqueeze(2).to_broadcast([P, HC, NT]),
                       iota_i[:, 0:NT].unsqueeze(1).to_broadcast([P, HC, NT]), ALU.is_equal).then_inc(S["hist_oh"], 1)
            v.wait_ge(S["hist_used"], 2 * NHIST + 3)
            ch.link(copy(deg[:, :], bank[0][:, 0:NT]))
            v.sem_inc(S["deg_ready"], 1)

            v.wait_ge(S["rowp_ps"], 1)
            ch.link(scan(small[:, 0, :], onesf[:, 0:NT], bank[1][:, 64:64 + NT], 0.0, ALU.mult, ALU.add))
            ch.link(tt(small[:, 1, :], small[:, 0, :], bank[1][:, 64:64 + NT], ALU.subtract))
            ch.link(tt(rowp[:, :], small[:, 1, :], bank[1][:, 0:NT], ALU.add))

            v.wait_ge(S["order_red"], 1)
            ch.step(copy(falls[:, :], fallf[:, 1:2]))
            ch.step(copy(ordn[:, :, 0], node_i[:, :]))
            ch.step(copy(ordn[:, :, 1], rowp[:, :]))
            ch.step(copy(ordn[:, :, 2], deg[:, :]))
            ch.step(nc.vector.memset(ordn[:, :, 3], 0))
            ch.step(nc.vector.memset(winr[:, 0:4], E_REAL))
            ch.wait()
            v.sem_inc(S["order_known"], 1)
            unsorted = v.value_load(falls[0:1, 0:1], min_val=0, max_val=1)
            with v.If(unsorted > 0):
                cs, per = Chain(v, S["sort_step"]), 13
                v.wait_ge(S["sort_in"], 32)
                with v.Fori(0, EC) as j:
                    cs.at(j * per)
                    v.wait_ge(S["sort_free"], j + 1)
                    cs.step(copy(key, dstc[:, bass.ds(j, 1)]))
                    cs.step(copy(edge_src, srcc[:, bass.ds(j, 1)]))
                    cs.step(copy(keyf, dstc[:, bass.ds(j, 1)]))
                    cs.step(copy(key_b, dstc[:, bass.ds(j, 1)].to_broadcast([P, P])))
                    cs.wait()
                    v.sem_inc(S["sort_key"], 1)
                    v.wait_ge(S["sort_ps"], j + 1)
                    cs.link(ts(key_eq, bank[2][:, 0:P], keyf, None, ALU.is_equal))
                    cs.step(inner_sum(total, key_eq))
                    cs.link(tt(key_lt, key_eq, ltf[:, :], ALU.mult))
                    cs.link(inner_sum(later, key_lt))
                    v.wait_ge(S["cur_in"], j * 16 + 16)
                    cs.link(copy(curf, cur[:, 1:2]))
                    cs.step(tt(placef[:, 0:1], curf, later, ALU.add))
                    cs.step(tt(placef[:, 1:2], curf, total, ALU.add))
                    cs.wait()
                    cs.step(copy(place, placef[:, 0:1]))
                    cs.step(copy(cur[:, 1:2], placef[:, 1:2]))
                    cs.wait()
                    v.sem_inc(S["sort_placed"], 1)
                    assert cs.n == per, cs.n
                v.wait_ge(S["sort_free"], EC + 1)
                apart(v)

            ch.link(ts(small[:, 2, :], deg[:, :], float(NBUCK - 1), -1.0, ALU.min, ALU.mult))
            ch.link(ts(small[:, 3, :], small[:, 2, :], float(NBUCK - 1), None, ALU.add))
            ch.link(tt(oh_d, small[:, 3, :].unsqueeze(2).to_broadcast([P, NT, NBUCK]),
                       iota_f[:, 0:NBUCK].unsqueeze(1).to_broadcast([P, NT, NBUCK]), ALU.is_equal))
            v.sem_inc(S["ohd_ready"], 1)
            rin = r_in.rearrange("p (t c) -> p t c", t=NT)
            rc = r_cnt.rearrange("p (c t) -> p c t", t=NT)
            rsc = r_scan.rearrange("p (c t) -> p c t", t=NT)
            for n, lo in enumerate(range(0, NT, BT)):
                k = min(BT, NT - lo)
                v.wait_ge(S["cnt_ps"], n + 1)
                bk = 2 + 2 * (n % 2)
                ch.step(copy(rin[:, lo:lo + k, :], bank[bk][:, 0:k * NBUCK].rearrange("p (t c) -> p t c", t=k)))
                ch.step(copy(rc[:, :, lo:lo + k], bank[bk + 1][:, 0:k * NBUCK].rearrange("p (t c) -> p c t", t=k)))
                ch.wait()
                v.sem_inc(S["cnt_used"], 1)
            ch.link(scan(r_scan, onesf[:, 0:1].to_broadcast([P, NT * NBUCK]), r_cnt, 0.0, ALU.mult, ALU.add))
            ch.link(tt(r_scan, r_scan, r_cnt, ALU.subtract))
            ch.link(tt(rin, rin, rsc.rearrange("p c t -> p t c"), ALU.add))
            ch.link(tt(rin, rin, oh_d, ALU.mult))
            ch.link(inner_sum(small[:, 2, :], rin))
            ch.step(copy(ranki[:, :], small[:, 2, :]))
            ch.wait()
            v.sem_inc(S["rank_ready"], 1)

            v.wait_ge(S["weights_in"], 16 * NLOAD)
            for s in range(2):
                tmp = kvq[:, :, s * D:(s + 1) * D]
                ch.link(tt(tmp, wcat[:, :, 0:D], avec[:, s, :].unsqueeze(1).to_broadcast([P, KD, D]), ALU.mult))
                ch.step(inner_sum(wcat[:, :, D + s * H:D + (s + 1) * H], tmp.rearrange("p k (h d) -> p k h d", h=H)))
                ch.link(tt(whs[:, s, 0:D], avec[:, 2, :], avec[:, s, :], ALU.mult))
                ch.step(inner_sum(bias1[:, D + s * H:D + (s + 1) * H], whs[:, s, 0:D].rearrange("p (h d) -> p h d", h=H)))
            ch.step(copy(bias1[:, 0:D], avec[:, 2, :]))
            ch.wait()
            ch.link(tt(bias1[:, D + H:WCOL], bias1[:, D + H:WCOL], abias[:, :], ALU.add))
            wk4 = wkv.rearrange("p k (h d) -> p k h d", d=MD)
            ch.link(inner_sum(kvr[:, 0, :, :], wk4))
            ch.link(ts(kvr[:, 1, :, :], kvr[:, 0, :, :], -1.0 / MD, None, ALU.mult))
            for k in range(KD):
                ch.step(tt(wk4[:, k], wk4[:, k], kvr[:, 1, k, :].unsqueeze(2).to_broadcast([P, 8, MD]), ALU.add))
            ch.wait()

            def x_rows(i):
                return lambda b: x_all[:, bass.ds(i * 2 + b, 1), :].rearrange("p o d -> p (o d)")

            def first_phase(i, now=True, ahead=True):
                if ahead:
                    for b in range(2):
                        ch.step(nc.vector.bn_stats(stats[:, b, :], x_rows(i + 1)(b)))
                    stats_in = ch.n
                if now:
                    v.wait_ge(S["wh_ps"], i + 1)
                    v.wait_ge(S["whs_free"], i + 1)
                    for b in range(2):
                        ch.step(tt(whs[:, b, :], bank[b][:, 0:WCOL], bias1, ALU.add))
                    wh_out = ch.n
                if ahead:
                    ch.wait(stats_in)
                    apart(v)
                    for b in range(2):
                        ch.step(nc.vector.bn_aggr(mv[:, b, :], stats[:, b, :]))
                    aggregated = ch.n
                if now:
                    for b in range(2):
                        v.wait_ge(S["sq_ready"], i * 2 + (b + 1))
                        ch.step(inner_sum(kvr[:, 0, b, :], kvq[:, b, :].rearrange("p (h d) -> p h d", d=MD)))
                    summed = ch.n
                if ahead:
                    ch.wait(aggregated)
                    ch.step(ts(vare[:, :], mv[:, :, 1], EPS, None, ALU.add))
                    var_in = ch.n
                if now:
                    ch.wait(wh_out)
                    v.sem_inc(S["wh_ready"], 1)
                    ch.wait(summed)
                    ch.step(ts(kvr[:, 0, :, :], kvr[:, 0, :, :], 1.0 / MD, EPS, ALU.mult, ALU.add))
                    kvar_in = ch.n
                if ahead:
                    ch.wait(var_in)
                    nc.vector.reciprocal(rs[:, :, 0], vare[:, :]).then_inc(S["var_ready"], 1)
                if now:
                    ch.wait(kvar_in)
                    nc.vector.reciprocal(kvr[:, 0, :, :], kvr[:, 0, :, :]).then_inc(S["kvar_ready"], 1)
                if ahead:
                    v.wait_ge(S["rstd_ready"], i + 2)
                    if now:
                        v.wait_ge(S["tp_ready"], i + 1)
                    for b in range(2):
                        last = ts(xn[:, b, :], x_rows(i + 1)(b), mv[:, b, 0:1], rs[:, b, 1:2], ALU.subtract, ALU.mult)
                    last.then_inc(S["xn_ready"], 1)
                if now:
                    v.wait_ge(S["krs_ready"], i + 1)
                    v.wait_ge(S["kv_done"], i + 1)
                    for b in range(2):
                        tt(kvs[:, b, :].rearrange("p (h d) -> p h d", d=MD), bank[2 + b][:, :].rearrange("p (h d) -> p h d", d=MD),
                           kvr[:, 1, b, :].unsqueeze(2).to_broadcast([P, 8, MD]), ALU.mult).then_inc(S["kn_ready"], 1)

            first_phase(-1, now=False)
            start, per = ch.base + ch.n, 10
            with v.Fori(0, SPLIT) as i:
                ch.at(i * per + start)
                first_phase(i)
                assert ch.n == per, ch.n
            ch.at(start + SPLIT * per)

            v.wait_ge(S["ord_in"], 16)
            ch.step(copy(rowp[:, :], ordn[:, :, 1]))
            ch.step(copy(deg[:, :], ordn[:, :, 2]))
            ch.step(ts(valid[:, :], ordn[:, :, 0], float(N), None, ALU.is_lt))
            ch.step(nc.vector.memset(m_all[:, :, :], LOW))
            ch.step(nc.vector.memset(den_all[:, :, :], 0.0))
            ch.step(nc.vector.memset(ctlf[:, :], 0.0))
            ch.wait()
            v.sem_inc(S["mx_ready"], 1)

            def windows(c):
                c.link(copy(starti[:, :], rowp[:, :]))
                c.step(ts(winr[:, :], starti[:, :], WSTEP.bit_length() - 1, None, ALU.arith_shift_right))
                for n in range(4):
                    c.step(ts(bits[:, n, :], starti[:, :], n, 1, ALU.arith_shift_right, ALU.bitwise_and))
                c.wait()
                c.link(ts(winr[:, :], winr[:, :], NWROW - 1, None, ALU.min))

            def shifted(c, lo, n_tiles, o):
                tiles = slice(lo, lo + n_tiles)
                cur, other, width = wina, winb, WLEN
                for n in (3, 2, 1, 0):
                    width -= 1 << n
                    to = other[:, tiles, 0:width] if n else o[:, tiles, 0:WIN]
                    take = width if n else WIN
                    c.link(copy(to, cur[:, tiles, 0:take]))
                    apart(v)
                    c.link(nc.vector.copy_predicated(to, bits[:, n, tiles].unsqueeze(2).to_broadcast([P, n_tiles, take]),
                                                     cur[:, tiles, (1 << n):(1 << n) + take]))
                    cur, other = other, cur
                apart(v)

            def slot_groups(c):
                c.link(ts(small[:, 2, :], mxrem[:, :], 1.0, float(WIN), ALU.max, ALU.min))
                c.step(copy(slots[:, :], small[:, 2, :]))
                c.link(ts(small[:, 0, :], small[:, 2, :], float(SG - 1), None, ALU.add))
                c.link(copy(groups[:, :], small[:, 0, :]))
                c.link(ts(groups[:, :], groups[:, :], SG.bit_length() - 1, None, ALU.arith_shift_right))

            def running_sums(c, of_groups, of_slots):
                by_buffer = lambda a: a.rearrange("p (i b) -> p b i", b=2)
                for b in range(2):
                    for sums, at, of in ((gcumf, 5, of_groups), (scumf, 7, of_slots)):
                        c.step(scan(sums[:, b, :], onesf[:, 0:NPAIR], by_buffer(of)[:, b, :], ctlf[:, at + b:at + b + 1], ALU.mult, ALU.add))
                c.wait()
                c.step(copy(ctlf[:, 5:7], gcumf[:, :, NPAIR - 1]))
                c.step(copy(ctlf[:, 7:9], scumf[:, :, NPAIR - 1]))
                c.step(copy(scum[:, :, :], scumf[:, :, :]))
                c.step(tt(gbase[:, :, :], gcumf[:, :, :], by_buffer(groups[:, :]), ALU.subtract))

            windows(ch)
            v.sem_inc(S["lwin_ready"], 1)
            v.wait_ge(S["mx_done"], 1)
            ch.link(reduce(ctlf[:, 3:4], mxrem[:, :], AX.X, ALU.max))
            ch.link(ts(ctlf[:, 3:4], ctlf[:, 3:4], (WIN - 1) / 2 - WIN, 1.0 / WIN, ALU.add, ALU.mult))
            ch.link(ts(ctlf[:, 3:4], ctlf[:, 3:4], 0.0, None, ALU.max))
            ch.link(copy(nextra[:, :], ctlf[:, 3:4]))
            start = ch.base + ch.n
            with v.Fori(SPLIT, NPAIR - 1) as i:
                ch.at(i * per + (start - SPLIT * per))
                first_phase(i)
            ch.at(start + (NPAIR - 1 - SPLIT) * per)
            first_phase(NPAIR - 1, ahead=False)
            ch.wait()
            v.sem_inc(S["tables_ready"], 1)

            v.wait_ge(S["mw_in"], 32)
            v.wait_ge(S["kv_done"], NPAIR + 2)
            per_head = lambda a: a.unsqueeze(1).to_broadcast([P, MH, MD])
            kv, aside = [base_s[:, i, :].rearrange("p (h d) -> p h d", h=MH) for i in range(2)]
            ch.step(nc.vector.memset(kvd, 0.0))
            ch.step(copy(ksum[:, :], bank[7][:, 0:2]))
            ch.link(tt(kv, bank[4][:, 0:D].rearrange("p (h d) -> p h d", h=MH), per_head(lngb[:, 0, 1, :]), ALU.mult))
            for j in range(2):
                ch.step(ts(aside[:, 2 * j:2 * j + 2, :], lngb[:, 1, 1, :].unsqueeze(1).to_broadcast([P, 2, MD]), ksum[:, j:j + 1], None, ALU.mult))
            ch.wait()
            ch.link(tt(kv, kv, aside, ALU.add))
            ch.step(ts(base_s[:, 0, :], base_s[:, 0, :], kcol[:, 0:1], None, ALU.mult))
            ch.link(tt(aside, bank[6][:, 0:D].rearrange("p (h d) -> p h d", h=MH), per_head(lngb[:, 0, 1, :]), ALU.mult))
            ch.link(ts(lngb[:, 1, 1, :], lngb[:, 1, 1, :], float(N), None, ALU.mult))
            ch.link(tt(aside, aside, per_head(lngb[:, 1, 1, :]), ALU.add))
            ch.link(ts(base_s[:, 1, :], base_s[:, 1, :], kcol[:, 1:2], None, ALU.mult))
            ch.link(tt(kv, kv, aside, ALU.add))
            for j in range(2):
                for q in range(2):
                    r = slice(q * MD, (q + 1) * MD)
                    ch.step(ts(kvd[r, j, r], base_s[r, 0, j * P + q * MD:j * P + (q + 1) * MD], 1.0 / N, None, ALU.mult))
            ch.wait()
            v.sem_inc(S["kvd_ready"], 1)
            v.wait_ge(S["t1_ps"], 1)
            ch.link(copy(t1, bank[6][:, :].rearrange("p (k c) -> p k c", k=2)))
            v.sem_inc(S["t1_ready"], 1)
            v.wait_ge(S["mix_ps"], 1)
            ch.link(copy(mixw[:, :, :], bank[7][:, :].rearrange("p (k c) -> p k c", k=2)))
            v.sem_inc(S["mix_ready"], 1)
            start, per = ch.base + ch.n, 5
            with v.Fori(0, NPAIR) as i:
                ch.at(i * per + start)
                v.wait_ge(S["base_ps"], i + 2)
                for b in range(2):
                    ch.step(tt(t1[:, b, :], bank[b][:, 0:D], bo_b[:, :], ALU.add))
                ch.wait()
                v.sem_inc(S["base_copied"], 1)
                v.wait_ge(S["bases_free"], i + 1)
                for b in range(2):
                    ch.step(tt(base_s[:, b, :], t1[:, b, :], x_rows(i)(b), ALU.add))
                ch.wait()
                v.sem_inc(S["base_ready"], 1)
                ch.step(copy(x_all[:, bass.ds(i * 2, 2), :], zeros[:, :].unsqueeze(1).to_broadcast([P, 2, D])))
                assert ch.n == per, ch.n
            ch.at(start + NPAIR * per)
            v.wait_ge(S["lwin_in"], 16 * NT)
            v.wait_ge(S["s2_in"], 16 * NT)
            shifted(ch, 0, NT, idx)

            UNIT = 14

            def stage(p, i, b, index):
                copy(idxs[:, b, :], index[:, bass.ds(i * 2 + b, 1), :].rearrange("p o k -> p (o k)")
                     ).then_inc(S[p, "idxs_ready"][b], 1)

            def attend(p, cu, i, u, b, meanwhile=None):
                cu.at(u * (2 * UNIT) + b * UNIT)
                t = i * 2 + b
                one = lambda a: a[:, bass.ds(t, 1), :].rearrange("p o h -> p (o h)")
                ngath = v.value_load(scum[0:1, b, bass.ds(i, 1)], min_val=1, max_val=NT * EP)
                v.wait_ge(S[p, "gath_in"][b], ngath * 16)
                cu.step(ts(pen[:, :], iota_f[:, 0:WIN], deg[:, bass.ds(t, 1)], LOWER, ALU.is_ge, ALU.mult))
                cu.link(tt(ez[:, :, :], gath[:, b, :, D:ROW], s2_all[:, bass.ds(t, 1), :].to_broadcast([P, WIN, H]), ALU.add))
                cu.link(nc.vector.scalar_tensor_tensor(ez[:, :, :], ez[:, :, :], ALPHA, ez[:, :, :], ALU.mult, ALU.max))
                cu.link(tt(ez[:, :, :], ez[:, :, :], pen[:, :].unsqueeze(2).to_broadcast([P, WIN, H]), ALU.add))
                cu.link(reduce(es[:, 0, :], ez[:, :, :].rearrange("p k h -> p h k"), AX.X, ALU.max))
                cu.link(tt(es[:, 1, :], es[:, 0, :], one(m_all), ALU.max))
                cu.link(tt(es[:, 2, :], one(m_all), es[:, 1, :], ALU.subtract))
                v.sem_inc(S[p, "f_in"], 1)
                cu.step(copy(one(m_all), es[:, 1, :]))
                cu.link(tt(ez[:, :, :], ez[:, :, :], es[:, 1, :].unsqueeze(1).to_broadcast([P, WIN, H]), ALU.subtract))
                v.sem_inc(S[p, "ex_in"], 1)
                v.wait_ge(S[p, "f_ready"], u * 2 + (b + 1))
                cu.step(tt(accf[:, :].rearrange("p (h d) -> p h d", h=H), one(x_all).rearrange("p (h d) -> p h d", h=H),
                           es[:, 3, :].unsqueeze(2).to_broadcast([P, H, DH]), ALU.mult))
                cu.step(tt(es[:, 4, :], one(den_all), es[:, 3, :], ALU.mult))
                cu.wait()
                v.sem_inc(S[p, "accf_ready"], 1)
                v.wait_ge(S[p, "ex_ready"], u * 2 + (b + 1))
                ng = v.value_load(groups[0:1, bass.ds(t, 1)], min_val=1, max_val=NG)
                for q in range(NG):
                    ks = slice(q * SG, (q + 1) * SG)
                    rows = gath[:, b, ks, 0:D].rearrange("p k (h d) -> p k h d", h=H)
                    with v.If(ng > q):
                        tt(rows, rows, ez[:, ks, :].unsqueeze(3).to_broadcast([P, SG, H, DH]), ALU.mult).then_inc(S[p, "prod"][b], 1)
                cu.link(reduce(es[:, 5, :], ez[:, :, :].rearrange("p k h -> p h k"), AX.X, ALU.add))
                cu.step(tt(one(den_all), es[:, 4, :], es[:, 5, :], ALU.add))
                if meanwhile:
                    meanwhile()
                v.wait_ge(S[p, "acc_ps"], u * 2 + (b + 1))
                apart(v)
                cu.step(copy(one(x_all), bank[b][:, 0:D]))
                cu.wait()
                apart(v)
                assert cu.n == UNIT, cu.n

            def next_stage(p, i, b, n, index):
                if isinstance(i, int):
                    stage(p, i + 1, b, index)
                else:
                    with v.If(i < n - 1):
                        stage(p, i + 1, b, index)

            cx, ci, cu = Chain(v, S["x_pass"]), Chain(v, S["idx_step"]), Chain(v, S["x", "unit"])
            PASS, IDX = 38, 8
            nx = v.value_load(nextra[0:1, 0:1], min_val=0, max_val=EP // WIN)
            for a, f in ((deg, -float(WIN)), (rowp, float(WIN)), (mxrem, -float(WIN))):
                ch.link(ts(ctlf[:, 2:3], nextra[:, 0:1], f, None, ALU.mult))
                ch.link(ts(a[:, :], a[:, :], ctlf[:, 2:3], None, ALU.add))
            with v.If(nx > 0):
                with v.Fori(0, nx) as w:
                    cx.at(w * PASS)
                    slot_groups(cx)
                    cx.link(ts(small[:, 1, :], mxrem[:, :], 0.0, None, ALU.is_gt))
                    cx.link(inner_sum(ctlf[:, 1:2], small[:, 1, :]))
                    cx.step(ts(ctl[:, 3:4], ctlf[:, 1:2], 1.0, None, ALU.add))
                    cx.link(ts(ctlf[:, 2:3], ctlf[:, 1:2], (WT - 1) / 2, 1.0 / WT, ALU.add, ALU.mult))
                    cx.step(ts(ctl[:, 3:4], ctl[:, 3:4], 1, None, ALU.arith_shift_right))
                    cx.step(copy(ctl[:, 2:3], ctlf[:, 2:3]))
                    cx.link(copy(ctl[:, 0:1], ctlf[:, 0:1]))
                    cx.link(ts(ctl[:, 2:4], ctl[:, 2:4], 1, None, ALU.max))
                    cx.step(tt(ctlf[:, 0:1], ctlf[:, 0:1], ctl[:, 3:4], ALU.add))
                    cx.step(tt(ctlf[:, 4:5], ctlf[:, 4:5], ctl[:, 2:3], ALU.add))
                    cx.link(ts(ctlf[:, 1:2], ctl[:, 3:4], 2.0, None, ALU.mult))
                    cx.step(copy(ctl[:, 4:5], ctlf[:, 4:5]))
                    cx.link(ts(gmask[:, :], iota_f[:, 0:NT], ctlf[:, 1:2], None, ALU.is_lt))
                    cx.link(tt(small[:, 0, :], gmask[:, :], slots[:, :], ALU.mult))
                    cx.link(tt(gmask[:, :], gmask[:, :], groups[:, :], ALU.mult))
                    running_sums(cx, gmask[:, :], small[:, 0, :])
                    windows(cx)
                    v.sem_inc(S["x_ready"], 1)
                    npr = v.value_load(ctl[0:1, 3:4], min_val=1, max_val=NPAIR)
                    lo = v.value_load(ctl[0:1, 0:1], min_val=0, max_val=unit_bound)
                    ngr = v.value_load(ctl[0:1, 2:3], min_val=1, max_val=NT // WT)
                    nwt = v.value_load(ctl[0:1, 4:5], min_val=1, max_val=NT * EP)
                    v.wait_ge(S["x_win_in"], nwt * (16 * WT))
                    ci.at(w * (IDX * NT // WT))
                    for gr in range(NT // WT):
                        with v.If(ngr > gr):
                            n0 = ci.n
                            shifted(ci, gr * WT, WT, idx_x)
                            assert ci.n - n0 == IDX, ci.n - n0
                        with v.Else():
                            v.sem_inc(S["idx_step"], IDX)
                    v.sem_inc(S["x_idx_ready"], 1)
                    for b in range(2):
                        stage("x", 0, b, idx_x)
                    with v.Fori(0, npr) as i:
                        for b in range(2):
                            attend("x", cu, i, i + lo, b)
                            next_stage("x", i, b, npr, idx_x)
                    v.wait_ge(S["x", "unit"], (lo + npr) * (2 * UNIT))
                    apart(v)
                    cx.step(ts(deg[:, :], deg[:, :], float(WIN), None, ALU.add))
                    cx.step(ts(rowp[:, :], rowp[:, :], -float(WIN), None, ALU.add))
                    cx.step(ts(mxrem[:, :], mxrem[:, :], float(WIN), None, ALU.add))
                    cx.wait()
                    apart(v)
                    assert cx.n == PASS, cx.n
                    v.sem_inc(S["x_done"], 1)

            slot_groups(ch)
            ch.link(nc.vector.memset(ctlf[:, :], 0.0))
            running_sums(ch, groups[:, :], slots[:, :])
            ch.wait()
            v.sem_inc(S["l_ready"], 1)
            for b in range(2):
                stage("l", 0, b, idx)
            cl, ce = Chain(v, S["l", "unit"]), Chain(v, S["dve_end"])
            per = 13
            heads = lambda a: a.rearrange("p (h d) -> p h d", h=H)

            def nodes(i):
                copy(basei[:, :], ordn[:, bass.ds(i * 2, 2), 0]).then_inc(S["basei_ready"], 1)

            def x1_rows(i):
                ce.at(i * per)
                one = lambda a, b: a[:, bass.ds(i * 2 + b, 1), :].rearrange("p o h -> p (o h)")
                pair = den_all[:, bass.ds(i * 2, 2), :]
                ce.link(ts(pair, pair, 1e-30, None, ALU.max))
                apart(v)
                ce.link(nc.vector.reciprocal(pair, pair))
                for b in range(2):
                    ce.step(tt(heads(x_rows(i)(b)), heads(x_rows(i)(b)), one(den_all, b).unsqueeze(2).to_broadcast([P, H, DH]), ALU.mult))
                ce.wait()
                for b in range(2):
                    v.wait_ge(S["baseg_in"][b], i * 16 + 16)
                    ce.step(tt(x_rows(i)(b), x_rows(i)(b), baseg[:, b, :], ALU.add))
                ce.wait()
                apart(v)
                for b in range(2):
                    ce.step(nc.vector.bn_stats(stats[:, b, :], x_rows(i)(b)))
                ce.wait()
                apart(v)
                for b in range(2):
                    ce.step(nc.vector.bn_aggr(mv[:, b, :], stats[:, b, :]))
                ce.wait()
                ce.link(ts(vare[:, :], mv[:, :, 1], EPS, None, ALU.add))
                nc.vector.reciprocal(rs[:, :, 0], vare[:, :]).then_inc(S["v2_ready"], 1)

            def x1_norm(i):
                ce.at(i * per + (per - 2))
                v.wait_ge(S["r2_ready"], i + 1)
                v.wait_ge(S["lg_copied"], i + 1)
                for b in range(2):
                    ce.step(ts(xn2s[:, b, :], x_rows(i)(b), mv[:, b, 0:1], rs[:, b, 1:2], ALU.subtract, ALU.mult))
                ce.wait()
                v.sem_inc(S["xn2_ready"], 1)
                assert ce.n == 2, ce.n

            def l_pair(i, first=False):
                def between_a():
                    x1_rows(i - 1)
                    nodes(i)
                attend("l", cl, i, i, 0, None if first else between_a)
                next_stage("l", i, 0, NPAIR, idx)
                attend("l", cl, i, i, 1, None if first else lambda: x1_norm(i - 1))
                next_stage("l", i, 1, NPAIR, idx)

            nodes(0)
            l_pair(0, True)
            with v.Fori(1, NPAIR) as i:
                l_pair(i)
            x1_rows(NPAIR - 1)
            x1_norm(NPAIR - 1)
            ce.at(NPAIR * per)
            v.sem_inc(S["lg_done"], 1)
            v.wait_ge(S["lg_copied"], NPAIR + 1)
            ce.link(tt(logit, logit, bg_b[:, :].unsqueeze(1).to_broadcast([P, NT, NE]), ALU.add))

            bt = lambda a: a.unsqueeze(2).to_broadcast([P, NT, NE, NE])
            be = lambda a: a.unsqueeze(3).to_broadcast([P, NT, NE, NE])
            ce.step(tt(cmp8, bt(logit), be(logit), ALU.is_gt))
            ce.step(tt(cmp8b, bt(logit), be(logit), ALU.is_equal))
            ce.step(tt(tri8, iota_f[:, 0:NE].unsqueeze(1).to_broadcast([P, NE, NE]),
                       iota_f[:, 0:NE].unsqueeze(2).to_broadcast([P, NE, NE]), ALU.is_lt))
            ce.wait()
            ce.link(tt(cmp8b, cmp8b, tri8.unsqueeze(1).to_broadcast([P, NT, NE, NE]), ALU.mult))
            ce.link(tt(cmp8, cmp8, cmp8b, ALU.add))
            ce.link(inner_sum(pos, cmp8))
            for j in range(2):
                ce.step(ts(msk[:, j], pos, float(j), None, ALU.is_equal))
            ce.wait()
            for j in range(2):
                ce.step(tt(cmp8[:, :, j, :], msk[:, j], logit, ALU.mult))
            ce.wait()
            for j in range(2):
                ce.step(inner_sum(small[:, j, :], cmp8[:, :, j, :]))
            ce.wait()
            ce.link(tt(small[:, 2, :], small[:, 1, :], small[:, 0, :], ALU.subtract))
            v.sem_inc(S["gap_ready"], 1)
            for j in range(2):
                ce.step(tt(msk[:, j], msk[:, j], valid[:, :].unsqueeze(2).to_broadcast([P, NT, NE]), ALU.mult))
            ce.wait()
            ce.link(tt(m01.rearrange("p (t e) -> p t e", t=NT), msk[:, 0], msk[:, 1], ALU.add))
            v.sem_inc(S["m01_ready"], 1)
            v.wait_ge(S["pre_ps"], 1)
            ce.step(copy(pos, bank[0][:, 0:NT * NE].rearrange("p (t e) -> p t e", t=NT)))
            ce.step(copy(tex3, bank[1][:, 0:NT * NE].rearrange("p (t e) -> p e t", t=NT)))
            ce.wait()
            for e in range(NE):
                ce.step(scan(tsc3[:, e, :], onesf[:, 0:NT], tex3[:, e, :], 0.0, ALU.mult, ALU.add))
            ce.wait()
            ce.step(copy(cnt[:, 0, :], tsc3[:, :, NT - 1]))
            ce.link(tt(tex3, tsc3, tex3, ALU.subtract))
            ce.link(ts(cnt[:, 0, :], cnt[:, 0, :], float(TT - 1), None, ALU.add))
            ce.link(copy(cnti[:, :], cnt[:, 0, :]))
            ce.link(ts(cnti[:, :], cnti[:, :], TT.bit_length() - 1, None, ALU.arith_shift_right))
            ce.link(ts(cnti[:, :], cnti[:, :], 1, None, ALU.max))
            ce.link(copy(cnt[:, 1, :], cnti[:, :]))
            ce.link(scan(cnt[:, 2, :], onesf[:, 0:NE], cnt[:, 1, :], 0.0, ALU.mult, ALU.add))
            ce.link(tt(cnt[:, 3, :], cnt[:, 2, :], cnt[:, 1, :], ALU.subtract))
            ce.step(copy(ebnd[:, 0, :], cnt[:, 3, :]))
            ce.step(copy(ebnd[:, 1, :], cnt[:, 2, :]))
            ce.link(ts(cnt[:, 0, :], cnt[:, 3, :], float(TT), None, ALU.mult))
            v.sem_inc(S["bounds_ready"], 1)
            ce.link(tt(pos, pos, tex3.rearrange("p e t -> p t e"), ALU.add))
            ce.link(tt(pos, pos, cnt[:, 0, :].unsqueeze(1).to_broadcast([P, NT, NE]), ALU.add))
            for j in range(2):
                ce.step(tt(cmp8[:, :, j, :], msk[:, j], pos, ALU.mult))
            ce.link(ts(small[:, 0, :], valid[:, :], 1.0, -float(NOWHERE), ALU.subtract, ALU.mult))
            for j in range(2):
                ce.step(inner_sum(slotf[:, j, :], cmp8[:, :, j, :]))
            ce.wait()
            for j in range(2):
                ce.step(tt(slotf[:, j, :], slotf[:, j, :], small[:, 0, :], ALU.add))
            ce.wait()
            ce.link(copy(sloti[:, :, :], slotf[:, :, :]))
            v.wait_ge(S["gexp_ready"], 1)
            ce.link(ts(small[:, 1, :], small[:, 3, :], 1.0, None, ALU.add))
            ce.link(nc.vector.reciprocal(wts[:, 0, :], small[:, 1, :]))
            ce.link(tt(wts[:, 1, :], wts[:, 0, :], small[:, 3, :], ALU.mult))
            for j in range(2):
                ce.step(tt(msk[:, j], msk[:, j], wts[:, j, :].unsqueeze(2).to_broadcast([P, NT, NE]), ALU.mult))
            ce.wait()
            v.wait_ge(S["xn2_copied"], NPAIR)
            ce.step(tt(xrow_all[:, :, D:D + NE], msk[:, 0], msk[:, 1], ALU.add))
            ce.link(copy(xrow_all[:, :, D + NE:XROW].bitcast(I32), ordn[:, :, 0:1]))
            v.sem_inc(S["slot_ready"], 1)

            v.sem_inc(S["y_ready"], 1)
            cy = Chain(v, S["y_step"])

            def tokens_in(i, par):
                v.wait_ge(S["xs_in"], i * 16 + 16)
                copy(meta[:, :, :], xs_s[:, :, D:XROW])
                v.wait_ge(S["xte_ps"], i + 1)
                copy(xTe[:, bass.ds(par, 1), :, :].rearrange("p o k n -> p (o k) n"),
                     bank[6][:, :].rearrange("p (k n) -> p k n", k=KD)).then_inc(S["xte_ready"], 1)

            tokens_in(0, 0)
            with v.Fori(0, NE // 2) as ep:
                for s in range(2):
                    e = ep * 2 + s
                    lo = v.value_load(ebnd[0:1, 0, bass.ds(e, 1)], min_val=0, max_val=XT - 2)
                    hi = v.value_load(ebnd[0:1, 1, bass.ds(e, 1)], min_val=1, max_val=XT - 1)
                    v.wait_ge(S["ew_in"][s], ep * 64 + 64)
                    apart(v)
                    with v.Fori(lo, hi) as i:
                        cy.at(i * 3)
                        v.wait_ge(S["ys_free"], i + 1)
                        v.wait_ge(S["xte_ready"], i + 1)
                        cy.link(copy(metao[:, :, :], meta[:, :, :]))
                        tokens_in(i + 1, (i + 1) % 2)
                        v.wait_ge(S["y_ps"], i + 1)
                        for a in range(2):
                            cy.step(tt(ysb[:, a, :], bank[4 + a][:, 0:D], b2s[:, s, :], ALU.add))
                        cy.wait()
                        for a in range(2):
                            last = ts(ysb[:, a, :], ysb[:, a, :], metao[:, a, bass.ds(e, 1)], None, ALU.mult)
                        last.then_inc(S["y_ready"], 1)
                    v.wait_ge(S["y_ready"], hi + 1)
                    v.sem_inc(S["ew_used"][s], 1)

        @block.tensor
        def _(pe):
            mm = nc.tensor.matmul

            pe.wait_ge(S["consts"], 1)
            zb = zeros[:, :].bitcast(BF16)[:, 0:NT]
            mm(bank[0][:, 0:NT], onesb[:, :], zb, start=True, stop=False)
            pe.sem_inc(S["hist_used"], 2)
            with pe.Fori(0, NHIST) as i:
                for a in range(2):
                    pe.wait_ge(S["hist_oh"], i * 2 + (a + 1))
                    for j in range(HC):
                        last = mm(bank[0][:, 0:NT], oh_b[:, a, j, :], oh_a[:, a, j, :], start=False, stop=False)
                    last.then_inc(S["hist_used"], 1)
            mm(bank[0][:, 0:NT], onesb[:, :], zb, start=False, stop=True).then_inc(S["hist_used"], 1)
            pe.wait_ge(S["deg_ready"], 1)
            mm(bank[1][:, 0:NT], ltf[:, :], deg[:, :], start=True, stop=True)
            mm(bank[1][:, 64:64 + NT], onesf[:, :], deg[:, :], start=True, stop=True).then_inc(S["rowp_ps"], 1)
            pe.wait_ge(S["order_known"], 1)
            unsorted = pe.value_load(falls[0:1, 0:1], min_val=0, max_val=1)
            with pe.If(unsorted > 0):
                with pe.Fori(0, EC) as j:
                    pe.wait_ge(S["sort_key"], j + 1)
                    mm(bank[2][:, 0:P], key_b, ident[:, :], start=True, stop=True).then_inc(S["sort_ps"], 1)
            pe.wait_ge(S["ohd_ready"], 1)
            for n, lo in enumerate(range(0, NT, BT)):
                k = min(BT, NT - lo)
                if n >= 2:
                    pe.wait_ge(S["cnt_used"], n - 1)
                bk = 2 + 2 * (n % 2)
                oh = oh_d[:, lo:lo + k, :].rearrange("p t c -> p (t c)")
                mm(bank[bk][:, 0:k * NBUCK], ltb[:, :], oh, start=True, stop=True)
                mm(bank[bk + 1][:, 0:k * NBUCK], onesb[:, :], oh, start=True, stop=True).then_inc(S["cnt_ps"], 1)

            pe.wait_ge(S["cnt_used"], (NT + BT - 1) // BT)
            for at in (bank[4][:, 0:D], bank[7][:, 0:2], bank[6][:, 0:D]):
                mm(at, ident[:, :], zeros[:, 0:at.shape[1]], start=True, stop=False)
            pe.sem_inc(S["kv_done"], 1)

            def kv_outer(i, rows=(P, P)):
                for b in range(2):
                    if rows[b]:
                        pe.wait_ge(S["kn_ready"], i * 2 + (b + 1))
                        for j in range(2):
                            keys = kvs[0:rows[b], b, j * P:(j + 1) * P]
                            mm(bank[4][:, j * P:(j + 1) * P], keys, kvs[0:rows[b], b, D + j * P:D + (j + 1) * P], start=False, stop=False)
                            mm(bank[7][:, j:j + 1], keys, onesf[0:rows[b], 0:1], start=False, stop=False)
                        last = mm(bank[6][:, 0:D], onesf[0:rows[b], :], kvs[0:rows[b], b, D:2 * D], start=False, stop=False)
                last.then_inc(S["kv_done"], 1)

            def first_phase(i, first=False):
                pe.wait_ge(S["xn_ready"], i + 1)
                if not first:
                    pe.wait_ge(S["xT_ready"], i * 2)
                for k in range(KD):
                    for b in range(2):
                        last = nc.tensor.transpose(bank[5][:, k * 2 * P + b * P:k * 2 * P + (b + 1) * P],
                                                   xn[:, b, k * P:(k + 1) * P], ident[:, :])
                last.then_inc(S["tp_ready"], 1)
                pe.wait_ge(S["xT_ready"], i * 2 + 1)
                if not first:
                    pe.wait_ge(S["wh_ready"], i)
                for b in range(2):
                    for k in range(KD):
                        last = mm(bank[b][:, 0:WCOL], xTs[:, k, b * P:(b + 1) * P], wcat[:, k, :], start=(k == 0), stop=(k == KD - 1))
                last.then_inc(S["wh_ps"], 1)
                if not first:
                    pe.wait_ge(S["kn_ready"], i * 2)
                for b in range(2):
                    for k in range(KD):
                        last = mm(bank[2 + b][:, :], xTs[:, k, b * P:(b + 1) * P], wkv[:, k, :], start=(k == 0), stop=(k == KD - 1))
                    last.then_inc(S["kv_ps"], 1)

            first_phase(0, True)
            with pe.Fori(1, NPAIR) as i:
                first_phase(i)
                kv_outer(i - 1)
            kv_outer(NPAIR - 1, (TAIL, 0))
            for at in (bank[4][:, 0:D], bank[7][:, 0:2], bank[6][:, 0:D]):
                last = mm(at, ident[:, :], zeros[:, 0:at.shape[1]], start=False, stop=True)
            last.then_inc(S["kv_done"], 1)

            pe.wait_ge(S["mw_in"], 32)
            pe.wait_ge(S["kvd_ready"], 1)
            for j in range(2):
                last = mm(bank[6][:, j * D:(j + 1) * D], kvd[:, j, :], wq_s[:, j, :], start=True, stop=True)
            last.then_inc(S["t1_ps"], 1)
            pe.wait_ge(S["t1_ready"], 1)
            for k in range(KD):
                for j in range(2):
                    last = mm(bank[7][:, k * D:(k + 1) * D], t1[:, j, k * P:(k + 1) * P], wo_s[:, j, :], start=(j == 0), stop=(j == 1))
            last.then_inc(S["mix_ps"], 1)
            pe.wait_ge(S["mix_ready"], 1)
            pe.sem_inc(S["base_ps"], 1)

            def mixed(i, first=False):
                pe.wait_ge(S["mxs_ready"], i + 1)
                if not first:
                    pe.wait_ge(S["base_copied"], i)
                for b in range(2):
                    for k in range(KD):
                        last = mm(bank[b][:, 0:D], mxs[:, k, b * P:(b + 1) * P], mixw[:, k, :], start=(k == 0), stop=(k == KD - 1))
                last.then_inc(S["base_ps"], 1)

            mixed(0, True)
            with pe.Fori(1, NPAIR) as i:
                mixed(i)

            def slot_sums(p, i, u, b):
                ng = pe.value_load(groups[0:1, bass.ds(i * 2 + b, 1)], min_val=1, max_val=NG)
                nprod = pe.value_load(gbase[0:1, b, bass.ds(i, 1)], min_val=0, max_val=NT * EP)
                pe.wait_ge(S[p, "accf_ready"], u * 2 + (b + 1))
                mm(bank[b][:, 0:D], ident[:, :], accf[:, :], start=True, stop=False)
                for q in range(NG):
                    with pe.If(ng > q):
                        pe.wait_ge(S[p, "prod"][b], nprod + (q + 1))
                        for k in range(q * SG, (q + 1) * SG):
                            mm(bank[b][:, 0:D], ident[:, :], gath[:, b, k, 0:D], start=False, stop=False)
                mm(bank[b][:, 0:D], ident[:, :], zeros[:, :], start=False, stop=True).then_inc(S[p, "acc_ps"], 1)

            pe.wait_ge(S["tables_ready"], 1)
            nx = pe.value_load(nextra[0:1, 0:1], min_val=0, max_val=EP // WIN)
            with pe.If(nx > 0):
                with pe.Fori(0, nx) as w:
                    pe.wait_ge(S["x_ready"], w + 1)
                    apart(pe)
                    lo = pe.value_load(ctl[0:1, 0:1], min_val=0, max_val=unit_bound)
                    npr = pe.value_load(ctl[0:1, 3:4], min_val=1, max_val=NPAIR)
                    with pe.Fori(0, npr) as i:
                        for b in range(2):
                            slot_sums("x", i, i + lo, b)
                    pe.wait_ge(S["x_done"], w + 1)
                    apart(pe)
            pe.wait_ge(S["l_ready"], 1)

            def gate(i):
                pe.wait_ge(S["xn2_ready"], i + 1)
                for k in range(KD):
                    for b in range(2):
                        last = nc.tensor.transpose(bank[5][:, k * 2 * P + b * P:k * 2 * P + (b + 1) * P],
                                                   xn2s[:, b, k * P:(k + 1) * P], ident[:, :])
                last.then_inc(S["tp2_ready"], 1)
                pe.wait_ge(S["xTr_ready"], i + 1)
                for b in range(2):
                    for k in range(KD):
                        last = mm(bank[6][:, b * NE:(b + 1) * NE], xTr[:, k, b * P:(b + 1) * P], wg_s[:, k, :], start=(k == 0), stop=(k == KD - 1))
                last.then_inc(S["lg_ps"], 1)

            for b in range(2):
                slot_sums("l", 0, 0, b)
            with pe.Fori(1, NPAIR) as i:
                for b in range(2):
                    slot_sums("l", i, i, b)
                gate(i - 1)
            gate(NPAIR - 1)
            pe.wait_ge(S["m01_ready"], 1)
            mm(bank[0][:, 0:NT * NE], ltb[:, :], m01, start=True, stop=True)
            mm(bank[1][:, 0:NT * NE], onesb[:, :], m01, start=True, stop=True).then_inc(S["pre_ps"], 1)

            def tokens_in(i, first=False):
                pe.wait_ge(S["xs_in"], i * 16 + 16)
                if not first:
                    pe.wait_ge(S["xte_ready"], i)
                for k in range(KD):
                    for a in range(2):
                        last = nc.tensor.transpose(bank[6][:, k * TT + a * P:k * TT + (a + 1) * P],
                                                   xs_s[:, a, k * P:(k + 1) * P], ident[:, :])
                last.then_inc(S["xte_ps"], 1)

            pe.wait_ge(S["bounds_ready"], 1)
            tokens_in(0, True)
            with pe.Fori(0, NE // 2) as ep:
                for s in range(2):
                    lo = pe.value_load(ebnd[0:1, 0, bass.ds(ep * 2 + s, 1)], min_val=0, max_val=XT - 2)
                    hi = pe.value_load(ebnd[0:1, 1, bass.ds(ep * 2 + s, 1)], min_val=1, max_val=XT - 1)
                    pe.wait_ge(S["ew_in"][s], ep * 64 + 64)
                    apart(pe)

                    def up(i, c):
                        pe.wait_ge(S["h_ready"], i * FC + (c + 1))
                        for k in range(KD):
                            last = mm(bank[c % 4][:, 0:TT], w1s[:, s, k, c * P:(c + 1) * P],
                                      xTe[:, bass.ds(i % 2, 1), k, :].rearrange("p o n -> p (o n)"), start=(k == 0), stop=(k == KD - 1))
                        last.then_inc(S["h_ps"], 1)

                    def down(i, c):
                        pe.wait_ge(S["h_ready"], i * FC + (c + 5))
                        for a in range(2):
                            last = mm(bank[4 + a][:, 0:D], hT[:, c, a * P:(a + 1) * P], w2s[:, s, c, :], start=(c == 0), stop=(c == FC - 1))
                        if c == FC - 1:
                            last.then_inc(S["y_ps"], 1)

                    with pe.Fori(lo, hi) as i:
                        pe.wait_ge(S["xte_ready"], i + 1)
                        for c in range(FC):
                            up(i, c)
                            if c == 2:
                                pe.wait_ge(S["y_ready"], i + 1)
                            if c >= 2:
                                down(i, c - 2)
                            if c == FC // 2:
                                tokens_in(i + 1)
                        down(i, FC - 2)
                        down(i, FC - 1)


def kernel(x, src, dst, L0_gnn_W, L0_gnn_bW, L0_gnn_a_src, L0_gnn_a_dst, L0_gnn_a_bias, L0_mix_wq, L0_mix_wk, L0_mix_wv,
           L0_mix_wo, L0_mix_bo, L0_mix_ln_k_g, L0_mix_ln_k_b, L0_mix_ln_v_g, L0_mix_ln_v_b, L0_ffn_Wg, L0_ffn_bg,
           L0_ffn_W1, L0_ffn_b1, L0_ffn_W2, L0_ffn_b2):
    import numpy as np
    import concourse.bacc as bacc
    from concourse.bass_utils import run_bass_kernel_spmd as run

    a = lambda v: np.ascontiguousarray(np.asarray(v))
    src_, dst_ = a(src), a(dst)
    arrays = {
        "x": np.pad(a(x), ((0, NP - N), (0, 0))),
        "src": np.pad(src_, (0, EP - E_REAL)),
        "dst": np.pad(dst_, (0, EP - E_REAL), constant_values=NP),
        "dst_next": np.pad(dst_[1:], (0, EP - E_REAL + 1), constant_values=NP),
        "gW": a(np.asarray(L0_gnn_W).transpose(1, 0, 2).reshape(D, D)),
        "gbW": a(L0_gnn_bW).reshape(-1),
        "gas": a(L0_gnn_a_src).reshape(-1),
        "gad": a(L0_gnn_a_dst).reshape(-1),
        "gab": a(L0_gnn_a_bias),
        "wkvT": a(np.concatenate([np.asarray(L0_mix_wk).T, np.asarray(L0_mix_wv).T], axis=1)),
        "wq": a(L0_mix_wq),
        "woT": a(np.asarray(L0_mix_wo).T),
        "bo": a(L0_mix_bo),
        "lng": a(np.concatenate([np.asarray(L0_mix_ln_k_g), np.asarray(L0_mix_ln_v_g)])),
        "lnb": a(np.concatenate([np.asarray(L0_mix_ln_k_b), np.asarray(L0_mix_ln_v_b)])),
        "lncol": a(np.tile(np.stack([np.asarray(L0_mix_ln_k_g), np.asarray(L0_mix_ln_k_b)], axis=1), (P // MD, 1))),
        "Wg": a(L0_ffn_Wg),
        "bg": a(L0_ffn_bg),
        "W1": a(L0_ffn_W1).reshape(NE * D, HID),
        "b1": a(np.asarray(L0_ffn_b1).reshape(NE, FC, P).transpose(0, 2, 1)).reshape(NE * P, FC),
        "W2": a(L0_ffn_W2).reshape(NE * HID, D),
        "b2": a(L0_ffn_b2),
    }
    nc = bacc.Bacc("TRN2", target_bir_lowering=False, num_devices=1)
    args = [nc.dram_tensor(f"in_{n}", v.shape, mybir.dt.from_np(v.dtype), kind="ExternalInput").ap() for n, v in arrays.items()]
    out = nc.dram_tensor("out", (N, D), F32, kind="ExternalOutput").ap()
    gps_layer(nc, *args, out)
    r = run(nc, [{f"in_{n}": v for n, v in arrays.items()}], core_ids=[0])
    return r.results[0]["out"]
```
